# Optimizing a Trainium2 kernel written in Bass

```python
import numpy as np
import jax
import jax.numpy as jnp

def _softmax(x, axis=-1):
    return jax.nn.softmax(x, axis=axis)

def _gelu(x):
    return jax.nn.gelu(x, approximate=True)

def _silu(x):
    return jax.nn.silu(x)

def _sigmoid(x):
    return jax.nn.sigmoid(x)

def _layernorm(x, axis=-1, eps=1e-05):
    m = jnp.mean(x, axis=axis, keepdims=True)
    v = jnp.var(x, axis=axis, keepdims=True)
    return (x - m) / jnp.sqrt(v + eps)

def _scatter_add(tgt, idx, src, axis=0):
    return tgt.at[idx].add(src)

def _segment_sum(src, seg, n):
    return jax.ops.segment_sum(src, seg, n)
kernel_name = 'mk_lm_tower_d2_tok_ids4096_r4_f92cc0'

def setup_inputs(seed: int=0):
    np.random.seed(seed)
    _w = jnp.asarray

    def _rec_inputs():
        import jax
        import jax.numpy as jnp
        _rk = jax.random.key(seed)
        x = jax.random.randint(jax.random.fold_in(_rk, 1), (8, 512), 0, 8500, jnp.int32)
        return x
    x = _rec_inputs()

    def _L0_tok_setup():
        import math
        import jax, jax.numpy as jnp
        import numpy as np
        N_TOK = 8000
        CANVAS = 125
        SIN_DIM = 128
        HID = 256
        TOK_DIM = 1024
        E = 4
        B, S = (4, 512)

        def _sinusoidal(added_idx):
            x = added_idx.astype(jnp.float32) / CANVAS * CANVAS
            half = SIN_DIM // 2
            freqs = jnp.exp(jnp.arange(half, dtype=jnp.float32) * (-math.log(100.0) / (half - 1)))
            ang = x[..., None] * freqs
            return jnp.concatenate([jnp.sin(ang), jnp.cos(ang)], axis=-1)
        key = jax.random.key(seed)
        ks = jax.random.split(key, 8)
        inp = {'input_ids': jax.random.randint(ks[0], (B, S), 0, N_TOK + E * CANVAS, dtype=jnp.int64) if jax.config.jax_enable_x64 else jax.random.randint(ks[0], (B, S), 0, N_TOK + E * CANVAS, dtype=jnp.int32), 'embed_table': jax.random.normal(ks[1], (N_TOK, TOK_DIM), dtype=jnp.float32) * 0.02, 'W1': jax.random.normal(ks[2], (E, SIN_DIM, HID), dtype=jnp.float32) * 0.05, 'b1': jnp.zeros((E, HID), dtype=jnp.float32), 'W2': jax.random.normal(ks[3], (E, HID, HID), dtype=jnp.float32) * 0.03, 'b2': jnp.zeros((E, HID), dtype=jnp.float32), 'W3': jax.random.normal(ks[4], (E, HID, TOK_DIM), dtype=jnp.float32) * 0.03, 'b3': jnp.zeros((E, TOK_DIM), dtype=jnp.float32)}
        return inp
    _L0_tok_all = _L0_tok_setup()
    _L0_tok_in = {k: v for k, v in _L0_tok_all.items() if k in ('embed_table', 'W1', 'b1', 'W2', 'b2', 'W3', 'b3')}
    del _L0_tok_all

    def _L0_attn_setup():
        import jax, jax.numpy as jnp
        import numpy as np
        HDC_DIM = 1024
        N_HEADS = 4
        HEAD_DIM = HDC_DIM // N_HEADS

        def _ste_sign(w):
            alpha = jnp.mean(jnp.abs(w), axis=-1, keepdims=True)
            hard = alpha * jnp.sign(w)
            hard = jnp.where(hard == 0, alpha, hard)
            return jax.lax.stop_gradient(hard - w) + w
        key = jax.random.key(seed)
        kx, kq, kk, kv = jax.random.split(key, 4)
        B, T = (4, 512)
        x = jax.random.normal(kx, (B, T, HDC_DIM), dtype=jnp.float32)
        bv_q = jax.random.normal(kq, (N_HEADS, HEAD_DIM), dtype=jnp.float32) * 0.02
        bv_k = jax.random.normal(kk, (N_HEADS, HEAD_DIM), dtype=jnp.float32) * 0.02
        bv_v = jax.random.normal(kv, (N_HEADS, HEAD_DIM), dtype=jnp.float32) * 0.02
        return {'x': x, 'bv_q': bv_q, 'bv_k': bv_k, 'bv_v': bv_v}
    _L0_attn_all = _L0_attn_setup()
    _L0_attn_in = {k: v for k, v in _L0_attn_all.items() if k in ('bv_q', 'bv_k', 'bv_v')}
    del _L0_attn_all

    def _L0_ffn_setup():
        import jax, jax.numpy as jnp
        import numpy as np
        SCALING = 32.0 / 16.0
        key = jax.random.key(seed)
        ks = jax.random.split(key, 7)
        B, T, D, O, R, E = (4, 512, 1024, 1024, 16, 8)
        x = jax.random.normal(ks[0], (B, T, D), dtype=jnp.float32)
        base_W = jax.random.normal(ks[1], (O, D), dtype=jnp.float32) * D ** (-0.5)
        base_b = jax.random.normal(ks[2], (O,), dtype=jnp.float32) * 0.01
        router_W = jax.random.normal(ks[3], (2 * E - 1, D), dtype=jnp.float32) * D ** (-0.5)
        router_b = jax.random.normal(ks[4], (2 * E - 1,), dtype=jnp.float32) * 0.01
        A = jax.random.normal(ks[5], (E, R, D), dtype=jnp.float32) * D ** (-0.5)
        Bm = jax.random.normal(ks[6], (E, O, R), dtype=jnp.float32) * R ** (-0.5)
        assigned_idx = 0
        others = [i for i in range(E) if i != assigned_idx]
        expert_map = jnp.array([assigned_idx] * E + others, dtype=jnp.int32)
        return {'x': x, 'base_W': base_W, 'base_b': base_b, 'router_W': router_W, 'router_b': router_b, 'A': A, 'B': Bm, 'expert_map': expert_map}
    _L0_ffn_all = _L0_ffn_setup()
    _L0_ffn_in = {k: v for k, v in _L0_ffn_all.items() if k in ('base_W', 'base_b', 'router_W', 'router_b', 'A', 'B', 'expert_map')}
    del _L0_ffn_all

    def _L1_attn_setup():
        import jax, jax.numpy as jnp
        import numpy as np
        HID = 1024
        DM = 128
        DIN = 2 * DM
        DST = 16
        HD = 64
        NH = DIN // HD
        DCONV = 7
        CONV_DIM = DIN + 2 * DST
        DIN_PROJ = 2 * DIN + 2 * DST + 2 * NH
        SEQ, BATCH = (512, 4)

        def _causal_conv(x, w, b):
            y = jax.lax.conv_general_dilated(jnp.transpose(x, (0, 2, 1)), w, (1,), [(DCONV - 1, 0)], feature_group_count=CONV_DIM, dimension_numbers=('NCH', 'OIH', 'NCH'))
            return jnp.transpose(y, (0, 2, 1)) + b

        def _ssm_scan(x, dt, A, B, C):
            dA = jnp.exp(dt * A)
            dBx = dt[..., None] * x

            def step(h, t):
                dA_t, dBx_t, B_t, C_t = t
                h = dA_t[:, :, None, None] * h + dBx_t[..., None] * B_t[:, None, None, :]
                y = jnp.einsum('bhpn,bn->bhp', h, C_t)
                return (h, y)
            h0 = jnp.zeros((x.shape[0], NH, HD, DST), x.dtype)
            _, ys = jax.lax.scan(step, h0, (jnp.moveaxis(dA, 1, 0), jnp.moveaxis(dBx, 1, 0), jnp.moveaxis(B, 1, 0), jnp.moveaxis(C, 1, 0)))
            return jnp.moveaxis(ys, 0, 1)

        def _hydra(u, in_w, conv_w, conv_b, dt_bias, A_log, D, fcD_w, norm_w, out_w):
            b, l, _ = u.shape
            zxbcdt = u @ in_w.T
            z = zxbcdt[..., :DIN]
            xBC = zxbcdt[..., DIN:DIN + CONV_DIM]
            dt2 = zxbcdt[..., DIN + CONV_DIM:]
            dt_fw = jax.nn.softplus(dt2[..., :NH] + dt_bias)
            dt_bw = jax.nn.softplus(jnp.flip(dt2[..., NH:], 1) + dt_bias)
            xBC = jax.nn.silu(_causal_conv(xBC, conv_w, conv_b))
            xs = xBC[..., :DIN]
            Bm = xBC[..., DIN:DIN + DST]
            Cm = xBC[..., DIN + DST:]
            A = -jnp.exp(A_log)
            x4 = xs.reshape(b, l, NH, HD)
            y_fw = _ssm_scan(x4, dt_fw, A, Bm, Cm).reshape(b, l, DIN)
            y_bw = jnp.flip(_ssm_scan(jnp.flip(x4, 1), dt_bw, A, jnp.flip(Bm, 1), jnp.flip(Cm, 1)).reshape(b, l, DIN), 1)
            zero = jnp.zeros((b, 1, DIN), u.dtype)
            y = jnp.concatenate([zero, y_fw[:, :-1]], 1) + jnp.concatenate([y_bw[:, 1:], zero], 1)
            y = y + xs * jnp.repeat(xs @ fcD_w.T + D, HD, axis=-1)
            yz = y * jax.nn.silu(z)
            y = yz * jax.lax.rsqrt(jnp.mean(jnp.square(yz), -1, keepdims=True) + 1e-05) * norm_w
            return y @ out_w.T
        key = jax.random.key(seed)
        ks = jax.random.split(key, 12)
        rn = lambda k, shape, s=0.02: jax.random.normal(k, shape, jnp.float32) * s
        dt = jnp.exp(jax.random.uniform(ks[5], (NH,), jnp.float32, np.log(0.001), np.log(0.1)))
        return dict(x=jax.random.normal(ks[0], (SEQ, BATCH, HID), jnp.float32), w_down=rn(ks[1], (DM, HID)), b_down=jnp.zeros((DM,), jnp.float32), w_up=rn(ks[2], (HID, DM)), b_up=jnp.zeros((HID,), jnp.float32), gate1=jnp.asarray(0.6, jnp.float32), hy_in_w=rn(ks[3], (DIN_PROJ, DM)), hy_conv_w=rn(ks[4], (CONV_DIM, 1, DCONV), 0.2), hy_conv_b=jnp.zeros((CONV_DIM,), jnp.float32), hy_dt_bias=jnp.log(jnp.expm1(dt)), hy_A_log=jnp.log(jax.random.uniform(ks[6], (NH,), jnp.float32, 1.0, 16.0)), hy_D=jnp.ones((NH,), jnp.float32), hy_fcD_w=rn(ks[7], (NH, DIN)), hy_norm_w=jnp.ones((DIN,), jnp.float32), hy_out_w=rn(ks[8], (DM, DIN)))
    _L1_attn_all = _L1_attn_setup()
    _L1_attn_in = {k: v for k, v in _L1_attn_all.items() if k in ('w_down', 'b_down', 'w_up', 'b_up', 'gate1', 'hy_in_w', 'hy_conv_w', 'hy_conv_b', 'hy_dt_bias', 'hy_A_log', 'hy_D', 'hy_fcD_w', 'hy_norm_w', 'hy_out_w')}
    del _L1_attn_all

    def _L1_ffn_setup():
        import jax, jax.numpy as jnp
        import numpy as np
        BATCH, SEQ, D = (2, 512, 1024)
        K, TOPK, RANK = (64, 16, 16)
        ALPHA = 32.0
        SCALING = ALPHA / RANK
        key = jax.random.key(seed)
        k1, k2, k3, k4 = jax.random.split(key, 4)
        x = jax.random.normal(k1, (BATCH, SEQ, D), dtype=jnp.float32)
        A = jax.random.normal(k2, (K, RANK, D), dtype=jnp.float32) * 0.02
        B = jax.random.normal(k3, (K, D, RANK), dtype=jnp.float32) * 0.02
        Wr = jax.random.normal(k4, (K, D), dtype=jnp.float32) * 0.02
        return {'x': x, 'A': A, 'B': B, 'Wr': Wr}
    _L1_ffn_all = _L1_ffn_setup()
    _L1_ffn_in = {k: v for k, v in _L1_ffn_all.items() if k in ('A', 'B', 'Wr')}
    del _L1_ffn_all
    return {'x': x, 'L0_tok_embed_table': _L0_tok_in['embed_table'], 'L0_tok_W1': _L0_tok_in['W1'], 'L0_tok_b1': _L0_tok_in['b1'], 'L0_tok_W2': _L0_tok_in['W2'], 'L0_tok_b2': _L0_tok_in['b2'], 'L0_tok_W3': _L0_tok_in['W3'], 'L0_tok_b3': _L0_tok_in['b3'], 'L0_attn_bv_q': _L0_attn_in['bv_q'], 'L0_attn_bv_k': _L0_attn_in['bv_k'], 'L0_attn_bv_v': _L0_attn_in['bv_v'], 'L0_ffn_base_W': _L0_ffn_in['base_W'], 'L0_ffn_base_b': _L0_ffn_in['base_b'], 'L0_ffn_router_W': _L0_ffn_in['router_W'], 'L0_ffn_router_b': _L0_ffn_in['router_b'], 'L0_ffn_A': _L0_ffn_in['A'], 'L0_ffn_B': _L0_ffn_in['B'], 'L0_ffn_expert_map': _L0_ffn_in['expert_map'], 'L1_attn_w_down': _L1_attn_in['w_down'], 'L1_attn_b_down': _L1_attn_in['b_down'], 'L1_attn_w_up': _L1_attn_in['w_up'], 'L1_attn_b_up': _L1_attn_in['b_up'], 'L1_attn_gate1': _L1_attn_in['gate1'], 'L1_attn_hy_in_w': _L1_attn_in['hy_in_w'], 'L1_attn_hy_conv_w': _L1_attn_in['hy_conv_w'], 'L1_attn_hy_conv_b': _L1_attn_in['hy_conv_b'], 'L1_attn_hy_dt_bias': _L1_attn_in['hy_dt_bias'], 'L1_attn_hy_A_log': _L1_attn_in['hy_A_log'], 'L1_attn_hy_D': _L1_attn_in['hy_D'], 'L1_attn_hy_fcD_w': _L1_attn_in['hy_fcD_w'], 'L1_attn_hy_norm_w': _L1_attn_in['hy_norm_w'], 'L1_attn_hy_out_w': _L1_attn_in['hy_out_w'], 'L1_ffn_A': _L1_ffn_in['A'], 'L1_ffn_B': _L1_ffn_in['B'], 'L1_ffn_Wr': _L1_ffn_in['Wr']}

def reference(x, L0_tok_embed_table, L0_tok_W1, L0_tok_b1, L0_tok_W2, L0_tok_b2, L0_tok_W3, L0_tok_b3, L0_attn_bv_q, L0_attn_bv_k, L0_attn_bv_v, L0_ffn_base_W, L0_ffn_base_b, L0_ffn_router_W, L0_ffn_router_b, L0_ffn_A, L0_ffn_B, L0_ffn_expert_map, L1_attn_w_down, L1_attn_b_down, L1_attn_w_up, L1_attn_b_up, L1_attn_gate1, L1_attn_hy_in_w, L1_attn_hy_conv_w, L1_attn_hy_conv_b, L1_attn_hy_dt_bias, L1_attn_hy_A_log, L1_attn_hy_D, L1_attn_hy_fcD_w, L1_attn_hy_norm_w, L1_attn_hy_out_w, L1_ffn_A, L1_ffn_B, L1_ffn_Wr):
    import jax
    import jax.numpy as jnp

    def _L0_tok_ref(input_ids, embed_table, W1, b1, W2, b2, W3, b3):
        import math
        import jax, jax.numpy as jnp
        import numpy as np
        N_TOK = 8000
        CANVAS = 125
        SIN_DIM = 128
        HID = 256
        TOK_DIM = 1024
        E = 4
        B, S = (4, 512)

        def _sinusoidal(added_idx):
            x = added_idx.astype(jnp.float32) / CANVAS * CANVAS
            half = SIN_DIM // 2
            freqs = jnp.exp(jnp.arange(half, dtype=jnp.float32) * (-math.log(100.0) / (half - 1)))
            ang = x[..., None] * freqs
            return jnp.concatenate([jnp.sin(ang), jnp.cos(ang)], axis=-1)
        diff = input_ids - N_TOK
        q = jnp.floor_divide(diff, CANVAS)
        added = jnp.where(diff < 0, 0, diff)
        llm_idx = jnp.where(diff < 0, input_ids, 0)
        sin_vec = _sinusoidal(added)
        h = jax.nn.softplus(jnp.einsum('bsd,edh->ebsh', sin_vec, W1) + b1[:, None, None, :])
        h = jax.nn.softplus(jnp.einsum('ebsh,ehk->ebsk', h, W2) + b2[:, None, None, :])
        pos = jnp.einsum('ebsk,eko->ebso', h, W3) + b3[:, None, None, :]
        out = embed_table[llm_idx]
        for e in range(E):
            out = jnp.where((q == e)[..., None], pos[e], out)
        return out

    def _L0_attn_ref(x, bv_q, bv_k, bv_v):
        import jax, jax.numpy as jnp
        import numpy as np
        HDC_DIM = 1024
        N_HEADS = 4
        HEAD_DIM = HDC_DIM // N_HEADS

        def _ste_sign(w):
            alpha = jnp.mean(jnp.abs(w), axis=-1, keepdims=True)
            hard = alpha * jnp.sign(w)
            hard = jnp.where(hard == 0, alpha, hard)
            return jax.lax.stop_gradient(hard - w) + w
        B, T, D = x.shape
        H, HD = (N_HEADS, HEAD_DIM)
        scale = HD ** (-0.5)
        q_bind = _ste_sign(bv_q)
        k_bind = _ste_sign(bv_k)
        v_bind = _ste_sign(bv_v)
        xh = x.reshape(B, T, H, HD)
        Q = xh * q_bind
        K = xh * k_bind
        V = xh * v_bind
        scores = jnp.einsum('bthd,bshd->bhts', Q, K) * scale
        causal = jnp.tril(jnp.ones((T, T), dtype=bool))
        attn = jnp.where(causal, jax.nn.sigmoid(scores * 4.0), 0.0)
        out = jnp.einsum('bhts,bshd->bthd', attn, V)
        return out.reshape(B, T, D)

    def _L0_ffn_ref(x, base_W, base_b, router_W, router_b, A, B, expert_map):
        import jax, jax.numpy as jnp
        import numpy as np
        SCALING = 32.0 / 16.0
        E = A.shape[0]
        base_out = jnp.einsum('btd,od->bto', x, base_W) + base_b
        logits = jnp.einsum('btd,nd->btn', x, router_W) + router_b
        probs = jax.nn.softmax(logits, axis=-1)
        topk_p, topk_i = jax.lax.top_k(probs, E)
        mapped = expert_map[topk_i]
        onehot = (mapped[..., None] == jnp.arange(E)).astype(x.dtype)
        w = jnp.einsum('btk,btke->bte', topk_p, onehot)
        h = jnp.einsum('btd,erd->bter', x, A)
        lora = jnp.einsum('bter,eor->bto', h * w[..., None], B) * SCALING
        return base_out + lora

    def _L1_attn_ref(x, w_down, b_down, w_up, b_up, gate1, hy_in_w, hy_conv_w, hy_conv_b, hy_dt_bias, hy_A_log, hy_D, hy_fcD_w, hy_norm_w, hy_out_w):
        import jax, jax.numpy as jnp
        import numpy as np
        HID = 1024
        DM = 128
        DIN = 2 * DM
        DST = 16
        HD = 64
        NH = DIN // HD
        DCONV = 7
        CONV_DIM = DIN + 2 * DST
        DIN_PROJ = 2 * DIN + 2 * DST + 2 * NH
        SEQ, BATCH = (512, 4)

        def _causal_conv(x, w, b):
            y = jax.lax.conv_general_dilated(jnp.transpose(x, (0, 2, 1)), w, (1,), [(DCONV - 1, 0)], feature_group_count=CONV_DIM, dimension_numbers=('NCH', 'OIH', 'NCH'))
            return jnp.transpose(y, (0, 2, 1)) + b

        def _ssm_scan(x, dt, A, B, C):
            dA = jnp.exp(dt * A)
            dBx = dt[..., None] * x

            def step(h, t):
                dA_t, dBx_t, B_t, C_t = t
                h = dA_t[:, :, None, None] * h + dBx_t[..., None] * B_t[:, None, None, :]
                y = jnp.einsum('bhpn,bn->bhp', h, C_t)
                return (h, y)
            h0 = jnp.zeros((x.shape[0], NH, HD, DST), x.dtype)
            _, ys = jax.lax.scan(step, h0, (jnp.moveaxis(dA, 1, 0), jnp.moveaxis(dBx, 1, 0), jnp.moveaxis(B, 1, 0), jnp.moveaxis(C, 1, 0)))
            return jnp.moveaxis(ys, 0, 1)

        def _hydra(u, in_w, conv_w, conv_b, dt_bias, A_log, D, fcD_w, norm_w, out_w):
            b, l, _ = u.shape
            zxbcdt = u @ in_w.T
            z = zxbcdt[..., :DIN]
            xBC = zxbcdt[..., DIN:DIN + CONV_DIM]
            dt2 = zxbcdt[..., DIN + CONV_DIM:]
            dt_fw = jax.nn.softplus(dt2[..., :NH] + dt_bias)
            dt_bw = jax.nn.softplus(jnp.flip(dt2[..., NH:], 1) + dt_bias)
            xBC = jax.nn.silu(_causal_conv(xBC, conv_w, conv_b))
            xs = xBC[..., :DIN]
            Bm = xBC[..., DIN:DIN + DST]
            Cm = xBC[..., DIN + DST:]
            A = -jnp.exp(A_log)
            x4 = xs.reshape(b, l, NH, HD)
            y_fw = _ssm_scan(x4, dt_fw, A, Bm, Cm).reshape(b, l, DIN)
            y_bw = jnp.flip(_ssm_scan(jnp.flip(x4, 1), dt_bw, A, jnp.flip(Bm, 1), jnp.flip(Cm, 1)).reshape(b, l, DIN), 1)
            zero = jnp.zeros((b, 1, DIN), u.dtype)
            y = jnp.concatenate([zero, y_fw[:, :-1]], 1) + jnp.concatenate([y_bw[:, 1:], zero], 1)
            y = y + xs * jnp.repeat(xs @ fcD_w.T + D, HD, axis=-1)
            yz = y * jax.nn.silu(z)
            y = yz * jax.lax.rsqrt(jnp.mean(jnp.square(yz), -1, keepdims=True) + 1e-05) * norm_w
            return y @ out_w.T
        x_init = x
        h = x @ w_down.T + b_down
        h = jnp.transpose(h, (1, 0, 2))
        h = jax.nn.gelu(h, approximate=False)
        xmid = h
        hp = (hy_in_w, hy_conv_w, hy_conv_b, hy_dt_bias, hy_A_log, hy_D, hy_fcD_w, hy_norm_w, hy_out_w)
        h = _hydra(h, *hp)
        h = _hydra(h, *hp)
        alpha = jax.nn.sigmoid(gate1)
        h = alpha * xmid + (1.0 - alpha) * h
        h = xmid + h
        h = h @ w_up.T + b_up
        return x_init + jnp.transpose(h, (1, 0, 2))

    def _L1_ffn_ref(x, A, B, Wr):
        import jax, jax.numpy as jnp
        import numpy as np
        BATCH, SEQ, D = (2, 512, 1024)
        K, TOPK, RANK = (64, 16, 16)
        ALPHA = 32.0
        SCALING = ALPHA / RANK
        prefix = x.shape[:-1]
        xf = x.reshape(-1, x.shape[-1])
        N = xf.shape[0]
        scores = xf @ Wr.T
        top_vals, top_idx = jax.lax.top_k(scores, TOPK)
        gates = jax.nn.softmax(top_vals, axis=-1)
        G = jnp.zeros((N, K), xf.dtype).at[jnp.arange(N)[:, None], top_idx].set(gates)
        h = jnp.einsum('nd,krd->nkr', xf, A)
        out = jnp.einsum('nkr,kdr->nd', h * G[:, :, None], B)
        return (out * SCALING).reshape(*prefix, -1)
    h = _L0_tok_ref(x, L0_tok_embed_table, L0_tok_W1, L0_tok_b1, L0_tok_W2, L0_tok_b2, L0_tok_W3, L0_tok_b3)
    h = h + _L0_attn_ref(_layernorm(h, axis=-1), L0_attn_bv_q, L0_attn_bv_k, L0_attn_bv_v)
    h = h + _L0_ffn_ref(_layernorm(h, axis=-1), L0_ffn_base_W, L0_ffn_base_b, L0_ffn_router_W, L0_ffn_router_b, L0_ffn_A, L0_ffn_B, L0_ffn_expert_map)
    h = h + _L1_attn_ref(_layernorm(h, axis=-1), L1_attn_w_down, L1_attn_b_down, L1_attn_w_up, L1_attn_b_up, L1_attn_gate1, L1_attn_hy_in_w, L1_attn_hy_conv_w, L1_attn_hy_conv_b, L1_attn_hy_dt_bias, L1_attn_hy_A_log, L1_attn_hy_D, L1_attn_hy_fcD_w, L1_attn_hy_norm_w, L1_attn_hy_out_w)
    h = h + _L1_ffn_ref(_layernorm(h, axis=-1), L1_ffn_A, L1_ffn_B, L1_ffn_Wr)
    return h

_drawn_inputs = setup_inputs


def setup_inputs(seed=0):
    import zlib

    import numpy as np

    out = dict(_drawn_inputs(seed))
    spreads = {'L0_tok_b1': (0.0, 0.63),
     'L0_tok_b2': (0.0, 0.1),
     'L0_tok_b3': (0.0, 0.1),
     'L1_attn_b_down': (0.0, 0.79),
     'L1_attn_b_up': (0.0, 0.1),
     'L1_attn_hy_conv_b': (0.0, 0.8),
     'L1_attn_hy_D': (1.0, 0.6),
     'L1_attn_hy_norm_w': (1.0, 0.6)}
    factors = {'L0_attn_bv_q': 8.0,
     'L0_attn_bv_k': 8.0,
     'L0_ffn_base_b': 7.854,
     'L0_ffn_router_b': 6.353,
     'L1_attn_hy_in_w': 8.0,
     'L1_attn_hy_conv_w': 8.0,
     'L1_attn_hy_dt_bias': 8.0,
     'L1_attn_hy_A_log': 200.0,
     'L1_attn_hy_fcD_w': 8.0,
     'L1_attn_hy_out_w': 8.0,
     'L1_ffn_A': 4.981,
     'L1_ffn_B': 4.95,
     'L1_ffn_Wr': 5.49}
    for name, (base, spread) in spreads.items():
        noise = np.random.default_rng([zlib.crc32(name.encode()), seed]).standard_normal(out[name].shape)
        drawn = base * np.exp(spread * noise) if base else spread * noise
        out[name] = jnp.asarray(drawn.astype(out[name].dtype))
    for name, factor in factors.items():
        out[name] = (out[name] * factor).astype(out[name].dtype)
    return out
```

```python
from contextlib import ExitStack

import numpy as np
import concourse.bass as bass
from concourse import mybir

F32 = mybir.dt.float32
F32R = mybir.dt.float32r
I32 = mybir.dt.int32
ACT = mybir.ActivationFunctionType
ALU = mybir.AluOpType
AX = mybir.AxisListType.X
ds = bass.ds

P = 128
B, T, D = 8, 512, 1024
TT = T // P
DC = D // P
N_TOK, CANVAS, E_POS, HID = 8000, 125, 4, 256
N_POS = CANVAS * E_POS
H, HD = 4, 256
HC = HD // P
NR, E0, R0 = 15, 8, 16
RA = NR + 1 + E0 * R0
DM, DIN, DST, NH, HDIM, DCONV = 128, 256, 16, 4, 64, 7
KE, TOPK, RANK = 64, 16, 16
EPS = 1e-5
SKIP = 1 << 20
NEG = -3.0e38
BF = HDIM
DTB = 2 * DST
CONV = DIN + 2 * DST
NB = BF + NH
IC = 1024
NITEM = T // P
INV2PI = float(np.float32(1 / (2 * np.pi)))
PI_A, PI_B = 6.28125, float(np.float32(2 * np.pi - 6.28125))
ROUND = 12582912.0


TR2, TRW, TR3 = {0: 0}, {}, {}
_n = 2
for _t in range(TT):
    if _t < TT - 1:
        TR2[_t + 1] = _n
        _n += 2
    TRW[_t] = _n
    _n += 1
    if _t > 0:
        TR3[_t - 1] = _n
        _n += 2
TR3[TT - 1] = _n


class Chain:

    def __init__(self, eng, sem):
        self.eng, self.sem, self.n = eng, sem, 0

    def __call__(self, ins):
        self.n += 1
        ins.then_inc(self.sem, 1)
        self.eng.wait_ge(self.sem, self.n)

    def restart(self):
        self.eng.sem_clear(self.sem)
        self.n = 0


class Norm:

    def __init__(self, nc, ctx, name):
        sb = lambda n, s: ctx.enter_context(nc.sbuf_tensor(name + n, s, F32))
        self.stats, self.mean_var, self.var, self.rstd = sb("stats", [P, 2, 6]), sb("mv", [P, 2]), sb("var", [P, 1]), sb("rstd", [P, 1])
        self.scale, self.shift = sb("scale", [P, 1]), sb("shift", [P, 1])
        self.var_ready = ctx.enter_context(nc.semaphore(name + "var_ready"))
        self.rstd_ready = ctx.enter_context(nc.semaphore(name + "rstd_ready"))

    def rows(self, dve, chain, dst, src, n):
        dve.bn_stats(self.stats[:, 0, :], src[:, 0:D // 2])
        chain(dve.bn_stats(self.stats[:, 1, :], src[:, D // 2:D]))
        chain(dve.bn_aggr(self.mean_var[:], self.stats[:]))
        dve.tensor_scalar(self.var[:], self.mean_var[:, 1:2], EPS, None, ALU.add).then_inc(self.var_ready, 1)
        dve.wait_ge(self.rstd_ready, n + 1)
        return dve.tensor_scalar(dst, src, self.mean_var[:, 0:1], self.rstd[:, 0:1], ALU.subtract, ALU.mult)

    def with_residual(self, dve, chain, rows):
        dve.tensor_scalar(self.scale[:], self.rstd[:], 1.0, None, ALU.add)
        chain(dve.scalar_tensor_tensor(self.shift[:], self.mean_var[:, 0:1], -1.0, self.rstd[:], ALU.mult, ALU.mult))
        return dve.tensor_scalar(rows, rows, self.scale[:, 0:1], self.shift[:, 0:1], ALU.mult, ALU.add)

    def serve(self, pool, neg_half, n):
        pool.wait_ge(self.var_ready, n + 1)
        pool.tensor_tensor(self.rstd[:], self.var[:], neg_half[:], ALU.pow).then_inc(self.rstd_ready, 1)


def tables(nc, I, persist, W, scratch):
    ident, ids_emb, ids_pos = persist["ident"], persist["ids_emb"], persist["ids_pos"]
    baseH, baseL, qk, vb = W["baseH"], W["baseL"], W["qk"], W["vb"]
    with ExitStack() as ctx:
        sb = lambda n, s, d=F32: ctx.enter_context(nc.sbuf_tensor(n, s, d))
        sem = lambda n: ctx.enter_context(nc.semaphore(n))
        pos_in = sb("pos_in", [P, 2 + N_POS])
        ang = sb("ang", [P, N_POS])
        turns = sb("turns", [P, N_POS])
        w1, w2, w3 = sb("w1", [P, HID]), sb("w2", [P, 2, HID]), sb("w3", [P, 2, D])
        b12, b3 = sb("b12", [P, 2 * E_POS, 2]), sb("b3", [CANVAS, D])
        h1, h2 = sb("h1", [P, 2, CANVAS]), sb("h2", [P, 2, CANVAS])
        absx, lnx = sb("absx", [P, 2, CANVAS]), sb("lnx", [P, 2, CANVAS])
        posrow = sb("posrow", [CANVAS, D])
        stage = sb("stage", [P, 2, D])
        bq, bk, bv = sb("bq", [P, H, HD]), sb("bk", [P, H, HD]), sb("bv", [P, H, HD])
        sgn, alpha = sb("sgn", [P, H, HD]), sb("alpha", [P, H])
        idf, t0, t1, t2 = (sb(n, [P, (B + 1) * TT]) for n in ("idf", "t0", "t1", "t2"))
        ids = sb("ids", [P, (B + 1) * TT], I32)
        ph = ctx.enter_context(nc.psum_tensor("ph", [P, 2, 512], F32))
        pp = ctx.enter_context(nc.psum_tensor("pp", [P, 2, 512], F32))
        pq = ctx.enter_context(nc.psum_tensor("pq", [P, 2, 512], F32))
        in_ld, const_ld, stage_ld = sem("in_ld"), sem("const_ld"), [sem("stage_ld0"), sem("stage_ld1")]
        w_ld, pos_st = sem("w_ld"), sem("pos_st")
        stage_used, ident_done = sem("stage_used"), sem("ident_done")
        ang_ready, sin_ready = sem("ang_ready"), sem("sin_ready")
        h_full, h_pre, h_exp, h_ready = sem("h_full"), sem("h_pre"), sem("h_exp"), sem("h_ready")
        pos_full, pos_ready = sem("pos_full"), sem("pos_ready")
        qk_row, qk_full = sem("qk_row"), sem("qk_full")
        vchain = sem("vchain")
        block = ctx.enter_context(nc.Block())

        @block.sync
        def _(sp):
            sp.dma_start(pos_in[:], I["pos_const"]).then_inc(in_ld, 16)
            sp.dma_start(ids[:], I["ids"]).then_inc(in_ld, 16)
            sp.dma_start(b12[:], I["b12"]).then_inc(in_ld, 16)
            for t, name in ((bq, "bv_q"), (bk, "bv_k"), (bv, "bv_v")):
                sp.dma_start(t[:].rearrange("p h d -> p (h d)"), I[name].to_broadcast([P, D])).then_inc(in_ld, 16)
            for e in range(E_POS):
                if e:
                    sp.wait_ge(pos_full, 2 * e)
                    sp.wait_ge(pos_ready, e)
                sp.dma_start(w1[:], I["W1"][e]).then_inc(w_ld, 16)
                sp.dma_start(w2[:], I["W2"][e].rearrange("(c p) n -> p c n", p=P)).then_inc(w_ld, 16)
                sp.dma_start(w3[:], I["W3"][e].rearrange("(c p) n -> p c n", p=P)).then_inc(w_ld, 16)
                sp.dma_start(b3[:], I["b3"][e:e + 1, :].to_broadcast([CANVAS, D])).then_inc(w_ld, 16)
                sp.wait_ge(pos_ready, e + 1)
                sp.dma_start(scratch["pos"][e * CANVAS:(e + 1) * CANVAS, :], posrow[:]).then_inc(pos_st, 16)
            sp.wait_ge(pos_st, 16 * E_POS)

        @block.scalar
        def _(act):
            act.dma_start(W["raw_ra"][:], I["ra_w"].rearrange("(c p) n -> p c n", p=P)).then_inc(const_ld, 16)
            act.dma_start(W["lora_b"][:], I["lora_b"]).then_inc(const_ld, 16)
            act.dma_start(W["down"][:], I["w_down"].rearrange("(c p) n -> p c n", p=P)).then_inc(const_ld, 16)
            act.dma_start(W["b_down"][:], I["b_down"]).then_inc(const_ld, 16)
            act.dma_start(W["base_b"][:], I["base_b"].to_broadcast([P, D])).then_inc(const_ld, 16)
            act.dma_start(W["router_b"][:], I["router_b"].to_broadcast([P, NR])).then_inc(const_ld, 16)
            act.dma_start(W["emap_i"][:], I["expert_map"].to_broadcast([P, NR])).then_inc(const_ld, 16)
            for c in range(2):
                act.dma_start(stage[:, c, :], I["base_w"][c * P:(c + 1) * P, :]).then_inc(stage_ld[c % 2], 16)
            act.wait_ge(ang_ready, 1)
            act.activation(ang[:], ang[:], ACT.Sin).then_inc(sin_ready, 1)
            for s in range(2 * E_POS):
                act.wait_ge(h_pre, s + 1)
                act.activation(lnx[:], absx[:], ACT.Exp).then_inc(h_exp, 1)
                act.wait_ge(h_exp, 2 * s + 1)
                act.activation(lnx[:], lnx[:], ACT.Ln, bias=1.0).then_inc(h_exp, 1)
            for c in range(2, DC):
                act.wait_ge(stage_used, c - 1)
                act.dma_start(stage[:, c % 2, :], I["base_w"][c * P:(c + 1) * P, :]).then_inc(stage_ld[c % 2], 16)
            act.wait_ge(const_ld, 16 * 7)

        @block.gpsimd
        def _(pool):
            pool.memset(persist["neg_half"][:], -0.5)
            pool.memset(ident[:], 0.0).then_inc(ident_done, 1)
            pool.memset(persist["causal"][:], 1.0).then_inc(ident_done, 1)
            pool.wait_ge(ident_done, 2)
            pool.affine_select(out=ident[:], in_=ident[:], compare_op=ALU.not_equal, fill=1.0, base=0,
                               pattern=[[-1, P]], channel_multiplier=1).then_inc(ident_done, 1)
            pool.affine_select(out=persist["causal"][:], in_=persist["causal"][:], compare_op=ALU.is_ge, fill=0.0,
                               base=0, pattern=[[1, P]], channel_multiplier=-1).then_inc(ident_done, 1)

        @block.vector
        def _(dve):
            chain = Chain(dve, vchain)
            dve.wait_ge(in_ld, 16 * 6)
            chain(dve.tensor_scalar(turns[:], pos_in[:, 2:], 1.0 / CANVAS, float(CANVAS), ALU.mult, ALU.mult))
            chain(dve.tensor_scalar(ang[:], turns[:], pos_in[:, 0:1], None, ALU.mult))
            chain(dve.tensor_scalar(turns[:], ang[:], INV2PI, None, ALU.mult))
            chain(dve.tensor_scalar(turns[:], turns[:], pos_in[:, 1:2], ROUND, ALU.add, ALU.add))
            chain(dve.tensor_scalar(turns[:], turns[:], -ROUND, None, ALU.add))
            chain(dve.scalar_tensor_tensor(ang[:], turns[:], -PI_A, ang[:], ALU.mult, ALU.add))
            chain(dve.scalar_tensor_tensor(ang[:], turns[:], -PI_B, ang[:], ALU.mult, ALU.add))
            chain(dve.tensor_scalar(turns[:, 0:1], pos_in[:, 1:2], float(2 * np.pi), None, ALU.mult))
            chain(dve.tensor_scalar(ang[:], ang[:], turns[:, 0:1], None, ALU.add))
            dve.tensor_scalar(ang[:], ang[:], 3.1415925, -3.1415925, ALU.min, ALU.max).then_inc(ang_ready, 1)

            chain(dve.tensor_copy(idf[:], ids[:]))
            chain(dve.tensor_scalar(t0[:], idf[:], 0.0, float(N_TOK), ALU.is_lt, ALU.mult))
            chain(dve.tensor_scalar(t1[:], idf[:], float(N_TOK), None, ALU.is_ge))
            chain(dve.tensor_scalar(t2[:], idf[:], float(N_TOK + N_POS), None, ALU.is_ge))
            chain(dve.tensor_tensor(idf[:], idf[:], t0[:], ALU.add))
            chain(dve.tensor_scalar(t0[:], t1[:], -1.0, 1.0, ALU.mult, ALU.add))
            chain(dve.tensor_tensor(t0[:], t0[:], idf[:], ALU.mult))
            chain(dve.tensor_tensor(t1[:], t1[:], t2[:], ALU.subtract))
            chain(dve.scalar_tensor_tensor(t0[:], t1[:], float(SKIP), t0[:], ALU.mult, ALU.add))
            chain(dve.tensor_copy(ids_emb[:], t0[:]))
            chain(dve.tensor_scalar(t0[:], idf[:], -float(N_TOK), None, ALU.add))
            chain(dve.tensor_tensor(t0[:], t0[:], t1[:], ALU.mult))
            chain(dve.tensor_scalar(t1[:], t1[:], -float(SKIP), float(SKIP), ALU.mult, ALU.add))
            chain(dve.tensor_tensor(t0[:], t0[:], t1[:], ALU.add))
            chain(dve.tensor_copy(ids_pos[:], t0[:]))

            for src, dst in ((bq, bq), (bk, bk), (bv, vb)):
                chain(dve.tensor_reduce(alpha[:], src[:], AX, ALU.add, apply_absolute_value=True))
                chain(dve.tensor_scalar(alpha[:], alpha[:], 1.0 / HD, None, ALU.mult))
                chain(dve.tensor_scalar(sgn[:], src[:], 0.0, 2.0, ALU.is_ge, ALU.mult))
                for h in range(H):
                    last = dve.tensor_scalar(sgn[:, h, :], sgn[:, h, :], -1.0, alpha[:, h:h + 1], ALU.add, ALU.mult)
                    chain(last)
                chain(dve.tensor_tensor(sgn[:], sgn[:], src[:], ALU.subtract))
                chain(dve.tensor_tensor(dst[:], sgn[:], src[:], ALU.add))
            dve.tensor_tensor(bq[:], bq[:], bk[:], ALU.mult).then_inc(qk_row, 1)

            dve.wait_ge(ident_done, 4)
            for n in range(2):
                dve.wait_ge(qk_full, n + 1)
                chain(dve.tensor_copy(qk[:, 4 * n:4 * n + 4], pq[:, n, 0:512:P]))

            def split_base(c):
                dve.wait_ge(stage_ld[c % 2], 16 * (c // 2 + 1))
                chain(dve.tensor_copy(baseH[:, c, :], stage[:, c % 2, :]))
                dve.tensor_tensor(baseL[:, c, :], stage[:, c % 2, :], baseH[:, c, :].bitcast(F32),
                                  ALU.subtract).then_inc(stage_used, 1)

            split_base(0)
            split_base(1)
            for e in range(E_POS):
                for layer, h in ((0, h1), (1, h2)):
                    s = 2 * e + layer
                    dve.wait_ge(h_full, s + 1)
                    for c in range(2):
                        chain(dve.tensor_scalar(h[:, c, :], ph[:, c, 0:CANVAS], b12[:, 2 * e + layer, c:c + 1], None, ALU.add))
                    dve.scalar_tensor_tensor(absx[:], h[:], -1.0, h[:], ALU.mult, ALU.min).then_inc(h_pre, 1)
                    chain(dve.tensor_scalar(h[:], h[:], 0.0, None, ALU.max))
                    dve.wait_ge(h_exp, 2 * s + 2)
                    dve.tensor_tensor(h[:], h[:], lnx[:], ALU.add).then_inc(h_ready, 1)
                dve.wait_ge(w_ld, 64 * (e + 1))
                dve.wait_ge(pos_full, 2 * e + 2)
                if e:
                    dve.wait_ge(pos_st, 16 * e)
                chain(dve.tensor_tensor(posrow[:, 0:512], pp[0:CANVAS, 0, :], b3[:, 0:512], ALU.add))
                dve.tensor_tensor(posrow[:, 512:D], pp[0:CANVAS, 1, :], b3[:, 512:D], ALU.add).then_inc(pos_ready, 1)
            for c in range(2, DC):
                split_base(c)
            dve.wait_ge(const_ld, 16 * 7)
            chain(dve.tensor_copy(W["emap"][:], W["emap_i"][:]))
            for e in range(E0):
                last = dve.tensor_scalar(W["onehot"][:, e, :], W["emap"][:], float(e), None, ALU.is_equal)
            chain(last)
            dve.wait_ge(stage_used, DC)

        @block.tensor
        def _(pe):
            pe.wait_ge(ident_done, 4)
            pe.wait_ge(qk_row, 1)
            row = bq[:].rearrange("p h d -> p (h d)")
            for c in range(DC):
                last = pe.transpose(pq[:, c // 4, (c % 4) * P:(c % 4 + 1) * P], row[:, c * P:(c + 1) * P], ident[:])
                if c % 4 == 3:
                    last.then_inc(qk_full, 1)
            pe.wait_ge(sin_ready, 1)
            for e in range(E_POS):
                pe.wait_ge(w_ld, 64 * (e + 1))
                if e:
                    pe.wait_ge(h_ready, 2 * e)
                for c in range(2):
                    last = pe.matmul(ph[:, c, 0:CANVAS], w1[:, c * P:(c + 1) * P], ang[:, e * CANVAS:(e + 1) * CANVAS],
                                     start=True, stop=True)
                last.then_inc(h_full, 1)
                pe.wait_ge(h_ready, 2 * e + 1)
                for c in range(2):
                    for k in range(2):
                        last = pe.matmul(ph[:, c, 0:CANVAS], w2[:, k, c * P:(c + 1) * P], h1[:, k, :],
                                         start=k == 0, stop=k == 1)
                last.then_inc(h_full, 1)
                pe.wait_ge(h_ready, 2 * e + 2)
                if e:
                    pe.wait_ge(pos_ready, e)
                for n in range(2):
                    for k in range(2):
                        last = pe.matmul(pp[0:CANVAS, n, :], h2[:, k, :], w3[:, k, n * 512:(n + 1) * 512],
                                         start=k == 0, stop=k == 1)
                    last.then_inc(pos_full, 1)


def attend(nc, I, persist, W, scratch):
    ident, causal = persist["ident"], persist["causal"]
    with ExitStack() as ctx:
        sb = lambda n, s, d=F32: ctx.enter_context(nc.sbuf_tensor(n, s, d))
        sem = lambda n: ctx.enter_context(nc.semaphore(n))
        norm = Norm(nc, ctx, "a_")
        NORMS = 3 * TT
        emb = sb("emb", [P, TT, D])
        x1 = sb("x1", [P, TT, D])
        xT = sb("xT", [P, DC, T])
        kT = sb("kT", [P, DC, T])
        room = nc.lookup_mloc(kT).addr
        x2HL = [nc.alloc_sbuf_tensor_at(f"x2_{k}", [P, DC, P], F32R, offset=room + k * D * 4) for k in range(4)]
        att = sb("att", [P, 2, TT, T])
        att_flat = att[:].rearrange("p a s t -> p (a s t)")
        x3 = [att_flat[:, k * D:(k + 1) * D] for k in range(2)]
        x3T = [att_flat[:, (2 + k) * D:(3 + k) * D].rearrange("p (c t) -> p c t", c=DC) for k in range(2)]
        xT_flat = xT[:].rearrange("p c t -> p (c t)")
        x2 = [xT_flat[:, k * D:(k + 1) * D] for k in range(2)]
        x2F = [xT_flat[:, (2 + k) * D:(3 + k) * D].rearrange("p (c t) -> p c t", c=DC) for k in range(2)]
        x2H, x2L = [x2HL[0][:], x2HL[2][:]], [x2HL[1][:], x2HL[3][:]]
        hres = sb("hres", [P, TT, D])
        hw, hwT = sb("hw", [P, E0 * R0]), sb("hwT", [P, P])
        lg, rep, ex, top = sb("lg", [P, NR]), sb("rep", [P, NR]), sb("ex", [P, NR]), sb("top", [P, 8])
        pr, w8 = sb("pr", [P, E0, NR]), sb("w8", [P, E0])
        nmax, esum, rinv = sb("nmax", [P, 1]), sb("esum", [P, 1]), sb("rinv", [P, 1])
        cur_emb, cur_pos = sb("cur_emb", [P, TT], I32), sb("cur_pos", [P, TT], I32)
        ps = lambda n, s: ctx.enter_context(nc.psum_tensor(n, s, F32))
        ptr = ps("ptr", [P, 2, 512])
        psc = ps("psc", [P, 2, 512])
        pout = ps("pout", [P, 2, D])
        gather_go = sem("gather_go")
        idx_ready, emb_part, emb_ready, emb_used = sem("idx_ready"), sem("emb_part"), sem("emb_ready"), sem("emb_used")
        x1_ready, tr_full, tr_out = sem("x1_ready"), sem("tr_full"), sem("tr_out")
        k_ready, sc_full, sc_sig, att_ready = sem("k_ready"), sem("sc_full"), sem("sc_sig"), sem("att_ready")
        out_full, out_free, x2_ready, x2L_ready = sem("out_full"), sem("out_free"), sem("x2_ready"), sem("x2L_ready")
        ra_full, ra_free, nmax_ready, ex_ready = sem("ra_full"), sem("ra_free"), sem("nmax_ready"), sem("ex_ready")
        hw_ready, x3_ready, down_full, down_out = sem("hw_ready"), sem("x3_ready"), sem("down_full"), sem("down_out")
        res_ready, res_stored, vchain, h2_done = sem("res_ready"), sem("res_stored"), sem("vchain2"), sem("h2_done")
        TRN = DC + 5 * TT
        block = ctx.enter_context(nc.Block())
        raw_ra, baseH, baseL, lora_b, down = W["raw_ra"], W["baseH"], W["baseL"], W["lora_b"], W["down"]

        @block.gpsimd
        def _(pool):
            neg_half = persist["neg_half"]

            def gather_tokens():
                for t in range(TT):
                    pool.indirect_dma_start(emb[:, t, :], None, I["embed"],
                                            bass.IndirectOffsetOnAxis(ap=cur_emb[:, t:t + 1], axis=0),
                                            bounds_check=N_TOK - 1, oob_is_err=False).then_inc(emb_part, 16)

            def gather_positions(i):
                pool.wait_ge(emb_part, i * 64 + 64)
                pool.sem_inc(gather_go, 1)
                for t in range(TT):
                    pool.indirect_dma_start(emb[:, t, :], None, scratch["pos"],
                                            bass.IndirectOffsetOnAxis(ap=cur_pos[:, t:t + 1], axis=0),
                                            bounds_check=N_POS - 1, oob_is_err=False).then_inc(emb_ready, 16)

            pool.wait_ge(idx_ready, 1)
            gather_tokens()
            gather_positions(0)
            for t in range(TT):
                norm.serve(pool, neg_half, t)
            with pool.Fori(0, B) as b:
                norm.serve(pool, neg_half, b * NORMS + TT)
                pool.wait_ge(emb_used, b + 1)
                pool.sem_inc(gather_go, 1)
                pool.wait_ge(idx_ready, b + 2)
                pool.sem_inc(gather_go, 1)
                gather_tokens()
                norm.serve(pool, neg_half, b * NORMS + TT + 1)
                gather_positions(b + 1)
                for n in range(TT + 2, NORMS + TT):
                    norm.serve(pool, neg_half, b * NORMS + n)

        @block.sync
        def _(sp):
            with sp.Fori(0, B) as b:
                for t in range(TT):
                    sp.wait_ge(res_ready, b * TT + t + 1)
                    sp.dma_start(scratch["res"][ds(b, 1), t, :, :].rearrange("a p d -> (a p) d"),
                                 hres[:, t, :]).then_inc(res_stored, 16)
            sp.wait_ge(res_stored, 16 * TT * B + 16)

        @block.vector
        def _(dve):
            chain = Chain(dve, vchain)

            def next_lists(i):
                dve.tensor_copy(cur_emb[:], persist["ids_emb"][:, ds(i * TT, TT)])
                dve.tensor_copy(cur_pos[:], persist["ids_pos"][:, ds(i * TT, TT)]).then_inc(idx_ready, 1)

            def norm1(i, t):
                if t == 0:
                    dve.wait_ge(emb_ready, i * 64 + 64)
                norm.rows(dve, chain, x1[:, t, :], emb[:, t, :], count()).then_inc(x1_ready, 1)

            done = [0, 0]

            def count():
                done[1] += 1
                return done[0] + done[1] - 1

            next_lists(0)
            for t in range(TT):
                norm1(0, t)
            chain.restart()
            with dve.Fori(0, B) as b:
                done[:] = [b * NORMS + TT, 0]
                next_lists(b + 1)
                for c in range(DC):
                    dve.wait_ge(tr_out, b * TRN + c + 3)
                    dve.tensor_scalar(kT[:, c, :], xT[:, c, :], W["qk"][:, c:c + 1], None, ALU.mult).then_inc(k_ready, 1)

                def mask(h):
                    for s in range(TT):
                        dve.wait_ge(sc_sig, b * H * TT + h * TT + s + 3)
                        diag = att[:, h % 2, s, s * P:(s + 1) * P]
                        dve.tensor_tensor(diag, diag, causal[:], ALU.mult).then_inc(att_ready, 1)

                def add_head(h):
                    cols = slice(h * HD, (h + 1) * HD)
                    dve.wait_ge(out_full, b * (H + TT) + h + 1)
                    if h == 0:
                        dve.wait_ge(res_stored, b * 64 + 16)
                    v = W["vb"][:, h:h + 1, :].broadcast_to([P, TT, HD])
                    acc = hres[:, :, cols]
                    dve.tensor_tensor(acc, pout[:, h % 2, :].rearrange("p (t d) -> p t d", t=TT), v,
                                      ALU.mult).then_inc(out_free, 1)
                    dve.wait_ge(out_free, b * (H + TT) + h + 3)
                    ins = dve.tensor_tensor(acc, acc, emb[:, :, cols], ALU.add)
                    chain(ins)
                    if h == H - 1:
                        dve.engine_nop().then_inc(emb_used, 1)

                mask(0)
                mask(1)
                add_head(0)
                mask(2)
                add_head(1)
                mask(3)
                add_head(2)
                add_head(3)

                def norm2(t):
                    norm.rows(dve, chain, x2[t % 2], hres[:, t, :], count()).then_inc(x2_ready, 1)
                    dve.tensor_tensor(hres[:, t, :], hres[:, t, :], W["base_b"][:], ALU.add).then_inc(h2_done, 1)

                def low_part(t):
                    dve.wait_ge(tr_out, b * TRN + DC + TR2[t] + 4)
                    dve.tensor_tensor(x2L[t % 2], x2F[t % 2], x2H[t % 2].bitcast(F32), ALU.subtract).then_inc(x2L_ready, 1)

                def route(t):
                    dve.wait_ge(ra_full, b * TT + t + 1)
                    chain(dve.tensor_tensor(lg[:], psc[:, 0, 0:NR], W["router_b"][:], ALU.add))
                    chain(dve.max(top[:], lg[:]))
                    dve.tensor_scalar(nmax[:], top[:, 0:1], -1.0, None, ALU.mult).then_inc(nmax_ready, 1)
                    chain(dve.match_replace(rep[:], top[:], lg[:], NEG))
                    dve.wait_ge(ex_ready, b * TT + t + 1)
                    chain(dve.scalar_tensor_tensor(rep[:], rep[:], -1e38, ex[:], ALU.is_lt, ALU.mult))
                    chain(dve.reciprocal(rinv[:], esum[:]))
                    chain(dve.tensor_tensor(pr[:], W["onehot"][:],
                                            rep[:].rearrange("p (a n) -> p a n", a=1).broadcast_to([P, E0, NR]), ALU.mult))
                    chain(dve.tensor_reduce(w8[:], pr[:], AX, ALU.add))
                    chain(dve.tensor_scalar(w8[:], w8[:], rinv[:, 0:1], 2.0, ALU.mult, ALU.mult))
                    chain(dve.tensor_tensor(hw[:].rearrange("p (e r) -> p e r", e=E0),
                                            psc[:, 0, NR + 1:RA].rearrange("p (e r) -> p e r", e=E0),
                                            w8[:].rearrange("p (e a) -> p e a", a=1).broadcast_to([P, E0, R0]), ALU.mult))
                    dve.engine_nop().then_inc(hw_ready, 1)
                    dve.engine_nop().then_inc(ra_free, 1)

                def add_ffn(t):
                    dve.wait_ge(out_full, b * (H + TT) + H + t + 1)
                    dve.wait_ge(h2_done, b * TT + t + 1)
                    dve.tensor_tensor(hres[:, t, :], hres[:, t, :], pout[:, t % 2, :], ALU.add).then_inc(out_free, 1)
                    dve.wait_ge(out_free, b * (H + TT) + H + t + 3)
                    norm.rows(dve, chain, x3[t % 2], hres[:, t, :], count()).then_inc(x3_ready, 1)
                    norm.with_residual(dve, chain, hres[:, t, :]).then_inc(res_ready, 1)

                norm2(0)
                for t in range(TT):
                    low_part(t)
                    route(t)
                    if t < TT - 1:
                        norm2(t + 1)
                    if t >= 2:
                        norm1(b + 1, 2 * t - 4)
                        norm1(b + 1, 2 * t - 3)
                    add_ffn(t)
                chain.restart()

        @block.scalar
        def _(act):
            act.sem_inc(tr_out, 2)
            act.sem_inc(sc_sig, 2)
            act.sem_inc(down_out, 1)
            act.sem_inc(out_free, 2)
            act.sem_inc(ra_free, 1)
            act.sem_inc(res_stored, 16)
            with act.Fori(0, B) as b:
                n = 0

                def take(dst, n):
                    act.wait_ge(tr_full, b * TRN + n + 1)
                    act.activation(dst, ptr[:, n % 2, :], ACT.Copy).then_inc(tr_out, 1)

                for c in range(DC):
                    take(xT[:, c, :], c)
                for h in range(H):
                    if h >= 2:
                        act.wait_ge(out_full, b * (H + TT) + h - 1)
                    for s in range(TT):
                        k = h * TT + s
                        act.wait_ge(sc_full, b * H * TT + k + 1)
                        act.activation(att[:, h % 2, s, s * P:T], psc[:, k % 2, 0:T - s * P], ACT.Sigmoid,
                                       scale=4.0 * HD ** -0.5).then_inc(sc_sig, 1)

                def take2(t):
                    for g in range(2):
                        n = DC + TR2[t] + g
                        act.wait_ge(tr_full, b * TRN + n + 1)
                        src = ptr[:, n % 2, :].rearrange("p (c t) -> p c t", c=DC // 2)
                        cs = slice(g * DC // 2, (g + 1) * DC // 2)
                        act.activation(x2F[t % 2][:, cs, :], src, ACT.Copy)
                        act.activation(x2H[t % 2][:, cs, :], src, ACT.Copy).then_inc(tr_out, 1)

                def take3(t):
                    for g in range(2):
                        n = DC + TR3[t] + g
                        act.wait_ge(tr_full, b * TRN + n + 1)
                        src = ptr[:, n % 2, :].rearrange("p (c t) -> p c t", c=DC // 2)
                        act.activation(x3T[t % 2][:, g * DC // 2:(g + 1) * DC // 2, :], src, ACT.Copy).then_inc(tr_out, 1)

                take2(0)
                for t in range(TT):
                    act.wait_ge(nmax_ready, b * TT + t + 1)
                    act.activation(ex[:], lg[:], ACT.Exp, bias=nmax[:, 0:1], accum_out=esum[:, 0:1]).then_inc(ex_ready, 1)
                    if t < TT - 1:
                        take2(t + 1)
                    n = DC + TRW[t]
                    act.wait_ge(tr_full, b * TRN + n + 1)
                    act.activation(hwT[:], ptr[:, n % 2, 0:P], ACT.Copy).then_inc(tr_out, 1)
                    if t > 0:
                        take3(t - 1)
                take3(TT - 1)
                act.wait_ge(down_full, b + 1)
                act.activation(persist["xm"][:, ds(b, T, B)], psc[:, 1, :], ACT.Gelu,
                               bias=W["b_down"][:, 0:1]).then_inc(down_out, 1)

        @block.tensor
        def _(pe):
            with pe.Fori(0, B) as b:
                def bank(n):
                    pe.wait_ge(tr_out, b * TRN + n + 1)
                    return ptr[:, n % 2, :]

                for c in range(DC):
                    if c == 0:
                        pe.wait_ge(x1_ready, b * TT + TT)
                    dst = bank(c)
                    for t in range(TT):
                        last = pe.transpose(dst[:, t * P:(t + 1) * P], x1[:, t, c * P:(c + 1) * P], ident[:])
                    last.then_inc(tr_full, 1)

                def scores(h):
                    pe.wait_ge(k_ready, b * DC + HC * (h + 1))
                    for s in range(TT):
                        k = h * TT + s
                        pe.wait_ge(sc_sig, b * H * TT + k + 1)
                        if k == 1:
                            pe.wait_ge(down_out, b + 1)
                        for c in range(HC):
                            last = pe.matmul(psc[:, k % 2, 0:T - s * P], kT[:, HC * h + c, s * P:(s + 1) * P],
                                             xT[:, HC * h + c, s * P:T], start=c == 0, stop=c == HC - 1)
                        last.then_inc(sc_full, 1)

                def attn_out(h):
                    pe.wait_ge(att_ready, b * H * TT + (h + 1) * TT)
                    pe.wait_ge(out_free, b * (H + TT) + h + 1)
                    for t in range(TT):
                        for s in range(t + 1):
                            last = pe.matmul(pout[:, h % 2, t * HD:(t + 1) * HD], att[:, h % 2, s, t * P:(t + 1) * P],
                                             x1[:, s, h * HD:(h + 1) * HD], start=s == 0, stop=s == t)
                    last.then_inc(out_full, 1)

                scores(0)
                scores(1)
                attn_out(0)
                scores(2)
                attn_out(1)
                scores(3)
                attn_out(2)
                attn_out(3)

                def turn(src, n0):
                    for g in range(2):
                        dst = bank(n0 + g)
                        for k in range(DC // 2):
                            c = g * DC // 2 + k
                            last = pe.transpose(dst[:, k * P:(k + 1) * P], src[:, c * P:(c + 1) * P], ident[:])
                        last.then_inc(tr_full, 1)

                def turn2(t):
                    pe.wait_ge(x2_ready, b * TT + t + 1)
                    turn(x2[t % 2], DC + TR2[t])

                def ra(t):
                    pe.wait_ge(tr_out, b * TRN + DC + TR2[t] + 4)
                    pe.wait_ge(ra_free, b * TT + t + 1)
                    for c in range(DC):
                        last = pe.matmul(psc[:, 0, 0:RA], x2F[t % 2][:, c, :], raw_ra[:, c, :], start=c == 0, stop=c == DC - 1)
                    last.then_inc(ra_full, 1)

                def base(t):
                    pe.wait_ge(out_free, b * (H + TT) + H + t + 1)
                    for k, (lhs, rhs) in enumerate(((x2H, baseH), (x2H, baseL), (x2L, baseH))):
                        if k == 2:
                            pe.wait_ge(x2L_ready, b * TT + t + 1)
                        for c in range(DC):
                            for n in range(2):
                                pe.matmul(pout[:, t % 2, n * 512:(n + 1) * 512], lhs[t % 2][:, c, :],
                                          rhs[:, c, n * 512:(n + 1) * 512], start=k == 0 and c == 0, stop=False)

                def lora(t):
                    pe.wait_ge(hw_ready, b * TT + t + 1)
                    dst = bank(DC + TRW[t])
                    pe.transpose(dst[:, 0:P], hw[:], ident[:]).then_inc(tr_full, 1)
                    pe.wait_ge(tr_out, b * TRN + DC + TRW[t] + 3)
                    for n in range(2):
                        last = pe.matmul(pout[:, t % 2, n * 512:(n + 1) * 512], hwT[:], lora_b[:, n * 512:(n + 1) * 512],
                                         start=False, stop=True)
                    last.then_inc(out_full, 1)

                def project_down(t):
                    pe.wait_ge(x3_ready, b * TT + t + 1)
                    turn(x3[t % 2], DC + TR3[t])
                    pe.wait_ge(tr_out, b * TRN + DC + TR3[t] + 4)
                    for c in range(DC):
                        last = pe.matmul(psc[:, 1, t * P:(t + 1) * P], down[:, c, :], x3T[t % 2][:, c, :],
                                         start=c == 0, stop=c == DC - 1)
                    if t == TT - 1:
                        last.then_inc(down_full, 1)

                turn2(0)
                for t in range(TT):
                    ra(t)
                    base(t)
                    if t < TT - 1:
                        turn2(t + 1)
                    lora(t)
                    if t > 0:
                        project_down(t - 1)
                project_down(TT - 1)


def hydra(nc, I, persist, scratch):
    ident = persist["ident"]
    with ExitStack() as ctx:
        sb = lambda n, s, d=F32: ctx.enter_context(nc.sbuf_tensor(n, s, d))
        sem = lambda n: ctx.enter_context(nc.semaphore(n))
        flow = sb("flow", [P, 3 * B * T])
        cur = [sb(f"cur{k}", [P, IC]) for k in range(2)]
        in_w = sb("in_w", [P, DIN])
        conv_in = sb("conv_in", [P, CONV])
        conv_w = sb("conv_w", [P, DCONV, CONV])
        dt_w, dt_bias = sb("dt_w", [P, 2 * NH]), sb("dt_bias", [DTB + 2 * NH, 1])
        conv_bx, conv_bbc = sb("conv_bx", [P, 2]), sb("conv_bbc", [2 * DST, 1])
        fcd, d_bias = sb("fcd", [P, 2, NH]), sb("d_bias", [NB, 1])
        a_half = sb("a_half", [P, 2 * NH])
        out_w, norm_w = sb("out_w", [P, 2, DM]), sb("norm_w", [P, 2])
        ones, block_mask = sb("ones", [P, P]), sb("block_mask", [P, P])
        gate = sb("gate", [P, 3])
        zs = [sb(f"zs{k}", [P, 2, IC]) for k in range(2)]
        xs = [sb(f"xs{k}", [P, 2, IC]) for k in range(2)]
        stack = [sb(f"stack{k}", [NB, IC]) for k in range(2)]
        rows = [sb(f"rows{k}", [P, B, NB]) for k in range(2)]
        xrow = [sb(f"xrow{k}", [P, B, DIN]) for k in range(2)]
        mix = [sb(f"mix{k}", [P, B, B * NH]) for k in range(2)]
        mixT = [sb(f"mixT{k}", [P, B, B * NH]) for k in range(2)]
        diag = [sb(f"diag{k}", [P, B, NH, P]) for k in range(2)]
        fwd, bwd = sb("fwd", [P, B, B, NH]), sb("bwd", [P, B, B, NH])
        cb, cbn = sb("cb", [P, B, B]), sb("cbn", [P, B, B, DST])
        dt, u, ln1, pol, dec = (sb(n, [P, B, 2 * NH]) for n in ("dt", "u", "ln1", "pol", "dec"))
        yz, sq, rs = sb("yz", [P, 2, 512]), sb("sq", [P, 2, 512]), sb("rs", [P, 512])
        eps_col = sb("eps_col", [P, 1])
        ps = lambda n, s: ctx.enter_context(nc.psum_tensor(n, s, F32))
        pcv, pst = ps("pcv", [P, 2, 512]), ps("pst", [P, 2, 512])
        py, po = ps("py", [P, 2, 512]), ps("po", [P, 2, 512])
        cur_ready = sem("cur_ready")
        w_ld, w_ready, w_half = sem("hw_ld"), sem("hw_ready2"), sem("w_half")
        cv_full, cv_out, st_full, st_out, g_full, g_out = (sem(n) for n in ("cv_full", "cv_out", "st_full", "st_out", "g_full", "g_out"))
        t_full, t_out, xr_full, xr_out = sem("t_full"), sem("t_out"), sem("xr_full"), sem("xr_out")
        u_ready, ln_ready, dec_in, dec_ready = sem("u_ready"), sem("ln_ready"), sem("dec_in"), sem("dec_ready")
        mix_ready, mix_st, mix_ld = sem("mix_ready"), [sem("mix_st0"), sem("mix_st1")], [sem("mix_ld0"), sem("mix_ld1")]
        diag_ready, y_full, yz_ready, sq_ready = sem("diag_ready"), sem("y_full"), sem("yz_ready"), sem("sq_ready")
        o_full, rs_ready, flow_ready, vchain = sem("o_full"), sem("rs_ready"), sem("flow_ready"), sem("vchain3")
        block = ctx.enter_context(nc.Block())
        NW = 13

        @block.sync
        def _(sp):
            for dst, name in ((in_w[:], "in_z"), (conv_in[:], "in_xbc"), (dt_w[:], "in_dt"), (conv_bx[:], "conv_bx"),
                              (conv_bbc[:], "conv_bbc"), (d_bias[BF:NB, :], "hy_d"), (norm_w[:], "hy_norm")):
                sp.dma_start(dst, I[name]).then_inc(w_ld, 16)
            sp.dma_start(dt_bias[DTB:DTB + 2 * NH, :], I["dt_bias"]).then_inc(w_ld, 16)
            sp.dma_start(conv_w[:].rearrange("p k c -> p (k c)"), I["conv_w"].to_broadcast([P, DCONV * CONV])).then_inc(w_ld, 16)
            sp.dma_start(fcd[:], I["fcd"].rearrange("(c p) n -> p c n", p=P)).then_inc(w_ld, 16)
            sp.dma_start(out_w[:], I["hy_out"].rearrange("(c p) n -> p c n", p=P)).then_inc(w_ld, 16)
            sp.dma_start(a_half[:], I["a_log"].to_broadcast([P, 2 * NH])).then_inc(w_ld, 16)
            sp.dma_start(gate[:, 0:1], I["gate1"].to_broadcast([P, 1])).then_inc(w_ld, 16)
            with sp.Fori(0, NITEM) as j:
                for k in range(2):
                    at = (j * 2 + k) * P
                    sp.wait_ge(mix_ready, j * 2 + k + 1)
                    sp.dma_start(scratch["mix"][ds(at, P), :], mix[k][:].rearrange("p s c -> p (s c)")).then_inc(mix_st[k], 16)
                    sp.wait_ge(mix_st[k], j * 16 + 32)
                    sp.dma_start(mixT[k][:], scratch["mix"][ds(at, P), :].rearrange("m (s c) -> (m s) c", s=B)
                                 .rearrange("(n p) c -> p n c", p=P)).then_inc(mix_ld[k], 16)

        @block.gpsimd
        def _(pool):
            pool.memset(ones[:], 1.0)
            pool.memset(eps_col[:], EPS)
            for k in range(2):
                pool.memset(stack[k][:], 0.0)
            for m in (fwd, bwd):
                pool.memset(m[:], 0.0)
            pool.memset(block_mask[:], 1.0).then_inc(w_half, 1)
            pool.wait_ge(w_half, 1)
            m = block_mask[:].rearrange("p (r t) -> p r t", t=B)
            pool.affine_select(out=m, in_=m, compare_op=ALU.is_ge, fill=0.0, base=0,
                               pattern=[[-B, 16], [0, B]], channel_multiplier=1).then_inc(w_half, 1)
            pool.wait_ge(w_half, 2)
            pool.affine_select(out=m, in_=m, compare_op=ALU.is_ge, fill=0.0, base=B - 1,
                               pattern=[[B, 16], [0, B]], channel_multiplier=-1).then_inc(w_half, 1)
            pool.wait_ge(w_half, 3)
            for m in (fwd, bwd):
                flat = m[:].rearrange("p c s h -> p (c s) h")
                pool.memset(flat[:, 0:B * B:B + 1, :], 1.0).then_inc(w_half, 1)

        @block.scalar
        def _(act):
            act.wait_ge(w_ld, 16 * NW)
            act.wait_ge(w_ready, 1)
            act.activation(a_half[:], a_half[:], ACT.Exp, scale=0.5).then_inc(w_ready, 1)
            act.activation(gate[:, 1:2], gate[:, 0:1], ACT.Sigmoid).then_inc(w_ready, 1)
            act.sem_inc(cv_out, 2)
            act.sem_inc(xr_out, 1)
            for k in range(2):
                act.sem_inc(mix_st[k], 16)
            with act.Fori(0, NITEM) as j:
                for k in range(2):
                    for blk in range(2):
                        cols = slice(blk * 512, (blk + 1) * 512)
                        n0 = 8 * k + 4 * blk
                        for c in range(4):
                            act.wait_ge(cv_full, j * 16 + n0 + c + 1)
                            dst = (zs if c < 2 else xs)[k][:, c % 2, cols]
                            bias = 0.0 if c < 2 else conv_bx[:, c % 2:c % 2 + 1]
                            act.activation(dst, pcv[:, c % 2, :], ACT.Silu, bias=bias).then_inc(cv_out, 1)
                        act.wait_ge(st_full, j * 4 + 2 * k + blk + 1)
                        act.activation(stack[k][0:2 * DST, cols], pst[0:2 * DST, blk, :], ACT.Silu, bias=conv_bbc[:, 0:1])
                        act.activation(stack[k][DTB:DTB + 2 * NH, cols], pst[DTB:DTB + 2 * NH, blk, :], ACT.Identity,
                                       bias=dt_bias[DTB:DTB + 2 * NH, 0:1]).then_inc(st_out, 1)
                    for blk in range(2):
                        cols = slice(blk * 512, (blk + 1) * 512)
                        act.wait_ge(g_full, j * 4 + 2 * k + blk + 1)
                        act.activation(stack[k][BF:NB, cols], pst[BF:NB, blk, :], ACT.Identity,
                                       bias=d_bias[BF:NB, 0:1]).then_inc(g_out, 1)
                    for half in range(2):
                        act.wait_ge(t_full, j * 4 + 2 * k + half + 1)
                        act.activation(rows[k][:, 4 * half:4 * half + 4, :],
                                       po[:, half, 0:4 * NB].rearrange("p (s n) -> p s n", s=4), ACT.Copy).then_inc(t_out, 1)
                    for n in range(4):
                        act.wait_ge(xr_full, j * 8 + 4 * k + n + 1)
                        act.activation(xrow[k][:, 2 * n:2 * n + 2, :],
                                       pst[:, n % 2, :].rearrange("p (a c) -> p a c", a=2), ACT.Copy).then_inc(xr_out, 1)
                    act.wait_ge(u_ready, j * 2 + k + 1)
                    act.activation(u[:], u[:], ACT.Exp).then_inc(ln_ready, 1)
                    act.wait_ge(ln_ready, j * 4 + 2 * k + 1)
                    act.activation(ln1[:], u[:], ACT.Ln, bias=1.0).then_inc(ln_ready, 1)
                    act.wait_ge(dec_in, j * 2 + k + 1)
                    act.activation(dec[:], dec[:], ACT.Exp, scale=-1.0).then_inc(dec_ready, 1)
                for k in range(2):
                    for blk in range(2):
                        act.wait_ge(yz_ready, j * 4 + 2 * k + blk + 1)
                        act.activation(sq[:], yz[:], ACT.Square).then_inc(sq_ready, 1)
                        act.wait_ge(o_full, j * 4 + 2 * k + blk + 1)
                        act.activation(rs[:], po[:, 1, :], ACT.Sqrt, bias=eps_col[:, 0:1], scale=1.0 / DIN).then_inc(rs_ready, 1)

        @block.vector
        def _(dve):
            chain = Chain(dve, vchain)
            dve.wait_ge(w_ld, 16 * NW)
            dve.tensor_copy(flow[:, 0:B * T], persist["xm"][:])
            dve.tensor_scalar(a_half[:], a_half[:], 88.0, None, ALU.min).then_inc(w_ready, 1)
            for k in range(DCONV):
                dve.tensor_tensor(conv_w[:, k, :], conv_w[:, k, :], conv_in[:], ALU.mult)
            for c in range(2):
                last = dve.tensor_scalar(out_w[:, c, :], out_w[:, c, :], norm_w[:, c:c + 1], None, ALU.mult)
            last.then_inc(flow_ready, 1)
            dve.wait_ge(w_ready, 3)
            chain(dve.tensor_scalar(gate[:, 0:1], gate[:, 1:2], 1.0, None, ALU.add))
            chain(dve.tensor_scalar(gate[:, 2:3], gate[:, 1:2], -1.0, 1.0, ALU.mult, ALU.add))
            dve.wait_ge(w_half, 5)
            chain.restart()
            with dve.Fori(0, NITEM) as j:
                def mixing(k):
                    r = rows[k]
                    dve.wait_ge(t_out, j * 4 + 2 * k + 2)
                    raw = r[:, :, DTB:DTB + 2 * NH]
                    dve.scalar_tensor_tensor(u[:], raw, -1.0, raw, ALU.mult, ALU.min).then_inc(u_ready, 1)
                    cc = r[:, :, DST:2 * DST].rearrange("p c (a n) -> p c a n", a=1).broadcast_to([P, B, B, DST])
                    bb = r[:, :, 0:DST].rearrange("p (a s) n -> p a s n", a=1).broadcast_to([P, B, B, DST])
                    chain(dve.tensor_tensor(cbn[:], cc, bb, ALU.mult))
                    chain(dve.tensor_reduce(cb[:], cbn[:], AX, ALU.add))
                    dve.wait_ge(ln_ready, j * 4 + 2 * k + 2)
                    chain(dve.tensor_scalar(pol[:], u[:], -1.0 / 6, None, ALU.mult))
                    for coef in (1.0 / 5, -1.0 / 4, 1.0 / 3, -1.0 / 2, 1.0):
                        chain(dve.scalar_tensor_tensor(pol[:], pol[:], coef, u[:], ALU.add, ALU.mult))
                    chain(dve.tensor_tensor(pol[:], pol[:], ln1[:], ALU.subtract))
                    chain(dve.scalar_tensor_tensor(pol[:], u[:], 0.0625, pol[:], ALU.is_lt, ALU.mult))
                    chain(dve.tensor_tensor(pol[:], pol[:], ln1[:], ALU.add))
                    chain(dve.scalar_tensor_tensor(dt[:], raw, 0.0, pol[:], ALU.max, ALU.add))
                    ah = a_half[:].rearrange("p (a h) -> p a h", a=1).broadcast_to([P, B, 2 * NH])
                    chain(dve.tensor_tensor(dec[:], dt[:], ah, ALU.mult))
                    chain(dve.scalar_tensor_tensor(dec[:], dec[:], 1e18, ah, ALU.min, ALU.mult))
                    dve.tensor_scalar(dec[:], dec[:], 200.0, None, ALU.min).then_inc(dec_in, 1)
                    dve.wait_ge(dec_ready, j * 2 + k + 1)
                    for c in range(1, B - 1):
                        a = dec[:, c:c + 1, 0:NH].broadcast_to([P, c, NH])
                        chain(dve.tensor_tensor(fwd[:, c, 0:c, :], fwd[:, c - 1, 0:c, :], a, ALU.mult))
                        d = B - 1 - c
                        a = dec[:, d:d + 1, NH:2 * NH].broadcast_to([P, c, NH])
                        chain(dve.tensor_tensor(bwd[:, d, d + 1:B, :], bwd[:, d + 1, d + 1:B, :], a, ALU.mult))
                    w = mix[k][:].rearrange("p s (t h) -> p t s h", h=NH)
                    flat = mix[k][:].rearrange("p s (t h) -> p (s t) h", h=NH)
                    scale = cbn[:].rearrange("p c s (a h) -> p c s a h", h=NH)[:, :, :, 0, :]
                    scale2 = cbn[:].rearrange("p c s (a h) -> p c s a h", h=NH)[:, :, :, 1, :]
                    cb4 = cb[:].rearrange("p c (s a) -> p c s a", a=1).broadcast_to([P, B, B, NH])
                    for dst, src, off in ((scale, fwd, 0), (scale2, bwd, NH)):
                        d4 = dt[:, :, off:off + NH].rearrange("p (a s) h -> p a s h", a=1).broadcast_to([P, B, B, NH])
                        chain(dve.tensor_tensor(dst, src[:], d4, ALU.mult))
                        chain(dve.tensor_tensor(dst, dst, cb4, ALU.mult))
                    dve.wait_ge(mix_st[k], j * 16 + 16)
                    chain(dve.tensor_copy(w[:, 1:B], scale[:, 0:B - 1]))
                    chain(dve.memset(w[:, 0:1], 0.0))
                    chain(dve.tensor_tensor(w[:, 0:B - 1], w[:, 0:B - 1], scale2[:, 1:B], ALU.add))
                    dve.tensor_copy(flat[:, 0:B * B:B + 1, :], r[:, :, BF:NB]).then_inc(mix_ready, 1)

                def spread(k):
                    dve.wait_ge(mix_ld[k], j * 16 + 16)
                    mask = block_mask[:].rearrange("p (a n) -> p a n", a=1).broadcast_to([P, NH, P])
                    for n in range(B):
                        src = mixT[k][:, n, :].rearrange("p (a t h) -> p h a t", a=1, h=NH).broadcast_to([P, NH, 16, B])
                        last = dve.tensor_tensor(diag[k][:, n].rearrange("p h (q t) -> p h q t", t=B), src,
                                                 mask.rearrange("p h (q t) -> p h q t", t=B), ALU.mult)
                    last.then_inc(diag_ready, 1)

                def finish(k, blk):
                    m = 2 * k + blk
                    cols = slice(blk * 512, (blk + 1) * 512)
                    dve.wait_ge(y_full, j * 4 + m + 1)
                    chain(dve.tensor_tensor(yz[:], py[:], zs[k][:, :, cols], ALU.mult))
                    dve.engine_nop().then_inc(yz_ready, 1)
                    dve.wait_ge(o_full, j * 4 + m + 1)
                    dve.wait_ge(rs_ready, j * 4 + m + 1)
                    chain(dve.reciprocal(rs[:], rs[:]))
                    at = (j * 2 + k + NITEM) * IC + blk * 512
                    dve.tensor_tensor(flow[:, ds(at, 512)], po[:, 0, :], rs[:], ALU.mult).then_inc(flow_ready, 1)

                for k in range(2):
                    dve.tensor_copy(cur[k][:], flow[:, ds((j * 2 + k) * IC, IC)]).then_inc(cur_ready, 1)
                mixing(0)
                mixing(1)
                spread(0)
                spread(1)
                for k in range(2):
                    for blk in range(2):
                        finish(k, blk)
                chain.restart()
            dve.wait_ge(flow_ready, 1 + 4 * NITEM)
            chain(dve.tensor_scalar(flow[:, 0:B * T], flow[:, 0:B * T], gate[:, 0:1], None, ALU.mult))
            chain(dve.scalar_tensor_tensor(persist["xm"][:], flow[:, 2 * B * T:3 * B * T], gate[:, 2:3],
                                           flow[:, 0:B * T], ALU.mult, ALU.add))

        @block.tensor
        def _(pe):
            pe.wait_ge(w_ld, 16 * NW)
            pe.wait_ge(w_half, 5)
            pe.wait_ge(flow_ready, 1)
            with pe.Fori(0, NITEM) as j:
                def conv(dst, lhs_cols, src, m):
                    d3 = dst.rearrange("p (q s) -> p q s", s=B)
                    s3 = src.rearrange("p (q s) -> p q s", s=B)
                    for k in range(DCONV):
                        last = pe.matmul(d3[:, :, k:B], conv_w[:, DCONV - 1 - k, lhs_cols], s3[:, :, 0:B - k],
                                         start=k == 0, stop=k == DCONV - 1, skip_group_check=True)
                    return last

                def project(k):
                    pe.wait_ge(cur_ready, j * 2 + k + 1)
                    for blk in range(2):
                        src = cur[k][:, blk * 512:(blk + 1) * 512]
                        n0 = 8 * k + 4 * blk
                        for c in range(4):
                            pe.wait_ge(cv_out, j * 16 + n0 + c + 1)
                            if c < 2:
                                last = pe.matmul(pcv[:, c, :], in_w[:, c * P:(c + 1) * P], src, start=True, stop=True)
                            else:
                                last = conv(pcv[:, c % 2, :], slice((c - 2) * P, (c - 1) * P), src, P)
                            last.then_inc(cv_full, 1)
                        pe.wait_ge(xr_out, j * 8 + 4 * k + 1)
                        conv(pst[0:2 * DST, blk, :], slice(DIN, CONV), src, 2 * DST)
                        pe.matmul(pst[DTB:DTB + 2 * NH, blk, :], dt_w[:], src, start=True, stop=True).then_inc(st_full, 1)
                    for blk in range(2):
                        pe.wait_ge(cv_out, j * 16 + 8 * k + 4 * blk + 6)
                        for c in range(2):
                            last = pe.matmul(pst[BF:NB, blk, :], fcd[:, c, :], xs[k][:, c, blk * 512:(blk + 1) * 512],
                                             start=c == 0, stop=c == 1)
                        last.then_inc(g_full, 1)
                    pe.wait_ge(g_out, j * 4 + 2 * k + 2)
                    pe.wait_ge(st_out, j * 4 + 2 * k + 2)
                    if k:
                        pe.wait_ge(t_out, j * 4 + 2)
                    by_step = stack[k][:].rearrange("n (q s) -> n s q", s=B)
                    for half in range(2):
                        for s in range(4):
                            last = pe.transpose(po[:, half, s * NB:(s + 1) * NB], by_step[:, 4 * half + s, :], ident[0:NB, 0:NB])
                        last.then_inc(t_full, 1)
                    for n in range(4):
                        if n >= 2:
                            pe.wait_ge(xr_out, j * 8 + 4 * k + n)
                        for a in range(2):
                            for c in range(2):
                                t = 2 * n + a
                                last = pe.transpose(pst[:, n % 2, (2 * a + c) * P:(2 * a + c + 1) * P],
                                                    xs[k][:, c, t * P:(t + 1) * P], ident[:])
                        last.then_inc(xr_full, 1)

                def apply(k):
                    pe.wait_ge(diag_ready, j * 2 + k + 1)
                    pe.wait_ge(xr_out, j * 8 + 4 * k + 5)
                    for blk in range(2):
                        m = 2 * k + blk
                        for n in range(4):
                            t = 4 * blk + n
                            for h in range(NH):
                                q = HDIM * (h % 2)
                                last = pe.matmul(py[q:q + HDIM, h // 2, n * P:(n + 1) * P],
                                                 xrow[k][:, t, h * HDIM:(h + 1) * HDIM], diag[k][:, t, h, :],
                                                 start=True, stop=True)
                        last.then_inc(y_full, 1)
                        pe.wait_ge(sq_ready, j * 4 + m + 1)
                        pe.wait_ge(yz_ready, j * 4 + m + 1)
                        for c in range(2):
                            pe.matmul(po[:, 0, :], out_w[:, c, :], yz[:, c, :], start=c == 0, stop=c == 1)
                        for c in range(2):
                            last = pe.matmul(po[:, 1, :], ones[:], sq[:, c, :], start=c == 0, stop=c == 1)
                        last.then_inc(o_full, 1)
                        pe.wait_ge(flow_ready, j * 4 + m + 2)

                project(0)
                project(1)
                apply(0)
                apply(1)


class Tile:

    def __init__(self, i, k):
        self.i, self.k = (i + k // TT, k % TT) if k // TT else (i, k)
        self.n = self.i * TT + self.k
        self.exists = not isinstance(self.n, int) or 0 <= self.n < B * TT

    def after(self, d):
        return Tile(self.i, self.k + d)


def awaited(eng, sem, value):
    if not isinstance(value, int) or value > 0:
        eng.wait_ge(sem, value)


def experts(nc, I, persist, scratch, out):
    ident, neg_half, xm = persist["ident"], persist["neg_half"], persist["xm"]
    KR = KE * RANK
    with ExitStack() as ctx:
        sb = lambda n, s, d=F32: ctx.enter_context(nc.sbuf_tensor(n, s, d))
        sem = lambda n: ctx.enter_context(nc.semaphore(n))
        norm = Norm(nc, ctx, "e_")
        aH, aL = sb("aH", [P, DC, KR], F32R), sb("aL", [P, DC, KR], F32R)
        bH, bL = sb("bH", [P, DC, D], F32R), sb("bL", [P, DC, D], F32R)
        wr, up, b_up = sb("wr", [P, DC, KE]), sb("up", [P, D]), sb("b_up", [P, D])
        h = sb("h", [P, TT, D])
        x5, hg = sb("x5", [P, D]), sb("hg", [P, KR])
        xF, xH, xL = sb("xF", [P, DC, P]), sb("xH", [P, DC, P], F32R), sb("xL", [P, DC, P], F32R)
        gH, gL = sb("gH", [P, DC, P], F32R), sb("gL", [P, DC, P], F32R)
        mid = sb("mid", [P, 2, P])
        sc = sb("sc5", [P, KE])
        top, rep, rep2, ex, gt = sb("top5", [P, 16]), sb("rep5", [P, KE]), sb("rep6", [P, KE]), sb("ex5", [P, KE]), sb("gt", [P, KE])
        nmax, gsum, ginv = sb("nmax5", [P, 1]), sb("gsum", [P, 1]), sb("ginv", [P, 1])
        ps = lambda n, s: ctx.enter_context(nc.psum_tensor(n, s, F32))
        ptr, pup, psc, pa, po = ps("ptr5", [P, 2, 512]), ps("pup", [P, 512]), ps("psc5", [P, 512]), ps("pa", [P, 2, 512]), ps("po5", [P, 2, 512])
        w_ld, stage_ld, stage_used, stage_high = sem("ew_ld"), [sem(f"estage{k}") for k in range(4)], sem("estage_used"), sem("estage_high")
        res_ld, out_st = [sem(f"res_ld{k}") for k in range(TT)], [sem(f"out_st{k}") for k in range(TT)]
        bias_ready, mid_ready, up_full, up_added = sem("bias_ready"), sem("mid_ready"), sem("up_full"), sem("up_added")
        x5_ready, t5_full, t5_out, xL_ready = sem("x5_ready"), sem("t5_full"), sem("t5_out"), sem("xL_ready")
        sc_full, sc_used, nmax_ready, ex_ready = sem("sc_full5"), sem("sc_used"), sem("nmax5_ready"), sem("ex5_ready")
        a_full, hg_ready, t6_full, t6_high, t6_low = (sem(n) for n in ("a_full", "hg_ready", "t6_full", "t6_high", "t6_low"))
        store_go = sem("store_go")
        b_full, out_ready, vchain = sem("b_full"), sem("out_ready"), sem("vchain4")
        block = ctx.enter_context(nc.Block())
        GROUPS = B

        def run(eng, step, restart=lambda: None):
            step(Tile(0, -1))
            for k in range(TT):
                step(Tile(0, k))
            restart()
            with eng.Fori(1, GROUPS - 1) as i:
                for k in range(TT):
                    step(Tile(i, k))
                restart()
            for k in range(TT + 1):
                step(Tile(GROUPS - 1, k))
            restart()

        chunks = [(I["ea_w"], aH, aL, c) for c in range(DC)] + [(I["eb_w"], bH, bL, c) for c in range(DC)]

        @block.sync
        def _(sp):
            for n, (src, _, _, c) in enumerate(chunks):
                if n >= TT:
                    sp.wait_ge(stage_used, n - TT + 1)
                sp.dma_start(h[:, n % TT, :], src[c * P:(c + 1) * P, :]).then_inc(stage_ld[n % TT], 16)

            def load(t):
                if t.exists:
                    awaited(sp, out_st[t.k], 16 * t.i)
                    sp.dma_start(h[:, t.k, :], scratch["res"][at(t.i), t.k, :, :].rearrange("a p d -> (a p) d")).then_inc(res_ld[t.k], 16)

            def step(t):
                if t.after(-1).exists:
                    last = t.after(-1)
                    sp.wait_ge(out_ready, last.n + 1)
                    sp.sem_inc(store_go, 1)
                    sp.dma_start(out[at(last.i), last.k * P:(last.k + 1) * P, :].rearrange("a p d -> (a p) d"),
                                 h[:, last.k, :]).then_inc(out_st[last.k], 16)
                load(t.after(3))

            for n in range(2):
                sp.wait_ge(stage_used, len(chunks))
                load(Tile(0, n))
            run(sp, step)
            for k in range(TT):
                sp.wait_ge(out_st[k], 16 * B)

        @block.gpsimd
        def _(pool):
            def bias(t):
                if t.exists:
                    pool.wait_ge(res_ld[t.k], 16 * t.i + 16)
                    pool.tensor_tensor(h[:, t.k, :], h[:, t.k, :], b_up[:], ALU.add).then_inc(bias_ready, 1)

            def step(t):
                if t.after(1).exists:
                    norm.serve(pool, neg_half, t.after(1).n)
                bias(t.after(2))

            pool.wait_ge(w_ld, 48)
            bias(Tile(0, 0))
            run(pool, step)

        @block.scalar
        def _(act):
            act.dma_start(wr[:], I["wr"].rearrange("(c p) n -> p c n", p=P)).then_inc(w_ld, 16)
            act.dma_start(up[:], I["w_up"]).then_inc(w_ld, 16)
            act.dma_start(b_up[:], I["b_up"].to_broadcast([P, D])).then_inc(w_ld, 16)
            for n, (_, high, _, c) in enumerate(chunks):
                act.wait_ge(stage_ld[n % TT], 16 * (n // TT + 1))
                act.activation(high[:, c, :], h[:, n % TT, :], ACT.Copy).then_inc(stage_high, 1)

            def take_mid(t):
                if t.exists:
                    awaited(act, up_full, 2 * t.n - 2)
                    act.activation(mid[:, t.k % 2, :], xm[:, ds(t.i + t.k * P * B, P, B)], ACT.Copy).then_inc(mid_ready, 1)

            def step(t):
                if t.after(-1).exists:
                    last = t.after(-1)
                    for g in range(2):
                        act.wait_ge(t6_full, 2 * last.n + g + 1)
                        act.activation(gH[:, 4 * g:4 * g + 4, :], ptr[:, g, :].rearrange("p (c t) -> p c t", c=4), ACT.Copy).then_inc(t6_high, 1)
                if t.exists:
                    act.wait_ge(nmax_ready, t.n + 1)
                    act.activation(ex[:], sc[:], ACT.Exp, bias=nmax[:, 0:1]).then_inc(ex_ready, 1)
                take_mid(t.after(2))
                if t.after(1).exists:
                    nxt = t.after(1)
                    for g in range(2):
                        act.wait_ge(t5_full, 2 * nxt.n + g + 1)
                        src = ptr[:, g, :].rearrange("p (c t) -> p c t", c=4)
                        act.activation(xF[:, 4 * g:4 * g + 4, :], src, ACT.Copy)
                        act.activation(xH[:, 4 * g:4 * g + 4, :], src, ACT.Copy).then_inc(t5_out, 1)

            take_mid(Tile(0, 0))
            run(act, step)

        @block.vector
        def _(dve):
            chain = Chain(dve, vchain)
            for n, (_, high, low, c) in enumerate(chunks):
                dve.wait_ge(stage_high, n + 1)
                dve.tensor_tensor(low[:, c, :], h[:, n % TT, :], high[:, c, :].bitcast(F32), ALU.subtract).then_inc(stage_used, 1)

            def add_up(t, n):
                if t.exists:
                    if n == 0:
                        dve.wait_ge(bias_ready, t.n + 1)
                    dve.wait_ge(up_full, 2 * t.n + n + 1)
                    half = h[:, t.k, n * 512:(n + 1) * 512]
                    dve.tensor_tensor(half, half, pup[:], ALU.add).then_inc(up_added, 1)

            def gates(t):
                dve.wait_ge(sc_full, t.n + 1)
                chain(dve.tensor_copy(sc[:], psc[:, 0:KE]))
                dve.engine_nop().then_inc(sc_used, 1)
                chain(dve.max(top[:, 0:8], sc[:]))
                dve.tensor_scalar(nmax[:], top[:, 0:1], -1.0, None, ALU.mult).then_inc(nmax_ready, 1)
                chain(dve.match_replace(rep[:], top[:, 0:8], sc[:], NEG))
                chain(dve.max(top[:, 8:16], rep[:]))
                chain(dve.match_replace(rep2[:], top[:, 8:16], rep[:], NEG))
                dve.wait_ge(ex_ready, t.n + 1)
                chain(dve.scalar_tensor_tensor(gt[:], rep2[:], -1e38, ex[:], ALU.is_lt, ALU.mult))
                chain(dve.tensor_reduce(gsum[:], gt[:], AX, ALU.add))
                chain(dve.reciprocal(ginv[:], gsum[:]))
                chain(dve.tensor_scalar(gt[:], gt[:], ginv[:, 0:1], 2.0, ALU.mult, ALU.mult))

            def weigh(t):
                dve.wait_ge(a_full, t.n + 1)
                awaited(dve, t6_full, 2 * t.n)
                g4 = gt[:].rearrange("p (a k) -> p a k", a=1).broadcast_to([P, RANK // 2, KE])
                for n in range(2):
                    last = dve.tensor_tensor(hg[:, n * 512:(n + 1) * 512].rearrange("p (r k) -> p r k", k=KE),
                                             pa[:, n, :].rearrange("p (r k) -> p r k", k=KE), g4, ALU.mult)
                last.then_inc(hg_ready, 1)

            def step(t):
                nxt, last = t.after(1), t.after(-1)
                if nxt.exists:
                    dve.wait_ge(up_added, 2 * nxt.n + 2)
                    awaited(dve, t5_full, 2 * nxt.n)
                    norm.rows(dve, chain, x5[:], h[:, nxt.k, :], nxt.n).then_inc(x5_ready, 1)
                if last.exists:
                    for g in range(2):
                        dve.wait_ge(t6_high, 2 * last.n + g + 1)
                        dve.tensor_tensor(gL[:, 4 * g:4 * g + 4, :], ptr[:, g, :].rearrange("p (c t) -> p c t", c=4),
                                          gH[:, 4 * g:4 * g + 4, :].bitcast(F32), ALU.subtract).then_inc(t6_low, 1)
                if t.exists:
                    gates(t)
                    weigh(t)
                add_up(t.after(2), 0)
                if nxt.exists:
                    dve.wait_ge(t5_out, 2 * nxt.n + 2)
                    dve.tensor_tensor(xL[:], xF[:], xH[:].bitcast(F32), ALU.subtract).then_inc(xL_ready, 1)
                add_up(t.after(2), 1)
                if last.exists:
                    dve.wait_ge(b_full, last.n + 1)
                    dve.tensor_tensor(h[:, last.k, :], h[:, last.k, :], po[:].rearrange("p a n -> p (a n)"), ALU.add).then_inc(out_ready, 1)

            for n in range(2):
                add_up(Tile(0, 0), n)
            run(dve, step, chain.restart)

        @block.tensor
        def _(pe):
            pe.wait_ge(w_ld, 48)
            pe.wait_ge(stage_used, len(chunks))

            def project_up(t, n):
                if t.exists:
                    pe.wait_ge(mid_ready, t.n + 1)
                    awaited(pe, up_added, 2 * t.n + n)
                    pe.matmul(pup[:], mid[:, t.k % 2, :], up[:, n * 512:(n + 1) * 512], start=True, stop=True).then_inc(up_full, 1)

            def products(dst, high, low, wH, wL, low_ready):
                for k, (lhs, rhs) in enumerate(((high, wH), (high, wL), (low, wH))):
                    if k == 2:
                        low_ready()
                    for c in range(DC):
                        for n in range(2):
                            last = pe.matmul(dst[:, n, :], lhs[:, c, :], rhs[:, c, n * 512:(n + 1) * 512],
                                             start=k == 0 and c == 0, stop=k == 2 and c == DC - 1)
                return last

            def turn(src, g):
                for c in range(4):
                    k = 4 * g + c
                    last = pe.transpose(ptr[:, g, c * P:(c + 1) * P], src[:, k * P:(k + 1) * P], ident[:])
                return last

            def step(t):
                nxt, last = t.after(1), t.after(-1)
                if t.exists:
                    pe.wait_ge(t5_out, 2 * t.n + 2)
                    awaited(pe, hg_ready, t.n)
                    products(pa, xH, xL, aH, aL, lambda: pe.wait_ge(xL_ready, t.n + 1)).then_inc(a_full, 1)
                project_up(t.after(2), 0)
                if nxt.exists:
                    pe.wait_ge(x5_ready, nxt.n + 1)
                    for g in range(2):
                        awaited(pe, t6_low, 2 * nxt.n - 3 + g)
                        turn(x5, g).then_inc(t5_full, 1)
                    pe.wait_ge(t5_out, 2 * nxt.n + 2)
                    awaited(pe, sc_used, nxt.n)
                    for c in range(DC):
                        s = pe.matmul(psc[:, 0:KE], xF[:, c, :], wr[:, c, :], start=c == 0, stop=c == DC - 1)
                    s.then_inc(sc_full, 1)
                project_up(t.after(2), 1)
                if last.exists:
                    pe.wait_ge(t6_high, 2 * last.n + 2)
                    awaited(pe, out_ready, last.n)
                    products(po, gH, gL, bH, bL, lambda: pe.wait_ge(t6_low, 2 * last.n + 2)).then_inc(b_full, 1)
                if t.exists:
                    pe.wait_ge(hg_ready, t.n + 1)
                    for g in range(2):
                        pe.wait_ge(t5_out, 2 * nxt.n + g + 1) if nxt.exists else None
                        turn(hg, g).then_inc(t6_full, 1)

            for n in range(2):
                project_up(Tile(0, 0), n)
            run(pe, step)


def at(i):
    return slice(i, i + 1) if isinstance(i, int) else ds(i, 1)


def program(nc, I, out, stages=4, dbg=None):
    with ExitStack() as ctx:
        sb = lambda n, s, d=F32: ctx.enter_context(nc.sbuf_tensor(n, s, d))
        persist = {"ident": sb("ident", [P, P]), "causal": sb("causal", [P, P]), "xm": sb("xm", [P, T * B]), "neg_half": sb("neg_half", [P, 1]),
                   "ids_emb": sb("ids_emb", [P, (B + 1) * TT], I32), "ids_pos": sb("ids_pos", [P, (B + 1) * TT], I32)}
        scratch = {"pos": nc.dram_tensor("pos_rows", [N_POS, D], F32).ap(),
                   "res": nc.dram_tensor("residual", [B, TT, P, D], F32).ap(),
                   "mix": nc.dram_tensor("mixing", [2 * T, B * B * NH], F32).ap()}
        with ExitStack() as wctx:
            wb = lambda n, s, d=F32: wctx.enter_context(nc.sbuf_tensor(n, s, d))
            W = {"baseH": wb("baseH", [P, DC, D], F32R), "baseL": wb("baseL", [P, DC, D], F32R),
                 "raw_ra": wb("raw_ra", [P, DC, RA]), "lora_b": wb("lora_b", [P, D]), "down": wb("down", [P, DC, DM]),
                 "b_down": wb("b_down", [P, 1]), "base_b": wb("base_b", [P, D]), "router_b": wb("router_b", [P, NR]),
                 "emap_i": wb("emap_i", [P, NR], I32), "emap": wb("emap", [P, NR]), "onehot": wb("onehot", [P, E0, NR]),
                 "qk": wb("qk", [P, DC]), "vb": wb("vb", [P, H, HD])}
            tables(nc, I, persist, W, scratch)
            attend(nc, I, persist, W, scratch)
        if stages >= 3:
            hydra(nc, I, persist, scratch)
        if dbg:
            dbg(nc, persist, scratch)
        if stages >= 4:
            experts(nc, I, persist, scratch, out)


def layout(inputs):
    a = {k: np.asarray(v) for k, v in inputs.items()}
    f = np.float32
    half = P // 2
    freq = np.exp(np.arange(half, dtype=f) * f(-np.log(100.0) / (half - 1))).astype(f)
    pos_const = np.zeros((P, 2 + N_POS), f)
    pos_const[:, 0] = np.concatenate([freq, freq])
    pos_const[half:, 1] = 0.25
    pos_const[:, 2:] = np.arange(N_POS, dtype=f)
    ids = np.zeros((P, (B + 1) * TT), np.int32)
    ids[:, :B * TT] = a["x"].reshape(B * TT, P).T
    row = lambda v: np.ascontiguousarray(v.reshape(1, -1))
    con = np.ascontiguousarray
    ra_w = np.zeros((D, RA), f)
    ra_w[:, :NR] = a["L0_ffn_router_W"].T
    ra_w[:, NR + 1:] = a["L0_ffn_A"].reshape(E0 * R0, D).T
    b12 = np.stack([a["L0_tok_b1"], a["L0_tok_b2"]], 1).reshape(E_POS * 2, 2, P)
    return {
        "pos_const": pos_const, "ids": ids, "embed": a["L0_tok_embed_table"],
        "W1": a["L0_tok_W1"], "W2": a["L0_tok_W2"], "W3": a["L0_tok_W3"], "b3": a["L0_tok_b3"],
        "b12": con(b12.transpose(2, 0, 1)),
        "bv_q": row(a["L0_attn_bv_q"]), "bv_k": row(a["L0_attn_bv_k"]), "bv_v": row(a["L0_attn_bv_v"]),
        "base_w": con(a["L0_ffn_base_W"].T), "base_b": row(a["L0_ffn_base_b"]), "ra_w": ra_w,
        "router_b": row(a["L0_ffn_router_b"]), "expert_map": row(a["L0_ffn_expert_map"]),
        "lora_b": con(a["L0_ffn_B"].transpose(0, 2, 1).reshape(E0 * R0, D)),
        "in_z": con(a["L1_attn_hy_in_w"][:DIN].T), "in_xbc": con(a["L1_attn_hy_in_w"][DIN:DIN + CONV].T),
        "in_dt": con(a["L1_attn_hy_in_w"][DIN + CONV:].T),
        "conv_bx": con(a["L1_attn_hy_conv_b"][:DIN].reshape(2, P).T), "conv_bbc": con(a["L1_attn_hy_conv_b"][DIN:].reshape(-1, 1)),
        "hy_d": con(a["L1_attn_hy_D"].reshape(NH, 1)), "hy_norm": con(a["L1_attn_hy_norm_w"].reshape(2, P).T),
        "dt_bias": con(np.concatenate([a["L1_attn_hy_dt_bias"]] * 2).reshape(-1, 1)),
        "conv_w": con(a["L1_attn_hy_conv_w"][:, 0, :].T.reshape(1, -1)), "fcd": con(a["L1_attn_hy_fcD_w"].T),
        "hy_out": con(a["L1_attn_hy_out_w"].T), "a_log": con(np.concatenate([a["L1_attn_hy_A_log"]] * 2).reshape(1, -1)),
        "gate1": con(a["L1_attn_gate1"].reshape(1, 1)),
        "ea_w": con(a["L1_ffn_A"].transpose(2, 1, 0).reshape(D, RANK * KE)),
        "eb_w": con(a["L1_ffn_B"].transpose(2, 0, 1).reshape(RANK * KE, D)),
        "wr": con(a["L1_ffn_Wr"].T), "w_up": con(a["L1_attn_w_up"].T), "b_up": row(a["L1_attn_b_up"]),
        "w_down": con(a["L1_attn_w_down"].T), "b_down": a["L1_attn_b_down"].reshape(P, 1),
    }


def kernel(**inputs):
    from concourse import bacc
    from concourse.bass_utils import run_bass_kernel_spmd

    nc = bacc.Bacc("TRN2", target_bir_lowering=False, num_devices=1)
    arrays = {"in_" + k: v for k, v in layout(inputs).items()}
    I = {k[3:]: nc.dram_tensor(k, v.shape, mybir.dt.from_np(v.dtype), kind="ExternalInput").ap() for k, v in arrays.items()}
    out = nc.dram_tensor("out", (B, T, D), F32, kind="ExternalOutput").ap()
    program(nc, I, out)
    return run_bass_kernel_spmd(nc, [arrays], core_ids=[0]).results[0]["out"]
```

```python
from contextlib import ExitStack

import numpy as np
import concourse.bass as bass
from concourse import mybir

F32 = mybir.dt.float32
F32R = mybir.dt.float32r
I32 = mybir.dt.int32
ACT = mybir.ActivationFunctionType
ALU = mybir.AluOpType
AX = mybir.AxisListType.X
ds = bass.ds

P = 128
B, T, D = 8, 512, 1024
TT = T // P
DC = D // P
N_TOK, CANVAS, E_POS, HID = 8000, 125, 4, 256
N_POS = CANVAS * E_POS
H, HD = 4, 256
HC = HD // P
NR, E0, R0 = 15, 8, 16
RA = NR + 1 + E0 * R0
DM, DIN, DST, NH, HDIM, DCONV = 128, 256, 16, 4, 64, 7
KE, TOPK, RANK = 64, 16, 16
EPS = 1e-5
SKIP = 1 << 20
NEG = -3.0e38
DTB = 2 * DST
BF = DTB + 2 * NH
NB = BF + NH
IC = 1024
NITEM = T // P
INV2PI = float(np.float32(1 / (2 * np.pi)))
PI_A, PI_B = 6.28125, float(np.float32(2 * np.pi - 6.28125))
ROUND = 12582912.0


TR2, TRW, TR3 = {0: 0}, {}, {}
_n = 2
for _t in range(TT):
    if _t < TT - 1:
        TR2[_t + 1] = _n
        _n += 2
    TRW[_t] = _n
    _n += 1
    if _t > 0:
        TR3[_t - 1] = _n
        _n += 2
TR3[TT - 1] = _n


class Chain:

    def __init__(self, eng, sem):
        self.eng, self.sem, self.n = eng, sem, 0

    def __call__(self, ins):
        self.n += 1
        ins.then_inc(self.sem, 1)
        self.eng.wait_ge(self.sem, self.n)

    def restart(self):
        self.eng.sem_clear(self.sem)
        self.n = 0


class Norm:

    def __init__(self, nc, ctx, name):
        sb = lambda n, s: ctx.enter_context(nc.sbuf_tensor(name + n, s, F32))
        self.stats, self.mean_var, self.var, self.rstd = sb("stats", [P, 2, 6]), sb("mv", [P, 2]), sb("var", [P, 1]), sb("rstd", [P, 1])
        self.scale, self.shift = sb("scale", [P, 1]), sb("shift", [P, 1])
        self.var_ready = ctx.enter_context(nc.semaphore(name + "var_ready"))
        self.rstd_ready = ctx.enter_context(nc.semaphore(name + "rstd_ready"))

    def rows(self, dve, chain, dst, src, n):
        dve.bn_stats(self.stats[:, 0, :], src[:, 0:D // 2])
        chain(dve.bn_stats(self.stats[:, 1, :], src[:, D // 2:D]))
        chain(dve.bn_aggr(self.mean_var[:], self.stats[:]))
        dve.tensor_scalar(self.var[:], self.mean_var[:, 1:2], EPS, None, ALU.add).then_inc(self.var_ready, 1)
        dve.wait_ge(self.rstd_ready, n + 1)
        return dve.tensor_scalar(dst, src, self.mean_var[:, 0:1], self.rstd[:, 0:1], ALU.subtract, ALU.mult)

    def with_residual(self, dve, chain, rows):
        dve.tensor_scalar(self.scale[:], self.rstd[:], 1.0, None, ALU.add)
        chain(dve.scalar_tensor_tensor(self.shift[:], self.mean_var[:, 0:1], -1.0, self.rstd[:], ALU.mult, ALU.mult))
        return dve.tensor_scalar(rows, rows, self.scale[:, 0:1], self.shift[:, 0:1], ALU.mult, ALU.add)

    def serve(self, pool, neg_half, n):
        pool.wait_ge(self.var_ready, n + 1)
        pool.tensor_tensor(self.rstd[:], self.var[:], neg_half[:], ALU.pow).then_inc(self.rstd_ready, 1)


def tables(nc, I, persist, W, scratch):
    ident, ids_emb, ids_pos = persist["ident"], persist["ids_emb"], persist["ids_pos"]
    baseH, baseL, qk, vb = W["baseH"], W["baseL"], W["qk"], W["vb"]
    with ExitStack() as ctx:
        sb = lambda n, s, d=F32: ctx.enter_context(nc.sbuf_tensor(n, s, d))
        sem = lambda n: ctx.enter_context(nc.semaphore(n))
        pos_in = sb("pos_in", [P, 2 + N_POS])
        ang = sb("ang", [P, N_POS])
        turns = sb("turns", [P, N_POS])
        w1, w2, w3 = sb("w1", [P, HID]), sb("w2", [P, 2, HID]), sb("w3", [P, 2, D])
        b12, b3 = sb("b12", [P, 2 * E_POS, 2]), sb("b3", [CANVAS, D])
        h1, h2 = sb("h1", [P, 2, CANVAS]), sb("h2", [P, 2, CANVAS])
        absx, lnx = sb("absx", [P, 2, CANVAS]), sb("lnx", [P, 2, CANVAS])
        posrow = sb("posrow", [CANVAS, D])
        stage = sb("stage", [P, 2, D])
        bq, bk, bv = sb("bq", [P, H, HD]), sb("bk", [P, H, HD]), sb("bv", [P, H, HD])
        sgn, alpha = sb("sgn", [P, H, HD]), sb("alpha", [P, H])
        idf, t0, t1, t2 = (sb(n, [P, (B + 1) * TT]) for n in ("idf", "t0", "t1", "t2"))
        ids = sb("ids", [P, (B + 1) * TT], I32)
        ph = ctx.enter_context(nc.psum_tensor("ph", [P, 2, 512], F32))
        pp = ctx.enter_context(nc.psum_tensor("pp", [P, 2, 512], F32))
        pq = ctx.enter_context(nc.psum_tensor("pq", [P, 2, 512], F32))
        in_ld, const_ld, stage_ld = sem("in_ld"), sem("const_ld"), [sem("stage_ld0"), sem("stage_ld1")]
        w_ld, pos_st = sem("w_ld"), sem("pos_st")
        stage_used, ident_done = sem("stage_used"), sem("ident_done")
        ang_ready, sin_ready = sem("ang_ready"), sem("sin_ready")
        h_full, h_pre, h_exp, h_ready = sem("h_full"), sem("h_pre"), sem("h_exp"), sem("h_ready")
        pos_full, pos_ready = sem("pos_full"), sem("pos_ready")
        qk_row, qk_full = sem("qk_row"), sem("qk_full")
        vchain = sem("vchain")
        block = ctx.enter_context(nc.Block())

        @block.sync
        def _(sp):
            sp.dma_start(pos_in[:], I["pos_const"]).then_inc(in_ld, 16)
            sp.dma_start(ids[:], I["ids"]).then_inc(in_ld, 16)
            sp.dma_start(b12[:], I["b12"]).then_inc(in_ld, 16)
            for t, name in ((bq, "bv_q"), (bk, "bv_k"), (bv, "bv_v")):
                sp.dma_start(t[:].rearrange("p h d -> p (h d)"), I[name].to_broadcast([P, D])).then_inc(in_ld, 16)
            for e in range(E_POS):
                if e:
                    sp.wait_ge(pos_full, 2 * e)
                    sp.wait_ge(pos_ready, e)
                sp.dma_start(w1[:], I["W1"][e]).then_inc(w_ld, 16)
                sp.dma_start(w2[:], I["W2"][e].rearrange("(c p) n -> p c n", p=P)).then_inc(w_ld, 16)
                sp.dma_start(w3[:], I["W3"][e].rearrange("(c p) n -> p c n", p=P)).then_inc(w_ld, 16)
                sp.dma_start(b3[:], I["b3"][e:e + 1, :].to_broadcast([CANVAS, D])).then_inc(w_ld, 16)
                sp.wait_ge(pos_ready, e + 1)
                sp.dma_start(scratch["pos"][e * CANVAS:(e + 1) * CANVAS, :], posrow[:]).then_inc(pos_st, 16)
            sp.wait_ge(pos_st, 16 * E_POS)

        @block.scalar
        def _(act):
            act.dma_start(W["raw_ra"][:], I["ra_w"].rearrange("(c p) n -> p c n", p=P)).then_inc(const_ld, 16)
            act.dma_start(W["lora_b"][:], I["lora_b"]).then_inc(const_ld, 16)
            act.dma_start(W["down"][:], I["w_down"].rearrange("(c p) n -> p c n", p=P)).then_inc(const_ld, 16)
            act.dma_start(W["b_down"][:], I["b_down"]).then_inc(const_ld, 16)
            act.dma_start(W["base_b"][:], I["base_b"].to_broadcast([P, D])).then_inc(const_ld, 16)
            act.dma_start(W["router_b"][:], I["router_b"].to_broadcast([P, NR])).then_inc(const_ld, 16)
            act.dma_start(W["emap_i"][:], I["expert_map"].to_broadcast([P, NR])).then_inc(const_ld, 16)
            for c in range(2):
                act.dma_start(stage[:, c, :], I["base_w"][c * P:(c + 1) * P, :]).then_inc(stage_ld[c % 2], 16)
            act.wait_ge(ang_ready, 1)
            act.activation(ang[:], ang[:], ACT.Sin).then_inc(sin_ready, 1)
            for s in range(2 * E_POS):
                act.wait_ge(h_pre, s + 1)
                act.activation(lnx[:], absx[:], ACT.Exp).then_inc(h_exp, 1)
                act.wait_ge(h_exp, 2 * s + 1)
                act.activation(lnx[:], lnx[:], ACT.Ln, bias=1.0).then_inc(h_exp, 1)
            for c in range(2, DC):
                act.wait_ge(stage_used, c - 1)
                act.dma_start(stage[:, c % 2, :], I["base_w"][c * P:(c + 1) * P, :]).then_inc(stage_ld[c % 2], 16)
            act.wait_ge(const_ld, 16 * 7)

        @block.gpsimd
        def _(pool):
            pool.memset(persist["neg_half"][:], -0.5)
            pool.memset(ident[:], 0.0).then_inc(ident_done, 1)
            pool.memset(persist["causal"][:], 1.0).then_inc(ident_done, 1)
            pool.wait_ge(ident_done, 2)
            pool.affine_select(out=ident[:], in_=ident[:], compare_op=ALU.not_equal, fill=1.0, base=0,
                               pattern=[[-1, P]], channel_multiplier=1).then_inc(ident_done, 1)
            pool.affine_select(out=persist["causal"][:], in_=persist["causal"][:], compare_op=ALU.is_ge, fill=0.0,
                               base=0, pattern=[[1, P]], channel_multiplier=-1).then_inc(ident_done, 1)

        @block.vector
        def _(dve):
            chain = Chain(dve, vchain)
            dve.wait_ge(in_ld, 16 * 6)
            chain(dve.tensor_scalar(turns[:], pos_in[:, 2:], 1.0 / CANVAS, float(CANVAS), ALU.mult, ALU.mult))
            chain(dve.tensor_scalar(ang[:], turns[:], pos_in[:, 0:1], None, ALU.mult))
            chain(dve.tensor_scalar(turns[:], ang[:], INV2PI, None, ALU.mult))
            chain(dve.tensor_scalar(turns[:], turns[:], pos_in[:, 1:2], ROUND, ALU.add, ALU.add))
            chain(dve.tensor_scalar(turns[:], turns[:], -ROUND, None, ALU.add))
            chain(dve.scalar_tensor_tensor(ang[:], turns[:], -PI_A, ang[:], ALU.mult, ALU.add))
            chain(dve.scalar_tensor_tensor(ang[:], turns[:], -PI_B, ang[:], ALU.mult, ALU.add))
            chain(dve.tensor_scalar(turns[:, 0:1], pos_in[:, 1:2], float(2 * np.pi), None, ALU.mult))
            chain(dve.tensor_scalar(ang[:], ang[:], turns[:, 0:1], None, ALU.add))
            dve.tensor_scalar(ang[:], ang[:], 3.1415925, -3.1415925, ALU.min, ALU.max).then_inc(ang_ready, 1)

            chain(dve.tensor_copy(idf[:], ids[:]))
            chain(dve.tensor_scalar(t0[:], idf[:], 0.0, float(N_TOK), ALU.is_lt, ALU.mult))
            chain(dve.tensor_scalar(t1[:], idf[:], float(N_TOK), None, ALU.is_ge))
            chain(dve.tensor_scalar(t2[:], idf[:], float(N_TOK + N_POS), None, ALU.is_ge))
            chain(dve.tensor_tensor(idf[:], idf[:], t0[:], ALU.add))
            chain(dve.tensor_scalar(t0[:], t1[:], -1.0, 1.0, ALU.mult, ALU.add))
            chain(dve.tensor_tensor(t0[:], t0[:], idf[:], ALU.mult))
            chain(dve.tensor_tensor(t1[:], t1[:], t2[:], ALU.subtract))
            chain(dve.scalar_tensor_tensor(t0[:], t1[:], float(SKIP), t0[:], ALU.mult, ALU.add))
            chain(dve.tensor_copy(ids_emb[:], t0[:]))
            chain(dve.tensor_scalar(t0[:], idf[:], -float(N_TOK), None, ALU.add))
            chain(dve.tensor_tensor(t0[:], t0[:], t1[:], ALU.mult))
            chain(dve.tensor_scalar(t1[:], t1[:], -float(SKIP), float(SKIP), ALU.mult, ALU.add))
            chain(dve.tensor_tensor(t0[:], t0[:], t1[:], ALU.add))
            chain(dve.tensor_copy(ids_pos[:], t0[:]))

            for src, dst in ((bq, bq), (bk, bk), (bv, vb)):
                chain(dve.tensor_reduce(alpha[:], src[:], AX, ALU.add, apply_absolute_value=True))
                chain(dve.tensor_scalar(alpha[:], alpha[:], 1.0 / HD, None, ALU.mult))
                chain(dve.tensor_scalar(sgn[:], src[:], 0.0, 2.0, ALU.is_ge, ALU.mult))
                for h in range(H):
                    last = dve.tensor_scalar(sgn[:, h, :], sgn[:, h, :], -1.0, alpha[:, h:h + 1], ALU.add, ALU.mult)
                    chain(last)
                chain(dve.tensor_tensor(sgn[:], sgn[:], src[:], ALU.subtract))
                chain(dve.tensor_tensor(dst[:], sgn[:], src[:], ALU.add))
            dve.tensor_tensor(bq[:], bq[:], bk[:], ALU.mult).then_inc(qk_row, 1)

            dve.wait_ge(ident_done, 4)
            for n in range(2):
                dve.wait_ge(qk_full, n + 1)
                chain(dve.tensor_copy(qk[:, 4 * n:4 * n + 4], pq[:, n, 0:512:P]))

            def split_base(c):
                dve.wait_ge(stage_ld[c % 2], 16 * (c // 2 + 1))
                chain(dve.tensor_copy(baseH[:, c, :], stage[:, c % 2, :]))
                dve.tensor_tensor(baseL[:, c, :], stage[:, c % 2, :], baseH[:, c, :].bitcast(F32),
                                  ALU.subtract).then_inc(stage_used, 1)

            split_base(0)
            split_base(1)
            for e in range(E_POS):
                for layer, h in ((0, h1), (1, h2)):
                    s = 2 * e + layer
                    dve.wait_ge(h_full, s + 1)
                    for c in range(2):
                        chain(dve.tensor_scalar(h[:, c, :], ph[:, c, 0:CANVAS], b12[:, 2 * e + layer, c:c + 1], None, ALU.add))
                    dve.scalar_tensor_tensor(absx[:], h[:], -1.0, h[:], ALU.mult, ALU.min).then_inc(h_pre, 1)
                    chain(dve.tensor_scalar(h[:], h[:], 0.0, None, ALU.max))
                    dve.wait_ge(h_exp, 2 * s + 2)
                    dve.tensor_tensor(h[:], h[:], lnx[:], ALU.add).then_inc(h_ready, 1)
                dve.wait_ge(w_ld, 64 * (e + 1))
                dve.wait_ge(pos_full, 2 * e + 2)
                if e:
                    dve.wait_ge(pos_st, 16 * e)
                chain(dve.tensor_tensor(posrow[:, 0:512], pp[0:CANVAS, 0, :], b3[:, 0:512], ALU.add))
                dve.tensor_tensor(posrow[:, 512:D], pp[0:CANVAS, 1, :], b3[:, 512:D], ALU.add).then_inc(pos_ready, 1)
            for c in range(2, DC):
                split_base(c)
            dve.wait_ge(const_ld, 16 * 7)
            chain(dve.tensor_copy(W["emap"][:], W["emap_i"][:]))
            for e in range(E0):
                last = dve.tensor_scalar(W["onehot"][:, e, :], W["emap"][:], float(e), None, ALU.is_equal)
            chain(last)
            dve.wait_ge(stage_used, DC)

        @block.tensor
        def _(pe):
            pe.wait_ge(ident_done, 4)
            pe.wait_ge(qk_row, 1)
            row = bq[:].rearrange("p h d -> p (h d)")
            for c in range(DC):
                last = pe.transpose(pq[:, c // 4, (c % 4) * P:(c % 4 + 1) * P], row[:, c * P:(c + 1) * P], ident[:])
                if c % 4 == 3:
                    last.then_inc(qk_full, 1)
            pe.wait_ge(sin_ready, 1)
            for e in range(E_POS):
                pe.wait_ge(w_ld, 64 * (e + 1))
                if e:
                    pe.wait_ge(h_ready, 2 * e)
                for c in range(2):
                    last = pe.matmul(ph[:, c, 0:CANVAS], w1[:, c * P:(c + 1) * P], ang[:, e * CANVAS:(e + 1) * CANVAS],
                                     start=True, stop=True)
                last.then_inc(h_full, 1)
                pe.wait_ge(h_ready, 2 * e + 1)
                for c in range(2):
                    for k in range(2):
                        last = pe.matmul(ph[:, c, 0:CANVAS], w2[:, k, c * P:(c + 1) * P], h1[:, k, :],
                                         start=k == 0, stop=k == 1)
                last.then_inc(h_full, 1)
                pe.wait_ge(h_ready, 2 * e + 2)
                if e:
                    pe.wait_ge(pos_ready, e)
                for n in range(2):
                    for k in range(2):
                        last = pe.matmul(pp[0:CANVAS, n, :], h2[:, k, :], w3[:, k, n * 512:(n + 1) * 512],
                                         start=k == 0, stop=k == 1)
                    last.then_inc(pos_full, 1)


def attend(nc, I, persist, W, scratch):
    ident, causal = persist["ident"], persist["causal"]
    with ExitStack() as ctx:
        sb = lambda n, s, d=F32: ctx.enter_context(nc.sbuf_tensor(n, s, d))
        sem = lambda n: ctx.enter_context(nc.semaphore(n))
        norm = Norm(nc, ctx, "a_")
        NORMS = 3 * TT
        emb = sb("emb", [P, TT, D])
        x1 = sb("x1", [P, TT, D])
        xT = sb("xT", [P, DC, T])
        kT = sb("kT", [P, DC, T])
        room = nc.lookup_mloc(kT).addr
        x2HL = [nc.alloc_sbuf_tensor_at(f"x2_{k}", [P, DC, P], F32R, offset=room + k * D * 4) for k in range(4)]
        att = sb("att", [P, 2, TT, T])
        att_flat = att[:].rearrange("p a s t -> p (a s t)")
        x3 = [att_flat[:, k * D:(k + 1) * D] for k in range(2)]
        x3T = [att_flat[:, (2 + k) * D:(3 + k) * D].rearrange("p (c t) -> p c t", c=DC) for k in range(2)]
        xT_flat = xT[:].rearrange("p c t -> p (c t)")
        x2 = [xT_flat[:, k * D:(k + 1) * D] for k in range(2)]
        x2F = [xT_flat[:, (2 + k) * D:(3 + k) * D].rearrange("p (c t) -> p c t", c=DC) for k in range(2)]
        x2H, x2L = [x2HL[0][:], x2HL[2][:]], [x2HL[1][:], x2HL[3][:]]
        hres = sb("hres", [P, TT, D])
        hw, hwT = sb("hw", [P, E0 * R0]), sb("hwT", [P, P])
        lg, rep, ex, top = sb("lg", [P, NR]), sb("rep", [P, NR]), sb("ex", [P, NR]), sb("top", [P, 8])
        pr, w8 = sb("pr", [P, E0, NR]), sb("w8", [P, E0])
        nmax, esum, rinv = sb("nmax", [P, 1]), sb("esum", [P, 1]), sb("rinv", [P, 1])
        cur_emb, cur_pos = sb("cur_emb", [P, TT], I32), sb("cur_pos", [P, TT], I32)
        ps = lambda n, s: ctx.enter_context(nc.psum_tensor(n, s, F32))
        ptr = ps("ptr", [P, 2, 512])
        psc = ps("psc", [P, 2, 512])
        pout = ps("pout", [P, 2, D])
        gather_go = sem("gather_go")
        idx_ready, emb_part, emb_ready, emb_used = sem("idx_ready"), sem("emb_part"), sem("emb_ready"), sem("emb_used")
        x1_ready, tr_full, tr_out = sem("x1_ready"), sem("tr_full"), sem("tr_out")
        k_ready, sc_full, sc_sig, att_ready = sem("k_ready"), sem("sc_full"), sem("sc_sig"), sem("att_ready")
        out_full, out_free, x2_ready, x2L_ready = sem("out_full"), sem("out_free"), sem("x2_ready"), sem("x2L_ready")
        ra_full, ra_free, nmax_ready, ex_ready = sem("ra_full"), sem("ra_free"), sem("nmax_ready"), sem("ex_ready")
        hw_ready, x3_ready, down_full, down_out = sem("hw_ready"), sem("x3_ready"), sem("down_full"), sem("down_out")
        res_ready, res_stored, vchain, h2_done = sem("res_ready"), sem("res_stored"), sem("vchain2"), sem("h2_done")
        TRN = DC + 5 * TT
        block = ctx.enter_context(nc.Block())
        raw_ra, baseH, baseL, lora_b, down = W["raw_ra"], W["baseH"], W["baseL"], W["lora_b"], W["down"]

        @block.gpsimd
        def _(pool):
            neg_half = persist["neg_half"]

            def gather_tokens():
                for t in range(TT):
                    pool.indirect_dma_start(emb[:, t, :], None, I["embed"],
                                            bass.IndirectOffsetOnAxis(ap=cur_emb[:, t:t + 1], axis=0),
                                            bounds_check=N_TOK - 1, oob_is_err=False).then_inc(emb_part, 16)

            def gather_positions(i):
                pool.wait_ge(emb_part, i * 64 + 64)
                pool.sem_inc(gather_go, 1)
                for t in range(TT):
                    pool.indirect_dma_start(emb[:, t, :], None, scratch["pos"],
                                            bass.IndirectOffsetOnAxis(ap=cur_pos[:, t:t + 1], axis=0),
                                            bounds_check=N_POS - 1, oob_is_err=False).then_inc(emb_ready, 16)

            pool.wait_ge(idx_ready, 1)
            gather_tokens()
            gather_positions(0)
            for t in range(TT):
                norm.serve(pool, neg_half, t)
            with pool.Fori(0, B) as b:
                norm.serve(pool, neg_half, b * NORMS + TT)
                pool.wait_ge(emb_used, b + 1)
                pool.sem_inc(gather_go, 1)
                pool.wait_ge(idx_ready, b + 2)
                pool.sem_inc(gather_go, 1)
                gather_tokens()
                norm.serve(pool, neg_half, b * NORMS + TT + 1)
                gather_positions(b + 1)
                for n in range(TT + 2, NORMS + TT):
                    norm.serve(pool, neg_half, b * NORMS + n)

        @block.sync
        def _(sp):
            with sp.Fori(0, B) as b:
                for t in range(TT):
                    sp.wait_ge(res_ready, b * TT + t + 1)
                    sp.dma_start(scratch["res"][ds(b, 1), t, :, :].rearrange("a p d -> (a p) d"),
                                 hres[:, t, :]).then_inc(res_stored, 16)
            sp.wait_ge(res_stored, 16 * TT * B + 16)

        @block.vector
        def _(dve):
            chain = Chain(dve, vchain)

            def next_lists(i):
                dve.tensor_copy(cur_emb[:], persist["ids_emb"][:, ds(i * TT, TT)])
                dve.tensor_copy(cur_pos[:], persist["ids_pos"][:, ds(i * TT, TT)]).then_inc(idx_ready, 1)

            def norm1(i, t):
                if t == 0:
                    dve.wait_ge(emb_ready, i * 64 + 64)
                norm.rows(dve, chain, x1[:, t, :], emb[:, t, :], count()).then_inc(x1_ready, 1)

            done = [0, 0]

            def count():
                done[1] += 1
                return done[0] + done[1] - 1

            next_lists(0)
            for t in range(TT):
                norm1(0, t)
            chain.restart()
            with dve.Fori(0, B) as b:
                done[:] = [b * NORMS + TT, 0]
                next_lists(b + 1)
                for c in range(DC):
                    dve.wait_ge(tr_out, b * TRN + c + 3)
                    dve.tensor_scalar(kT[:, c, :], xT[:, c, :], W["qk"][:, c:c + 1], None, ALU.mult).then_inc(k_ready, 1)

                def mask(h):
                    for s in range(TT):
                        dve.wait_ge(sc_sig, b * H * TT + h * TT + s + 3)
                        diag = att[:, h % 2, s, s * P:(s + 1) * P]
                        dve.tensor_tensor(diag, diag, causal[:], ALU.mult).then_inc(att_ready, 1)

                def add_head(h):
                    cols = slice(h * HD, (h + 1) * HD)
                    dve.wait_ge(out_full, b * (H + TT) + h + 1)
                    if h == 0:
                        dve.wait_ge(res_stored, b * 64 + 16)
                    v = W["vb"][:, h:h + 1, :].broadcast_to([P, TT, HD])
                    acc = hres[:, :, cols]
                    dve.tensor_tensor(acc, pout[:, h % 2, :].rearrange("p (t d) -> p t d", t=TT), v,
                                      ALU.mult).then_inc(out_free, 1)
                    dve.wait_ge(out_free, b * (H + TT) + h + 3)
                    ins = dve.tensor_tensor(acc, acc, emb[:, :, cols], ALU.add)
                    chain(ins)
                    if h == H - 1:
                        dve.engine_nop().then_inc(emb_used, 1)

                mask(0)
                mask(1)
                add_head(0)
                mask(2)
                add_head(1)
                mask(3)
                add_head(2)
                add_head(3)

                def norm2(t):
                    norm.rows(dve, chain, x2[t % 2], hres[:, t, :], count()).then_inc(x2_ready, 1)
                    dve.tensor_tensor(hres[:, t, :], hres[:, t, :], W["base_b"][:], ALU.add).then_inc(h2_done, 1)

                def low_part(t):
                    dve.wait_ge(tr_out, b * TRN + DC + TR2[t] + 4)
                    dve.tensor_tensor(x2L[t % 2], x2F[t % 2], x2H[t % 2].bitcast(F32), ALU.subtract).then_inc(x2L_ready, 1)

                def route(t):
                    dve.wait_ge(ra_full, b * TT + t + 1)
                    chain(dve.tensor_tensor(lg[:], psc[:, 0, 0:NR], W["router_b"][:], ALU.add))
                    chain(dve.max(top[:], lg[:]))
                    dve.tensor_scalar(nmax[:], top[:, 0:1], -1.0, None, ALU.mult).then_inc(nmax_ready, 1)
                    chain(dve.match_replace(rep[:], top[:], lg[:], NEG))
                    dve.wait_ge(ex_ready, b * TT + t + 1)
                    chain(dve.scalar_tensor_tensor(rep[:], rep[:], -1e38, ex[:], ALU.is_lt, ALU.mult))
                    chain(dve.reciprocal(rinv[:], esum[:]))
                    chain(dve.tensor_tensor(pr[:], W["onehot"][:],
                                            rep[:].rearrange("p (a n) -> p a n", a=1).broadcast_to([P, E0, NR]), ALU.mult))
                    chain(dve.tensor_reduce(w8[:], pr[:], AX, ALU.add))
                    chain(dve.tensor_scalar(w8[:], w8[:], rinv[:, 0:1], 2.0, ALU.mult, ALU.mult))
                    chain(dve.tensor_tensor(hw[:].rearrange("p (e r) -> p e r", e=E0),
                                            psc[:, 0, NR + 1:RA].rearrange("p (e r) -> p e r", e=E0),
                                            w8[:].rearrange("p (e a) -> p e a", a=1).broadcast_to([P, E0, R0]), ALU.mult))
                    dve.engine_nop().then_inc(hw_ready, 1)
                    dve.engine_nop().then_inc(ra_free, 1)

                def add_ffn(t):
                    dve.wait_ge(out_full, b * (H + TT) + H + t + 1)
                    dve.wait_ge(h2_done, b * TT + t + 1)
                    dve.tensor_tensor(hres[:, t, :], hres[:, t, :], pout[:, t % 2, :], ALU.add).then_inc(out_free, 1)
                    dve.wait_ge(out_free, b * (H + TT) + H + t + 3)
                    norm.rows(dve, chain, x3[t % 2], hres[:, t, :], count()).then_inc(x3_ready, 1)
                    norm.with_residual(dve, chain, hres[:, t, :]).then_inc(res_ready, 1)

                norm2(0)
                for t in range(TT):
                    low_part(t)
                    route(t)
                    if t < TT - 1:
                        norm2(t + 1)
                    if t >= 2:
                        norm1(b + 1, 2 * t - 4)
                        norm1(b + 1, 2 * t - 3)
                    add_ffn(t)
                chain.restart()

        @block.scalar
        def _(act):
            act.sem_inc(tr_out, 2)
            act.sem_inc(sc_sig, 2)
            act.sem_inc(down_out, 1)
            act.sem_inc(out_free, 2)
            act.sem_inc(ra_free, 1)
            act.sem_inc(res_stored, 16)
            with act.Fori(0, B) as b:
                n = 0

                def take(dst, n):
                    act.wait_ge(tr_full, b * TRN + n + 1)
                    act.activation(dst, ptr[:, n % 2, :], ACT.Copy).then_inc(tr_out, 1)

                for c in range(DC):
                    take(xT[:, c, :], c)
                for h in range(H):
                    if h >= 2:
                        act.wait_ge(out_full, b * (H + TT) + h - 1)
                    for s in range(TT):
                        k = h * TT + s
                        act.wait_ge(sc_full, b * H * TT + k + 1)
                        act.activation(att[:, h % 2, s, s * P:T], psc[:, k % 2, 0:T - s * P], ACT.Sigmoid,
                                       scale=4.0 * HD ** -0.5).then_inc(sc_sig, 1)

                def take2(t):
                    for g in range(2):
                        n = DC + TR2[t] + g
                        act.wait_ge(tr_full, b * TRN + n + 1)
                        src = ptr[:, n % 2, :].rearrange("p (c t) -> p c t", c=DC // 2)
                        cs = slice(g * DC // 2, (g + 1) * DC // 2)
                        act.activation(x2F[t % 2][:, cs, :], src, ACT.Copy)
                        act.activation(x2H[t % 2][:, cs, :], src, ACT.Copy).then_inc(tr_out, 1)

                def take3(t):
                    for g in range(2):
                        n = DC + TR3[t] + g
                        act.wait_ge(tr_full, b * TRN + n + 1)
                        src = ptr[:, n % 2, :].rearrange("p (c t) -> p c t", c=DC // 2)
                        act.activation(x3T[t % 2][:, g * DC // 2:(g + 1) * DC // 2, :], src, ACT.Copy).then_inc(tr_out, 1)

                take2(0)
                for t in range(TT):
                    act.wait_ge(nmax_ready, b * TT + t + 1)
                    act.activation(ex[:], lg[:], ACT.Exp, bias=nmax[:, 0:1], accum_out=esum[:, 0:1]).then_inc(ex_ready, 1)
                    if t < TT - 1:
                        take2(t + 1)
                    n = DC + TRW[t]
                    act.wait_ge(tr_full, b * TRN + n + 1)
                    act.activation(hwT[:], ptr[:, n % 2, 0:P], ACT.Copy).then_inc(tr_out, 1)
                    if t > 0:
                        take3(t - 1)
                take3(TT - 1)
                act.wait_ge(down_full, b + 1)
                act.activation(persist["xm"][:, ds(b, T, B)], psc[:, 1, :], ACT.Gelu,
                               bias=W["b_down"][:, 0:1]).then_inc(down_out, 1)

        @block.tensor
        def _(pe):
            with pe.Fori(0, B) as b:
                def bank(n):
                    pe.wait_ge(tr_out, b * TRN + n + 1)
                    return ptr[:, n % 2, :]

                for c in range(DC):
                    if c == 0:
                        pe.wait_ge(x1_ready, b * TT + TT)
                    dst = bank(c)
                    for t in range(TT):
                        last = pe.transpose(dst[:, t * P:(t + 1) * P], x1[:, t, c * P:(c + 1) * P], ident[:])
                    last.then_inc(tr_full, 1)

                def scores(h):
                    pe.wait_ge(k_ready, b * DC + HC * (h + 1))
                    for s in range(TT):
                        k = h * TT + s
                        pe.wait_ge(sc_sig, b * H * TT + k + 1)
                        if k == 1:
                            pe.wait_ge(down_out, b + 1)
                        for c in range(HC):
                            last = pe.matmul(psc[:, k % 2, 0:T - s * P], kT[:, HC * h + c, s * P:(s + 1) * P],
                                             xT[:, HC * h + c, s * P:T], start=c == 0, stop=c == HC - 1)
                        last.then_inc(sc_full, 1)

                def attn_out(h):
                    pe.wait_ge(att_ready, b * H * TT + (h + 1) * TT)
                    pe.wait_ge(out_free, b * (H + TT) + h + 1)
                    for t in range(TT):
                        for s in range(t + 1):
                            last = pe.matmul(pout[:, h % 2, t * HD:(t + 1) * HD], att[:, h % 2, s, t * P:(t + 1) * P],
                                             x1[:, s, h * HD:(h + 1) * HD], start=s == 0, stop=s == t)
                    last.then_inc(out_full, 1)

                scores(0)
                scores(1)
                attn_out(0)
                scores(2)
                attn_out(1)
                scores(3)
                attn_out(2)
                attn_out(3)

                def turn(src, n0):
                    for g in range(2):
                        dst = bank(n0 + g)
                        for k in range(DC // 2):
                            c = g * DC // 2 + k
                            last = pe.transpose(dst[:, k * P:(k + 1) * P], src[:, c * P:(c + 1) * P], ident[:])
                        last.then_inc(tr_full, 1)

                def turn2(t):
                    pe.wait_ge(x2_ready, b * TT + t + 1)
                    turn(x2[t % 2], DC + TR2[t])

                def ra(t):
                    pe.wait_ge(tr_out, b * TRN + DC + TR2[t] + 4)
                    pe.wait_ge(ra_free, b * TT + t + 1)
                    for c in range(DC):
                        last = pe.matmul(psc[:, 0, 0:RA], x2F[t % 2][:, c, :], raw_ra[:, c, :], start=c == 0, stop=c == DC - 1)
                    last.then_inc(ra_full, 1)

                def base(t):
                    pe.wait_ge(out_free, b * (H + TT) + H + t + 1)
                    for k, (lhs, rhs) in enumerate(((x2H, baseH), (x2H, baseL), (x2L, baseH))):
                        if k == 2:
                            pe.wait_ge(x2L_ready, b * TT + t + 1)
                        for c in range(DC):
                            for n in range(2):
                                pe.matmul(pout[:, t % 2, n * 512:(n + 1) * 512], lhs[t % 2][:, c, :],
                                          rhs[:, c, n * 512:(n + 1) * 512], start=k == 0 and c == 0, stop=False)

                def lora(t):
                    pe.wait_ge(hw_ready, b * TT + t + 1)
                    dst = bank(DC + TRW[t])
                    pe.transpose(dst[:, 0:P], hw[:], ident[:]).then_inc(tr_full, 1)
                    pe.wait_ge(tr_out, b * TRN + DC + TRW[t] + 3)
                    for n in range(2):
                        last = pe.matmul(pout[:, t % 2, n * 512:(n + 1) * 512], hwT[:], lora_b[:, n * 512:(n + 1) * 512],
                                         start=False, stop=True)
                    last.then_inc(out_full, 1)

                def project_down(t):
                    pe.wait_ge(x3_ready, b * TT + t + 1)
                    turn(x3[t % 2], DC + TR3[t])
                    pe.wait_ge(tr_out, b * TRN + DC + TR3[t] + 4)
                    for c in range(DC):
                        last = pe.matmul(psc[:, 1, t * P:(t + 1) * P], down[:, c, :], x3T[t % 2][:, c, :],
                                         start=c == 0, stop=c == DC - 1)
                    if t == TT - 1:
                        last.then_inc(down_full, 1)

                turn2(0)
                for t in range(TT):
                    ra(t)
                    base(t)
                    if t < TT - 1:
                        turn2(t + 1)
                    lora(t)
                    if t > 0:
                        project_down(t - 1)
                project_down(TT - 1)


def awaited(eng, sem, value):
    if not isinstance(value, int) or value > 0:
        eng.wait_ge(sem, value)


def hydra(nc, I, persist, scratch):
    ident = persist["ident"]
    with ExitStack() as ctx:
        sb = lambda n, s, d=F32: ctx.enter_context(nc.sbuf_tensor(n, s, d))
        sem = lambda n: ctx.enter_context(nc.semaphore(n))
        flow = sb("flow", [P, 3 * B * T])
        cur = [sb(f"cur{k}", [P, IC]) for k in range(2)]
        in_w = sb("in_w", [P, DIN])
        conv_in = sb("conv_in", [P, DIN])
        conv_bc = sb("conv_bc", [P, DTB, DCONV])
        conv_x, conv_bx = sb("conv_x", [P, 2, DCONV]), sb("conv_bx", [P, 2])
        bcdt_w, fcd = sb("bcdt_w", [P, BF]), sb("fcd", [P, 2, NH])
        bias = sb("bias", [P, NB])
        a_half = sb("a_half", [P, 2 * NH])
        out_w, norm_w = sb("out_w", [P, 2, DM]), sb("norm_w", [P, 2])
        ones, block_mask = sb("ones", [P, P]), sb("block_mask", [P, P])
        gate = sb("gate", [P, 3])
        zs = [sb(f"zs{k}", [P, 2, IC]) for k in range(2)]
        xs = [sb(f"xs{k}", [P, 2, IC]) for k in range(2)]
        xraw = sb("xraw", [P, 2, IC])
        before = sb("before", [P, DCONV - 1 + B, BF])
        taps = sb("taps", [P, B, DTB, DCONV])
        rows = [sb(f"rows{k}", [P, B, NB]) for k in range(2)]
        xrow = [sb(f"xrow{k}", [P, B, DIN]) for k in range(2)]
        mix = [sb(f"mix{k}", [P, B, B * NH]) for k in range(2)]
        mixT = [sb(f"mixT{k}", [P, B, B * NH]) for k in range(2)]
        diag = [sb(f"diag{k}", [P, B, NH, P]) for k in range(2)]
        fwd, bwd = sb("fwd", [P, B, B, NH]), sb("bwd", [P, B, B, NH])
        cb, cbn = sb("cb", [P, B, B]), sb("cbn", [P, B, B, DST])
        dt, u, ln1, pol, dec = (sb(n, [P, B, 2 * NH]) for n in ("dt", "u", "ln1", "pol", "dec"))
        yz, sq, sqs, rs = sb("yz", [P, 2, 512]), sb("sq", [P, 2, 512]), sb("sqs", [P, 512]), sb("rs", [P, 512])
        eps_col = sb("eps_col", [P, 1])
        ps = lambda n, s: ctx.enter_context(nc.psum_tensor(n, s, F32))
        pcv, pst = ps("pcv", [P, 2, 512]), ps("pst", [P, 2, 512])
        py, po = ps("py", [P, 2, 512]), ps("po", [P, 2, 512])
        cur_ready = sem("cur_ready")
        w_ld, w_ready, w_half = sem("hw_ld"), sem("hw_ready2"), sem("w_half")
        cv_full, cv_out, g_full, g_out = (sem(n) for n in ("cv_full", "cv_out", "g_full", "g_out"))
        xraw_ready, xc_ready, xs_ready = sem("xraw_ready"), sem("xc_ready"), sem("xs_ready")
        bc_conv, bc_ready = sem("bc_conv"), sem("bc_ready")
        t_full, t_out, xr_full, xr_out = sem("t_full"), sem("t_out"), sem("xr_full"), sem("xr_out")
        u_ready, ln_ready, dec_in, dec_ready = sem("u_ready"), sem("ln_ready"), sem("dec_in"), sem("dec_ready")
        mix_ready, mix_st, mix_ld = sem("mix_ready"), [sem("mix_st0"), sem("mix_st1")], [sem("mix_ld0"), sem("mix_ld1")]
        diag_ready, y_full, yz_ready, sq_ready = sem("diag_ready"), sem("y_full"), sem("yz_ready"), sem("sq_ready")
        sqs_ready, log_ready = sem("sqs_ready"), sem("log_ready")
        o_full, rs_ready, flow_ready, vchain = sem("o_full"), sem("rs_ready"), sem("flow_ready"), sem("vchain3")
        block = ctx.enter_context(nc.Block())
        NW = 12
        LAST = 2 * NITEM - 1

        SPREAD = 5

        def spread_tiles(eng, k, tiles):
            mask = block_mask[:].rearrange("p (a n) -> p a n", a=1).broadcast_to([P, NH, P])
            for n in tiles:
                src = mixT[k][:, n, :].rearrange("p (a t h) -> p h a t", a=1, h=NH).broadcast_to([P, NH, 16, B])
                last = eng.tensor_tensor(diag[k][:, n].rearrange("p h (q t) -> p h q t", t=B), src,
                                         mask.rearrange("p h (q t) -> p h q t", t=B), ALU.mult)
            return last

        def run(eng, step, restart=lambda: None):
            with eng.Fori(0, NITEM - 1) as j:
                for k in range(2):
                    step(Item(j * 2 + k, k), 2)
                restart()
            for k in range(2):
                step(Item(LAST - 1 + k, k), 1 - k)
            restart()

        @block.sync
        def _(sp):
            for dst, name in ((in_w[:], "in_z"), (conv_in[:], "in_x"), (bcdt_w[:], "in_bcdt"), (conv_bx[:], "conv_bx"),
                              (conv_x[:], "conv_x"), (norm_w[:], "hy_norm")):
                sp.dma_start(dst, I[name]).then_inc(w_ld, 16)
            sp.dma_start(bias[:], I["hy_bias"].to_broadcast([P, NB])).then_inc(w_ld, 16)
            sp.dma_start(conv_bc[:].rearrange("p c k -> p (c k)"), I["conv_bc"].to_broadcast([P, DCONV * DTB])).then_inc(w_ld, 16)
            sp.dma_start(fcd[:], I["fcd"].rearrange("(c p) n -> p c n", p=P)).then_inc(w_ld, 16)
            sp.dma_start(out_w[:], I["hy_out"].rearrange("(c p) n -> p c n", p=P)).then_inc(w_ld, 16)
            sp.dma_start(a_half[:], I["a_log"].to_broadcast([P, 2 * NH])).then_inc(w_ld, 16)
            sp.dma_start(gate[:, 0:1], I["gate1"].to_broadcast([P, 1])).then_inc(w_ld, 16)
            def bounce(i, k):
                sp.wait_ge(mix_ready, i + 1)
                sp.dma_start(scratch["mix"][ds(i * P, P), :], mix[k][:].rearrange("p s c -> p (s c)")).then_inc(mix_st[k], 16)
                sp.wait_ge(mix_st[k], (i - k) * 8 + 32)
                sp.dma_start(mixT[k][:], scratch["mix"][ds(i * P, P), :].rearrange("m (s c) -> (m s) c", s=B)
                             .rearrange("(n p) c -> p n c", p=P)).then_inc(mix_ld[k], 16)

            with sp.Fori(0, NITEM) as j:
                for k in range(2):
                    bounce(j * 2 + k, k)

        @block.gpsimd
        def _(pool):
            pool.memset(ones[:], 1.0)
            pool.memset(eps_col[:], EPS)
            for m in (fwd, bwd):
                pool.memset(m[:], 0.0)
            pool.memset(block_mask[:], 1.0).then_inc(w_half, 1)
            pool.wait_ge(w_half, 1)
            m = block_mask[:].rearrange("p (r t) -> p r t", t=B)
            pool.affine_select(out=m, in_=m, compare_op=ALU.is_ge, fill=0.0, base=0,
                               pattern=[[-B, 16], [0, B]], channel_multiplier=1).then_inc(w_half, 1)
            pool.wait_ge(w_half, 2)
            pool.affine_select(out=m, in_=m, compare_op=ALU.is_ge, fill=0.0, base=B - 1,
                               pattern=[[B, 16], [0, B]], channel_multiplier=-1).then_inc(w_half, 1)
            pool.wait_ge(w_half, 3)
            for m in (fwd, bwd):
                flat = m[:].rearrange("p c s h -> p (c s) h")
                pool.memset(flat[:, 0:B * B:B + 1, :], 1.0).then_inc(w_half, 1)

            def take_item(i, k):
                pool.tensor_copy(cur[k][:], flow[:, ds(i * IC, IC)]).then_inc(cur_ready, 1)

            def spread(i, k):
                pool.wait_ge(mix_ld[k], (i - k) * 8 + 16)
                spread_tiles(pool, k, range(SPREAD)).then_inc(diag_ready, 1)

            def step(it, more):
                i, k, n = it.n, it.k, it.n + 1
                if more > 1:
                    pool.wait_ge(flow_ready, i * 2 + 1)
                    pool.wait_ge(cv_full, i * 8 + 8)
                    pool.wait_ge(t_full, i + 1)
                    take_item(i + 2, k)
                for blk in range(2):
                    pool.wait_ge(sq_ready, i * 2 + blk + 1)
                    pool.tensor_tensor(sqs[:], sq[:, 0, :], sq[:, 1, :], ALU.add).then_inc(sqs_ready, 1)
                if more:
                    spread(n, 1 - k)

            pool.wait_ge(flow_ready, 1)
            for k in range(2):
                take_item(k, k)
            spread(0, 0)
            run(pool, step)

        @block.scalar
        def _(act):
            act.wait_ge(w_ld, 16 * NW)
            act.wait_ge(w_ready, 1)
            act.activation(a_half[:], a_half[:], ACT.Exp, scale=0.5).then_inc(w_ready, 1)
            act.activation(gate[:, 1:2], gate[:, 0:1], ACT.Sigmoid).then_inc(w_ready, 1)
            act.sem_inc(cv_out, 2)
            act.sem_inc(xr_out, 1)
            for k in range(2):
                act.sem_inc(mix_st[k], 16)

            def take_x(i, k, blk):
                if blk == 0:
                    awaited(act, xc_ready, i)
                for c in range(2):
                    act.wait_ge(cv_full, i * 8 + 2 * blk + c + 1)
                    cols = slice(blk * 512, (blk + 1) * 512)
                    act.activation(xraw[:, c, cols], pcv[:, c, :], ACT.Copy)
                    act.activation(xs[k][:, c, cols], pcv[:, c, :], ACT.Copy, scale=conv_x[:, c, DCONV - 1:DCONV]).then_inc(cv_out, 1)
                if blk == 1:
                    act.wait_ge(cv_out, i * 8 + 4 + 2)
                    act.sem_inc(xraw_ready, 1)

            def silu_x(i, k):
                act.wait_ge(xc_ready, i + 1)
                for c in range(2):
                    act.activation(xs[k][:, c, :], xs[k][:, c, :], ACT.Silu, bias=conv_bx[:, c:c + 1]).then_inc(xs_ready, 1)

            def take_z(i, k, blk):
                for c in range(2):
                    act.wait_ge(cv_full, i * 8 + 4 + 2 * blk + c + 1)
                    act.activation(zs[k][:, c, blk * 512:(blk + 1) * 512], pcv[:, c, :], ACT.Silu).then_inc(cv_out, 1)

            def take_rows(i):
                act.wait_ge(t_full, i + 1)
                act.activation(before[:, DCONV - 1:, :], pst[:, 0, 0:B * BF].rearrange("p (s n) -> p s n", s=B), ACT.Copy).then_inc(t_out, 1)

            def silu_rows(i, k):
                act.wait_ge(bc_conv, i + 1)
                act.activation(rows[k][:, :, 0:DTB], rows[k][:, :, 0:DTB], ACT.Silu).then_inc(bc_ready, 1)

            def take_gates(i, k):
                act.wait_ge(g_full, i + 1)
                act.activation(rows[k][:, :, BF:NB], pst[:, 1, 0:B * NH].rearrange("p (s n) -> p s n", s=B), ACT.Copy).then_inc(g_out, 1)

            def take_xrows(i, k, half):
                for n in (2 * half, 2 * half + 1):
                    act.wait_ge(xr_full, i * 4 + n + 1)
                    act.activation(xrow[k][:, 2 * n:2 * n + 2, :],
                                   pst[:, n % 2, :].rearrange("p (a c) -> p a c", a=2), ACT.Copy).then_inc(xr_out, 1)

            def square(i, blk):
                act.wait_ge(yz_ready, i * 2 + blk + 1)
                act.activation(sq[:], yz[:], ACT.Square).then_inc(sq_ready, 1)

            def root(i, blk):
                act.wait_ge(o_full, i * 2 + blk + 1)
                act.activation(rs[:], po[:, 1, :], ACT.Ln, bias=eps_col[:, 0:1], scale=1.0 / DIN).then_inc(log_ready, 1)
                act.wait_ge(log_ready, i * 2 + blk + 1)
                act.activation(rs[:], rs[:], ACT.Exp, scale=-0.5).then_inc(rs_ready, 1)

            def soft(i):
                act.wait_ge(u_ready, i + 1)
                act.activation(u[:], u[:], ACT.Exp).then_inc(ln_ready, 1)
                act.wait_ge(ln_ready, i * 2 + 1)
                act.activation(ln1[:], u[:], ACT.Ln, bias=1.0).then_inc(ln_ready, 1)

            def decays(i):
                act.wait_ge(dec_in, i + 1)
                act.activation(dec[:], dec[:], ACT.Exp, scale=-1.0).then_inc(dec_ready, 1)

            def step(it, more):
                i, k, n = it.n, it.k, it.n + 1
                if more:
                    for blk in range(2):
                        take_z(n, 1 - k, blk)
                    silu_x(n, 1 - k)
                    silu_rows(n, 1 - k)
                    soft(n)
                for blk in range(2):
                    square(i, blk)
                    if more > 1:
                        take_x(i + 2, k, blk)
                    if more and blk == 1:
                        take_gates(n, 1 - k)
                        take_xrows(n, 1 - k, 0)
                    root(i, blk)
                    if more:
                        if blk == 0:
                            decays(n)
                        else:
                            take_xrows(n, 1 - k, 1)
                if more > 1:
                    take_rows(i + 2)

            for blk in range(2):
                take_x(0, 0, blk)
            take_rows(0)
            for blk in range(2):
                take_z(0, 0, blk)
            silu_x(0, 0)
            for blk in range(2):
                take_x(1, 1, blk)
            silu_rows(0, 0)
            take_gates(0, 0)
            soft(0)
            decays(0)
            for half in range(2):
                take_xrows(0, 0, half)
            take_rows(1)
            run(act, step)

        @block.vector
        def _(dve):
            chain = Chain(dve, vchain)
            dve.wait_ge(w_ld, 16 * NW)
            dve.tensor_copy(flow[:, 0:B * T], persist["xm"][:])
            dve.tensor_scalar(a_half[:], a_half[:], 88.0, None, ALU.min).then_inc(w_ready, 1)
            dve.memset(before[:, 0:DCONV - 1, :], 0.0)
            for c in range(2):
                last = dve.tensor_scalar(out_w[:, c, :], out_w[:, c, :], norm_w[:, c:c + 1], None, ALU.mult)
            last.then_inc(flow_ready, 1)
            dve.wait_ge(w_ready, 3)
            chain(dve.tensor_scalar(gate[:, 0:1], gate[:, 1:2], 1.0, None, ALU.add))
            chain(dve.tensor_scalar(gate[:, 2:3], gate[:, 1:2], -1.0, 1.0, ALU.mult, ALU.add))
            dve.wait_ge(w_half, 5)
            chain.restart()
            def raw_dt(k):
                return rows[k][:, :, DTB:DTB + 2 * NH]

            def convolve_rows(i, k):
                dve.wait_ge(t_out, i + 1)
                windows = bass.AP(before, 0, [list(before[:].ap[0]), [BF, B], [1, DTB], [BF, DCONV]])
                w = conv_bc[:].rearrange("p (a c) k -> p a c k", a=1).broadcast_to([P, B, DTB, DCONV])
                chain(dve.tensor_tensor(taps[:], windows, w, ALU.mult))
                bc = rows[k][:, :, 0:DTB]
                chain(dve.tensor_reduce(bc, taps[:], AX, ALU.add))
                over = lambda a, b: bias[:, a:b].rearrange("p (a c) -> p a c", a=1).broadcast_to([P, B, b - a])
                dve.tensor_tensor(bc, bc, over(0, DTB), ALU.add).then_inc(bc_conv, 1)
                chain(dve.tensor_tensor(raw_dt(k), before[:, DCONV - 1:, DTB:BF], over(DTB, BF), ALU.add))
                raw = raw_dt(k)
                dve.scalar_tensor_tensor(u[:], raw, -1.0, raw, ALU.mult, ALU.min).then_inc(u_ready, 1)

            def pairs(i, k):
                r = rows[k]
                dve.wait_ge(bc_ready, i + 1)
                cc = r[:, :, DST:2 * DST].rearrange("p c (a n) -> p c a n", a=1).broadcast_to([P, B, B, DST])
                bb = r[:, :, 0:DST].rearrange("p (a s) n -> p a s n", a=1).broadcast_to([P, B, B, DST])
                chain(dve.tensor_tensor(cbn[:], cc, bb, ALU.mult))
                chain(dve.tensor_reduce(cb[:], cbn[:], AX, ALU.add))

            def softplus(i, k):
                raw = raw_dt(k)
                dve.wait_ge(ln_ready, i * 2 + 2)
                chain(dve.tensor_scalar(pol[:], u[:], -1.0 / 6, None, ALU.mult))
                for coef in (1.0 / 5, -1.0 / 4, 1.0 / 3, -1.0 / 2, 1.0):
                    chain(dve.scalar_tensor_tensor(pol[:], pol[:], coef, u[:], ALU.add, ALU.mult))
                chain(dve.tensor_tensor(pol[:], pol[:], ln1[:], ALU.subtract))
                chain(dve.scalar_tensor_tensor(pol[:], u[:], 0.0625, pol[:], ALU.is_lt, ALU.mult))
                chain(dve.tensor_tensor(pol[:], pol[:], ln1[:], ALU.add))
                chain(dve.scalar_tensor_tensor(dt[:], raw, 0.0, pol[:], ALU.max, ALU.add))

                ah = a_half[:].rearrange("p (a h) -> p a h", a=1).broadcast_to([P, B, 2 * NH])
                chain(dve.tensor_tensor(dec[:], dt[:], ah, ALU.mult))
                chain(dve.scalar_tensor_tensor(dec[:], dec[:], 1e18, ah, ALU.min, ALU.mult))
                dve.tensor_scalar(dec[:], dec[:], 200.0, None, ALU.min).then_inc(dec_in, 1)

            def decay_products(i):
                dve.wait_ge(dec_ready, i + 1)
                for c in range(1, B - 1):
                    a = dec[:, c:c + 1, 0:NH].broadcast_to([P, c, NH])
                    chain(dve.tensor_tensor(fwd[:, c, 0:c, :], fwd[:, c - 1, 0:c, :], a, ALU.mult))
                    d = B - 1 - c
                    a = dec[:, d:d + 1, NH:2 * NH].broadcast_to([P, c, NH])
                    chain(dve.tensor_tensor(bwd[:, d, d + 1:B, :], bwd[:, d + 1, d + 1:B, :], a, ALU.mult))

            def mixing(i, k):
                r = rows[k]
                w = mix[k][:].rearrange("p s (t h) -> p t s h", h=NH)
                flat = mix[k][:].rearrange("p s (t h) -> p (s t) h", h=NH)
                scale = cbn[:].rearrange("p c s (a h) -> p c s a h", h=NH)[:, :, :, 0, :]
                scale2 = cbn[:].rearrange("p c s (a h) -> p c s a h", h=NH)[:, :, :, 1, :]
                cb4 = cb[:].rearrange("p c (s a) -> p c s a", a=1).broadcast_to([P, B, B, NH])
                for dst, src, off in ((scale, fwd, 0), (scale2, bwd, NH)):
                    d4 = dt[:, :, off:off + NH].rearrange("p (a s) h -> p a s h", a=1).broadcast_to([P, B, B, NH])
                    chain(dve.tensor_tensor(dst, src[:], d4, ALU.mult))
                    chain(dve.tensor_tensor(dst, dst, cb4, ALU.mult))
                dve.wait_ge(mix_st[k], (i - k) * 8 + 16)
                chain(dve.tensor_copy(w[:, 1:B], scale[:, 0:B - 1]))
                chain(dve.memset(w[:, 0:1], 0.0))
                chain(dve.tensor_tensor(w[:, 0:B - 1], w[:, 0:B - 1], scale2[:, 1:B], ALU.add))
                dve.wait_ge(g_out, i + 1)
                dve.tensor_tensor(flat[:, 0:B * B:B + 1, :], r[:, :, BF:NB], bias[:, BF:NB].rearrange("p (a h) -> p a h", a=1)
                                  .broadcast_to([P, B, NH]), ALU.add).then_inc(mix_ready, 1)

            def spread(i, k):
                dve.wait_ge(mix_ld[k], (i - k) * 8 + 16)
                spread_tiles(dve, k, range(SPREAD, B)).then_inc(diag_ready, 1)

            def convolve(i, k):
                dve.wait_ge(xraw_ready, i + 1)
                for d in range(1, DCONV):
                    for c in range(2):
                        acc = xs[k][:, c, :].rearrange("p (q s) -> p q s", s=B)[:, :, d:B]
                        src = xraw[:, c, :].rearrange("p (q s) -> p q s", s=B)[:, :, 0:B - d]
                        tap = conv_x[:, c, DCONV - 1 - d:DCONV - d]
                        last = dve.scalar_tensor_tensor(acc, src, tap, acc, ALU.mult, ALU.add)
                    chain(last)
                dve.engine_nop().then_inc(xc_ready, 1)

            def gated(i, k, blk):
                dve.wait_ge(y_full, i * 2 + blk + 1)
                cols = slice(blk * 512, (blk + 1) * 512)
                dve.tensor_tensor(yz[:], py[:], zs[k][:, :, cols], ALU.mult).then_inc(yz_ready, 1)

            def finish(i, blk):
                dve.wait_ge(rs_ready, i * 2 + blk + 1)
                at = (i + NITEM) * IC + blk * 512
                dve.tensor_tensor(flow[:, ds(at, 512)], po[:, 0, :], rs[:], ALU.mult).then_inc(flow_ready, 1)

            def step(it, more):
                i, k, n = it.n, it.k, it.n + 1
                if more:
                    pairs(n, 1 - k)
                gated(i, k, 0)
                if more:
                    softplus(n, 1 - k)
                finish(i, 0)
                gated(i, k, 1)
                if more:
                    decay_products(n)
                    mixing(n, 1 - k)
                if more > 1:
                    convolve(i + 2, k)
                finish(i, 1)
                if more > 1:
                    convolve_rows(i + 2, k)
                if more:
                    spread(n, 1 - k)

            convolve(0, 0)
            convolve_rows(0, 0)
            pairs(0, 0)
            softplus(0, 0)
            decay_products(0)
            mixing(0, 0)
            convolve(1, 1)
            convolve_rows(1, 1)
            spread(0, 0)
            chain.restart()
            run(dve, step, chain.restart)
            dve.wait_ge(flow_ready, 1 + 4 * NITEM)
            chain(dve.tensor_scalar(flow[:, 0:B * T], flow[:, 0:B * T], gate[:, 0:1], None, ALU.mult))
            chain(dve.scalar_tensor_tensor(persist["xm"][:], flow[:, 2 * B * T:3 * B * T], gate[:, 2:3],
                                           flow[:, 0:B * T], ALU.mult, ALU.add))

        @block.tensor
        def _(pe):
            pe.wait_ge(w_ld, 16 * NW)
            pe.wait_ge(w_half, 5)
            pe.wait_ge(flow_ready, 1)

            def block_of(k, blk):
                return cur[k][:, blk * 512:(blk + 1) * 512]

            def project_x(i, k, blk):
                pe.wait_ge(cur_ready, i + 1)
                for c in range(2):
                    pe.wait_ge(cv_out, i * 8 + 2 * blk + c + 1)
                    pe.matmul(pcv[:, c, :], conv_in[:, c * P:(c + 1) * P], block_of(k, blk), start=True, stop=True).then_inc(cv_full, 1)

            def project_z(i, k, blk):
                for c in range(2):
                    pe.wait_ge(cv_out, i * 8 + 4 + 2 * blk + c + 1)
                    pe.matmul(pcv[:, c, :], in_w[:, c * P:(c + 1) * P], block_of(k, blk), start=True, stop=True).then_inc(cv_full, 1)

            def project_rows(i, k):
                pe.wait_ge(xr_out, i * 4 + 1)
                at_step = cur[k][:].rearrange("p (q s) -> p s q", s=B)
                for s in range(B):
                    last = pe.matmul(pst[:, 0, s * BF:(s + 1) * BF], at_step[:, s, :], bcdt_w[:], start=True, stop=True)
                last.then_inc(t_full, 1)

            def project_gates(i, k):
                pe.wait_ge(xs_ready, i * 2 + 2)
                for s in range(B):
                    dst = pst[:, 1, s * NH:(s + 1) * NH]
                    for c in range(2):
                        last = pe.matmul(dst, xs[k][:, c, :].rearrange("p (q s) -> p s q", s=B)[:, s, :], fcd[:, c, :],
                                         start=c == 0, stop=c == 1)
                last.then_inc(g_full, 1)

            def turn_x(i, k, half):
                for n in (2 * half, 2 * half + 1):
                    if n == 0:
                        pe.wait_ge(t_out, i + 1)
                    elif n == 1:
                        pe.wait_ge(g_out, i + 1)
                    else:
                        pe.wait_ge(xr_out, i * 4 + n)
                    for a in range(2):
                        for c in range(2):
                            t = 2 * n + a
                            last = pe.transpose(pst[:, n % 2, (2 * a + c) * P:(2 * a + c + 1) * P],
                                                xs[k][:, c, t * P:(t + 1) * P], ident[:])
                    last.then_inc(xr_full, 1)

            def apply(i, k, blk):
                for n in range(4):
                    t = 4 * blk + n
                    for h in range(NH):
                        q = HDIM * (h % 2)
                        last = pe.matmul(py[q:q + HDIM, h // 2, n * P:(n + 1) * P],
                                         xrow[k][:, t, h * HDIM:(h + 1) * HDIM], diag[k][:, t, h, :],
                                         start=True, stop=True)
                last.then_inc(y_full, 1)

            def project_out(i, blk):
                pe.wait_ge(yz_ready, i * 2 + blk + 1)
                for c in range(2):
                    pe.matmul(po[:, 0, :], out_w[:, c, :], yz[:, c, :], start=c == 0, stop=c == 1)
                pe.wait_ge(sqs_ready, i * 2 + blk + 1)
                pe.matmul(po[:, 1, :], ones[:], sqs[:], start=True, stop=True).then_inc(o_full, 1)

            def step(it, more):
                i, k, n = it.n, it.k, it.n + 1
                if more:
                    for blk in range(2):
                        project_z(n, 1 - k, blk)
                pe.wait_ge(diag_ready, i * 2 + 2)
                pe.wait_ge(xr_out, i * 4 + 5)
                for blk in range(2):
                    apply(i, k, blk)
                    if more > 1:
                        project_x(i + 2, k, blk)
                    if more and blk == 1:
                        project_gates(n, 1 - k)
                        turn_x(n, 1 - k, 0)
                    pe.wait_ge(flow_ready, i * 2 + blk + 1)
                    project_out(i, blk)
                if more:
                    turn_x(n, 1 - k, 1)
                if more > 1:
                    project_rows(i + 2, k)

            for blk in range(2):
                project_x(0, 0, blk)
            project_rows(0, 0)
            for blk in range(2):
                project_z(0, 0, blk)
            for blk in range(2):
                project_x(1, 1, blk)
            project_gates(0, 0)
            for half in range(2):
                turn_x(0, 0, half)
            project_rows(1, 1)
            run(pe, step)


class Item:

    def __init__(self, n, k):
        self.n, self.k = n, k


class Tile:

    def __init__(self, i, k):
        self.i, self.k = (i + k // TT, k % TT) if k // TT else (i, k)
        self.n = self.i * TT + self.k
        self.exists = not isinstance(self.n, int) or 0 <= self.n < B * TT

    def after(self, d):
        return Tile(self.i, self.k + d)


def experts(nc, I, persist, scratch, out):
    ident, neg_half, xm = persist["ident"], persist["neg_half"], persist["xm"]
    KR = KE * RANK
    with ExitStack() as ctx:
        sb = lambda n, s, d=F32: ctx.enter_context(nc.sbuf_tensor(n, s, d))
        sem = lambda n: ctx.enter_context(nc.semaphore(n))
        norm = Norm(nc, ctx, "e_")
        aH, aL = sb("aH", [P, DC, KR], F32R), sb("aL", [P, DC, KR], F32R)
        bH, bL = sb("bH", [P, DC, D], F32R), sb("bL", [P, DC, D], F32R)
        wr, up, b_up = sb("wr", [P, DC, KE]), sb("up", [P, D]), sb("b_up", [P, D])
        h = sb("h", [P, TT, D])
        x5, hg = sb("x5", [P, D]), sb("hg", [P, KR])
        xF, xH, xL = sb("xF", [P, DC, P]), sb("xH", [P, DC, P], F32R), sb("xL", [P, DC, P], F32R)
        gH, gL = sb("gH", [P, DC, P], F32R), sb("gL", [P, DC, P], F32R)
        mid = sb("mid", [P, 2, P])
        sc = sb("sc5", [P, KE])
        top, rep, rep2, ex, gt = sb("top5", [P, 16]), sb("rep5", [P, KE]), sb("rep6", [P, KE]), sb("ex5", [P, KE]), sb("gt", [P, KE])
        nmax, gsum, ginv = sb("nmax5", [P, 1]), sb("gsum", [P, 1]), sb("ginv", [P, 1])
        ps = lambda n, s: ctx.enter_context(nc.psum_tensor(n, s, F32))
        ptr, pup, psc, pa, po = ps("ptr5", [P, 2, 512]), ps("pup", [P, 512]), ps("psc5", [P, 512]), ps("pa", [P, 2, 512]), ps("po5", [P, 2, 512])
        w_ld, stage_ld, stage_used, stage_high = sem("ew_ld"), [sem(f"estage{k}") for k in range(4)], sem("estage_used"), sem("estage_high")
        res_ld, out_st = [sem(f"res_ld{k}") for k in range(TT)], [sem(f"out_st{k}") for k in range(TT)]
        bias_ready, mid_ready, up_full, up_added = sem("bias_ready"), sem("mid_ready"), sem("up_full"), sem("up_added")
        x5_ready, t5_full, t5_out, xL_ready = sem("x5_ready"), sem("t5_full"), sem("t5_out"), sem("xL_ready")
        sc_full, sc_used, nmax_ready, ex_ready = sem("sc_full5"), sem("sc_used"), sem("nmax5_ready"), sem("ex5_ready")
        a_full, hg_ready, t6_full, t6_high, t6_low = (sem(n) for n in ("a_full", "hg_ready", "t6_full", "t6_high", "t6_low"))
        store_go = sem("store_go")
        b_full, out_ready, vchain = sem("b_full"), sem("out_ready"), sem("vchain4")
        block = ctx.enter_context(nc.Block())
        GROUPS = B

        def run(eng, step, restart=lambda: None):
            step(Tile(0, -1))
            for k in range(TT):
                step(Tile(0, k))
            restart()
            with eng.Fori(1, GROUPS - 1) as i:
                for k in range(TT):
                    step(Tile(i, k))
                restart()
            for k in range(TT + 1):
                step(Tile(GROUPS - 1, k))
            restart()

        chunks = [(I["ea_w"], aH, aL, c) for c in range(DC)] + [(I["eb_w"], bH, bL, c) for c in range(DC)]

        @block.sync
        def _(sp):
            for n, (src, _, _, c) in enumerate(chunks):
                if n >= TT:
                    sp.wait_ge(stage_used, n - TT + 1)
                sp.dma_start(h[:, n % TT, :], src[c * P:(c + 1) * P, :]).then_inc(stage_ld[n % TT], 16)

            def load(t):
                if t.exists:
                    awaited(sp, out_st[t.k], 16 * t.i)
                    sp.dma_start(h[:, t.k, :], scratch["res"][at(t.i), t.k, :, :].rearrange("a p d -> (a p) d")).then_inc(res_ld[t.k], 16)

            def step(t):
                if t.after(-1).exists:
                    last = t.after(-1)
                    sp.wait_ge(out_ready, last.n + 1)
                    sp.sem_inc(store_go, 1)
                    sp.dma_start(out[at(last.i), last.k * P:(last.k + 1) * P, :].rearrange("a p d -> (a p) d"),
                                 h[:, last.k, :]).then_inc(out_st[last.k], 16)
                load(t.after(3))

            for n in range(2):
                sp.wait_ge(stage_used, len(chunks))
                load(Tile(0, n))
            run(sp, step)
            for k in range(TT):
                sp.wait_ge(out_st[k], 16 * B)

        @block.gpsimd
        def _(pool):
            def bias(t):
                if t.exists:
                    pool.wait_ge(res_ld[t.k], 16 * t.i + 16)
                    pool.tensor_tensor(h[:, t.k, :], h[:, t.k, :], b_up[:], ALU.add).then_inc(bias_ready, 1)

            def step(t):
                if t.after(1).exists:
                    norm.serve(pool, neg_half, t.after(1).n)
                bias(t.after(2))

            pool.wait_ge(w_ld, 48)
            bias(Tile(0, 0))
            run(pool, step)

        @block.scalar
        def _(act):
            act.dma_start(wr[:], I["wr"].rearrange("(c p) n -> p c n", p=P)).then_inc(w_ld, 16)
            act.dma_start(up[:], I["w_up"]).then_inc(w_ld, 16)
            act.dma_start(b_up[:], I["b_up"].to_broadcast([P, D])).then_inc(w_ld, 16)
            for n, (_, high, _, c) in enumerate(chunks):
                act.wait_ge(stage_ld[n % TT], 16 * (n // TT + 1))
                act.activation(high[:, c, :], h[:, n % TT, :], ACT.Copy).then_inc(stage_high, 1)

            def take_mid(t):
                if t.exists:
                    awaited(act, up_full, 2 * t.n - 2)
                    act.activation(mid[:, t.k % 2, :], xm[:, ds(t.i + t.k * P * B, P, B)], ACT.Copy).then_inc(mid_ready, 1)

            def step(t):
                if t.after(-1).exists:
                    last = t.after(-1)
                    for g in range(2):
                        act.wait_ge(t6_full, 2 * last.n + g + 1)
                        act.activation(gH[:, 4 * g:4 * g + 4, :], ptr[:, g, :].rearrange("p (c t) -> p c t", c=4), ACT.Copy).then_inc(t6_high, 1)
                if t.exists:
                    act.wait_ge(nmax_ready, t.n + 1)
                    act.activation(ex[:], sc[:], ACT.Exp, bias=nmax[:, 0:1]).then_inc(ex_ready, 1)
                take_mid(t.after(2))
                if t.after(1).exists:
                    nxt = t.after(1)
                    for g in range(2):
                        act.wait_ge(t5_full, 2 * nxt.n + g + 1)
                        src = ptr[:, g, :].rearrange("p (c t) -> p c t", c=4)
                        act.activation(xF[:, 4 * g:4 * g + 4, :], src, ACT.Copy)
                        act.activation(xH[:, 4 * g:4 * g + 4, :], src, ACT.Copy).then_inc(t5_out, 1)

            take_mid(Tile(0, 0))
            run(act, step)

        @block.vector
        def _(dve):
            chain = Chain(dve, vchain)
            for n, (_, high, low, c) in enumerate(chunks):
                dve.wait_ge(stage_high, n + 1)
                dve.tensor_tensor(low[:, c, :], h[:, n % TT, :], high[:, c, :].bitcast(F32), ALU.subtract).then_inc(stage_used, 1)

            def add_up(t, n):
                if t.exists:
                    if n == 0:
                        dve.wait_ge(bias_ready, t.n + 1)
                    dve.wait_ge(up_full, 2 * t.n + n + 1)
                    half = h[:, t.k, n * 512:(n + 1) * 512]
                    dve.tensor_tensor(half, half, pup[:], ALU.add).then_inc(up_added, 1)

            def gates(t):
                dve.wait_ge(sc_full, t.n + 1)
                chain(dve.tensor_copy(sc[:], psc[:, 0:KE]))
                dve.engine_nop().then_inc(sc_used, 1)
                chain(dve.max(top[:, 0:8], sc[:]))
                dve.tensor_scalar(nmax[:], top[:, 0:1], -1.0, None, ALU.mult).then_inc(nmax_ready, 1)
                chain(dve.match_replace(rep[:], top[:, 0:8], sc[:], NEG))
                chain(dve.max(top[:, 8:16], rep[:]))
                chain(dve.match_replace(rep2[:], top[:, 8:16], rep[:], NEG))
                dve.wait_ge(ex_ready, t.n + 1)
                chain(dve.scalar_tensor_tensor(gt[:], rep2[:], -1e38, ex[:], ALU.is_lt, ALU.mult))
                chain(dve.tensor_reduce(gsum[:], gt[:], AX, ALU.add))
                chain(dve.reciprocal(ginv[:], gsum[:]))
                chain(dve.tensor_scalar(gt[:], gt[:], ginv[:, 0:1], 2.0, ALU.mult, ALU.mult))

            def weigh(t):
                dve.wait_ge(a_full, t.n + 1)
                awaited(dve, t6_full, 2 * t.n)
                g4 = gt[:].rearrange("p (a k) -> p a k", a=1).broadcast_to([P, RANK // 2, KE])
                for n in range(2):
                    last = dve.tensor_tensor(hg[:, n * 512:(n + 1) * 512].rearrange("p (r k) -> p r k", k=KE),
                                             pa[:, n, :].rearrange("p (r k) -> p r k", k=KE), g4, ALU.mult)
                last.then_inc(hg_ready, 1)

            def step(t):
                nxt, last = t.after(1), t.after(-1)
                if nxt.exists:
                    dve.wait_ge(up_added, 2 * nxt.n + 2)
                    awaited(dve, t5_full, 2 * nxt.n)
                    norm.rows(dve, chain, x5[:], h[:, nxt.k, :], nxt.n).then_inc(x5_ready, 1)
                if last.exists:
                    for g in range(2):
                        dve.wait_ge(t6_high, 2 * last.n + g + 1)
                        dve.tensor_tensor(gL[:, 4 * g:4 * g + 4, :], ptr[:, g, :].rearrange("p (c t) -> p c t", c=4),
                                          gH[:, 4 * g:4 * g + 4, :].bitcast(F32), ALU.subtract).then_inc(t6_low, 1)
                if t.exists:
                    gates(t)
                    weigh(t)
                add_up(t.after(2), 0)
                if nxt.exists:
                    dve.wait_ge(t5_out, 2 * nxt.n + 2)
                    dve.tensor_tensor(xL[:], xF[:], xH[:].bitcast(F32), ALU.subtract).then_inc(xL_ready, 1)
                add_up(t.after(2), 1)
                if last.exists:
                    dve.wait_ge(b_full, last.n + 1)
                    dve.tensor_tensor(h[:, last.k, :], h[:, last.k, :], po[:].rearrange("p a n -> p (a n)"), ALU.add).then_inc(out_ready, 1)

            for n in range(2):
                add_up(Tile(0, 0), n)
            run(dve, step, chain.restart)

        @block.tensor
        def _(pe):
            pe.wait_ge(w_ld, 48)
            pe.wait_ge(stage_used, len(chunks))

            def project_up(t, n):
                if t.exists:
                    pe.wait_ge(mid_ready, t.n + 1)
                    awaited(pe, up_added, 2 * t.n + n)
                    pe.matmul(pup[:], mid[:, t.k % 2, :], up[:, n * 512:(n + 1) * 512], start=True, stop=True).then_inc(up_full, 1)

            def products(dst, high, low, wH, wL, low_ready):
                for k, (lhs, rhs) in enumerate(((high, wH), (high, wL), (low, wH))):
                    if k == 2:
                        low_ready()
                    for c in range(DC):
                        for n in range(2):
                            last = pe.matmul(dst[:, n, :], lhs[:, c, :], rhs[:, c, n * 512:(n + 1) * 512],
                                             start=k == 0 and c == 0, stop=k == 2 and c == DC - 1)
                return last

            def turn(src, g):
                for c in range(4):
                    k = 4 * g + c
                    last = pe.transpose(ptr[:, g, c * P:(c + 1) * P], src[:, k * P:(k + 1) * P], ident[:])
                return last

            def step(t):
                nxt, last = t.after(1), t.after(-1)
                if t.exists:
                    pe.wait_ge(t5_out, 2 * t.n + 2)
                    awaited(pe, hg_ready, t.n)
                    products(pa, xH, xL, aH, aL, lambda: pe.wait_ge(xL_ready, t.n + 1)).then_inc(a_full, 1)
                project_up(t.after(2), 0)
                if nxt.exists:
                    pe.wait_ge(x5_ready, nxt.n + 1)
                    for g in range(2):
                        awaited(pe, t6_low, 2 * nxt.n - 3 + g)
                        turn(x5, g).then_inc(t5_full, 1)
                    pe.wait_ge(t5_out, 2 * nxt.n + 2)
                    awaited(pe, sc_used, nxt.n)
                    for c in range(DC):
                        s = pe.matmul(psc[:, 0:KE], xF[:, c, :], wr[:, c, :], start=c == 0, stop=c == DC - 1)
                    s.then_inc(sc_full, 1)
                project_up(t.after(2), 1)
                if last.exists:
                    pe.wait_ge(t6_high, 2 * last.n + 2)
                    awaited(pe, out_ready, last.n)
                    products(po, gH, gL, bH, bL, lambda: pe.wait_ge(t6_low, 2 * last.n + 2)).then_inc(b_full, 1)
                if t.exists:
                    pe.wait_ge(hg_ready, t.n + 1)
                    for g in range(2):
                        pe.wait_ge(t5_out, 2 * nxt.n + g + 1) if nxt.exists else None
                        turn(hg, g).then_inc(t6_full, 1)

            for n in range(2):
                project_up(Tile(0, 0), n)
            run(pe, step)


def at(i):
    return slice(i, i + 1) if isinstance(i, int) else ds(i, 1)


def program(nc, I, out, stages=4, dbg=None):
    with ExitStack() as ctx:
        sb = lambda n, s, d=F32: ctx.enter_context(nc.sbuf_tensor(n, s, d))
        persist = {"ident": sb("ident", [P, P]), "causal": sb("causal", [P, P]), "xm": sb("xm", [P, T * B]), "neg_half": sb("neg_half", [P, 1]),
                   "ids_emb": sb("ids_emb", [P, (B + 1) * TT], I32), "ids_pos": sb("ids_pos", [P, (B + 1) * TT], I32)}
        scratch = {"pos": nc.dram_tensor("pos_rows", [N_POS, D], F32).ap(),
                   "res": nc.dram_tensor("residual", [B, TT, P, D], F32).ap(),
                   "mix": nc.dram_tensor("mixing", [2 * T, B * B * NH], F32).ap()}
        with ExitStack() as wctx:
            wb = lambda n, s, d=F32: wctx.enter_context(nc.sbuf_tensor(n, s, d))
            W = {"baseH": wb("baseH", [P, DC, D], F32R), "baseL": wb("baseL", [P, DC, D], F32R),
                 "raw_ra": wb("raw_ra", [P, DC, RA]), "lora_b": wb("lora_b", [P, D]), "down": wb("down", [P, DC, DM]),
                 "b_down": wb("b_down", [P, 1]), "base_b": wb("base_b", [P, D]), "router_b": wb("router_b", [P, NR]),
                 "emap_i": wb("emap_i", [P, NR], I32), "emap": wb("emap", [P, NR]), "onehot": wb("onehot", [P, E0, NR]),
                 "qk": wb("qk", [P, DC]), "vb": wb("vb", [P, H, HD])}
            tables(nc, I, persist, W, scratch)
            attend(nc, I, persist, W, scratch)
        if stages >= 3:
            hydra(nc, I, persist, scratch)
        if dbg:
            dbg(nc, persist, scratch)
        if stages >= 4:
            experts(nc, I, persist, scratch, out)


def layout(inputs):
    a = {k: np.asarray(v) for k, v in inputs.items()}
    f = np.float32
    half = P // 2
    freq = np.exp(np.arange(half, dtype=f) * f(-np.log(100.0) / (half - 1))).astype(f)
    pos_const = np.zeros((P, 2 + N_POS), f)
    pos_const[:, 0] = np.concatenate([freq, freq])
    pos_const[half:, 1] = 0.25
    pos_const[:, 2:] = np.arange(N_POS, dtype=f)
    ids = np.zeros((P, (B + 1) * TT), np.int32)
    ids[:, :B * TT] = a["x"].reshape(B * TT, P).T
    row = lambda v: np.ascontiguousarray(v.reshape(1, -1))
    con = np.ascontiguousarray
    ra_w = np.zeros((D, RA), f)
    ra_w[:, :NR] = a["L0_ffn_router_W"].T
    ra_w[:, NR + 1:] = a["L0_ffn_A"].reshape(E0 * R0, D).T
    b12 = np.stack([a["L0_tok_b1"], a["L0_tok_b2"]], 1).reshape(E_POS * 2, 2, P)
    return {
        "pos_const": pos_const, "ids": ids, "embed": a["L0_tok_embed_table"],
        "W1": a["L0_tok_W1"], "W2": a["L0_tok_W2"], "W3": a["L0_tok_W3"], "b3": a["L0_tok_b3"],
        "b12": con(b12.transpose(2, 0, 1)),
        "bv_q": row(a["L0_attn_bv_q"]), "bv_k": row(a["L0_attn_bv_k"]), "bv_v": row(a["L0_attn_bv_v"]),
        "base_w": con(a["L0_ffn_base_W"].T), "base_b": row(a["L0_ffn_base_b"]), "ra_w": ra_w,
        "router_b": row(a["L0_ffn_router_b"]), "expert_map": row(a["L0_ffn_expert_map"]),
        "lora_b": con(a["L0_ffn_B"].transpose(0, 2, 1).reshape(E0 * R0, D)),
        "in_z": con(a["L1_attn_hy_in_w"][:DIN].T), "in_x": con(a["L1_attn_hy_in_w"][DIN:2 * DIN].T),
        "in_bcdt": con(a["L1_attn_hy_in_w"][2 * DIN:].T),
        "conv_bx": con(a["L1_attn_hy_conv_b"][:DIN].reshape(2, P).T),
        "hy_bias": con(np.concatenate([a["L1_attn_hy_conv_b"][DIN:]] + [a["L1_attn_hy_dt_bias"]] * 2 + [a["L1_attn_hy_D"]]).reshape(1, NB)),
        "hy_norm": con(a["L1_attn_hy_norm_w"].reshape(2, P).T),
        "conv_x": con(a["L1_attn_hy_conv_w"][:DIN, 0, :].reshape(2, P, DCONV).transpose(1, 0, 2)),
        "conv_bc": con(a["L1_attn_hy_conv_w"][DIN:, 0, :].reshape(1, -1)), "fcd": con(a["L1_attn_hy_fcD_w"].T),
        "hy_out": con(a["L1_attn_hy_out_w"].T), "a_log": con(np.concatenate([a["L1_attn_hy_A_log"]] * 2).reshape(1, -1)),
        "gate1": con(a["L1_attn_gate1"].reshape(1, 1)),
        "ea_w": con(a["L1_ffn_A"].transpose(2, 1, 0).reshape(D, RANK * KE)),
        "eb_w": con(a["L1_ffn_B"].transpose(2, 0, 1).reshape(RANK * KE, D)),
        "wr": con(a["L1_ffn_Wr"].T), "w_up": con(a["L1_attn_w_up"].T), "b_up": row(a["L1_attn_b_up"]),
        "w_down": con(a["L1_attn_w_down"].T), "b_down": a["L1_attn_b_down"].reshape(P, 1),
    }


def kernel(**inputs):
    from concourse import bacc
    from concourse.bass_utils import run_bass_kernel_spmd

    nc = bacc.Bacc("TRN2", target_bir_lowering=False, num_devices=1)
    arrays = {"in_" + k: v for k, v in layout(inputs).items()}
    I = {k[3:]: nc.dram_tensor(k, v.shape, mybir.dt.from_np(v.dtype), kind="ExternalInput").ap() for k, v in arrays.items()}
    out = nc.dram_tensor("out", (B, T, D), F32, kind="ExternalOutput").ap()
    program(nc, I, out)
    return run_bass_kernel_spmd(nc, [arrays], core_ids=[0]).results[0]["out"]
```

```python
from contextlib import ExitStack

import numpy as np
import concourse.bass as bass
from concourse import mybir

F32 = mybir.dt.float32
F32R = mybir.dt.float32r
I32 = mybir.dt.int32
ACT = mybir.ActivationFunctionType
ALU = mybir.AluOpType
AX = mybir.AxisListType.X
ds = bass.ds

P = 128
B, T, D = 8, 512, 1024
TT = T // P
DC = D // P
N_TOK, CANVAS, E_POS, HID = 8000, 125, 4, 256
N_POS = CANVAS * E_POS
H, HD = 4, 256
HC = HD // P
NR, E0, R0 = 15, 8, 16
RA = NR + 1 + E0 * R0
DM, DIN, DST, NH, HDIM, DCONV = 128, 256, 16, 4, 64, 7
KE, TOPK, RANK = 64, 16, 16
EPS = 1e-5
SKIP = 1 << 20
NEG = -3.0e38
DTB = 2 * DST
BF = DTB + 2 * NH
NB = BF + NH
IC = 1024
NITEM = T // P
INV2PI = float(np.float32(1 / (2 * np.pi)))
PI_A, PI_B = 6.28125, float(np.float32(2 * np.pi - 6.28125))
ROUND = 12582912.0


TR2, TRW, TR3 = {0: 0}, {}, {}
_n = 2
for _t in range(TT):
    if _t < TT - 1:
        TR2[_t + 1] = _n
        _n += 2
    TRW[_t] = _n
    _n += 1
    if _t > 0:
        TR3[_t - 1] = _n
        _n += 2
TR1 = _n
TR3[TT - 1] = TR1 + DC


class Chain:

    def __init__(self, eng, sem):
        self.eng, self.sem, self.n = eng, sem, 0

    def __call__(self, ins):
        self.n += 1
        ins.then_inc(self.sem, 1)
        self.eng.wait_ge(self.sem, self.n)

    def restart(self):
        self.eng.sem_clear(self.sem)
        self.n = 0


class Norm:

    def __init__(self, nc, ctx, name):
        sb = lambda n, s: ctx.enter_context(nc.sbuf_tensor(name + n, s, F32))
        self.stats, self.mean_var, self.var, self.rstd = sb("stats", [P, 2, 6]), sb("mv", [P, 2]), sb("var", [P, 1]), sb("rstd", [P, 1])
        self.scale, self.shift = sb("scale", [P, 1]), sb("shift", [P, 1])
        self.var_ready = ctx.enter_context(nc.semaphore(name + "var_ready"))
        self.rstd_ready = ctx.enter_context(nc.semaphore(name + "rstd_ready"))

    def rows(self, dve, chain, dst, src, n):
        dve.bn_stats(self.stats[:, 0, :], src[:, 0:D // 2])
        chain(dve.bn_stats(self.stats[:, 1, :], src[:, D // 2:D]))
        chain(dve.bn_aggr(self.mean_var[:], self.stats[:]))
        dve.tensor_scalar(self.var[:], self.mean_var[:, 1:2], EPS, None, ALU.add).then_inc(self.var_ready, 1)
        dve.wait_ge(self.rstd_ready, n + 1)
        return dve.tensor_scalar(dst, src, self.mean_var[:, 0:1], self.rstd[:, 0:1], ALU.subtract, ALU.mult)

    def with_residual(self, dve, chain, rows):
        dve.tensor_scalar(self.scale[:], self.rstd[:], 1.0, None, ALU.add)
        chain(dve.scalar_tensor_tensor(self.shift[:], self.mean_var[:, 0:1], -1.0, self.rstd[:], ALU.mult, ALU.mult))
        return lambda: dve.tensor_scalar(rows, rows, self.scale[:, 0:1], self.shift[:, 0:1], ALU.mult, ALU.add)

    def serve(self, pool, neg_half, n):
        pool.wait_ge(self.var_ready, n + 1)
        pool.tensor_tensor(self.rstd[:], self.var[:], neg_half[:], ALU.pow).then_inc(self.rstd_ready, 1)


def tables(nc, I, persist, W, scratch):
    ident, ids_emb, ids_pos = persist["ident"], persist["ids_emb"], persist["ids_pos"]
    baseH, baseL, qk, vb = W["baseH"], W["baseL"], W["qk"], W["vb"]
    with ExitStack() as ctx:
        sb = lambda n, s, d=F32: ctx.enter_context(nc.sbuf_tensor(n, s, d))
        sem = lambda n: ctx.enter_context(nc.semaphore(n))
        NE = E_POS
        pos_in = sb("pos_in", [P, 2 + N_POS])
        ang = sb("ang", [P, N_POS])
        turns = sb("turns", [P, N_POS])
        w1, w2, w3 = sb("w1", [P, NE, HID]), sb("w2", [P, NE, 2, HID]), sb("w3", [P, NE, 2, D])
        b12, b3, pick = sb("b12", [P, 2 * NE, 2]), sb("b3", [NE, D]), sb("pick", [NE, N_POS])
        h1, h2 = sb("h1", [P, 2, N_POS]), sb("h2", [P, 2, N_POS])
        room = [sb(f"room{k}", [P, D]) for k in range(2)]
        absx, lnx = (room[k][:, 0:2 * N_POS].rearrange("p (c n) -> p c n", c=2) for k in range(2))
        posrow = [room[k][0:CANVAS, :] for k in range(2)]
        stage = sb("stage", [P, 2, D])
        bv, sgn, alpha = sb("bv", [P, H, HD]), sb("sgn", [P, H, HD]), sb("alpha", [P, H])
        bqk, sqk = sb("bqk", [P, 2 * DC]), sb("sqk", [P, 2 * DC])
        aqk, mean_w = sb("aqk", [P, 2 * H]), sb("mean_w", [P, P])
        idf, t0, t1, t2 = (sb(n, [P, (B + 1) * TT]) for n in ("idf", "t0", "t1", "t2"))
        ids = sb("ids", [P, (B + 1) * TT], I32)
        ph = ctx.enter_context(nc.psum_tensor("ph", [P, 2, 512], F32))
        pp = [ctx.enter_context(nc.psum_tensor(f"pp{k}", [P, 2, 512], F32)) for k in range(2)]
        pq = ctx.enter_context(nc.psum_tensor("pq", [P, 512], F32))
        pos_ld, ids_ld = sem("pos_ld"), sem("ids_ld")
        in_ld, const_ld, stage_ld = sem("in_ld"), sem("const_ld"), [sem("stage_ld0"), sem("stage_ld1")]
        w_ld, w3_ld, pos_st = [sem("w1_ld"), sem("w2_ld")], [sem(f"w3_ld{e}") for e in range(NE)], [sem("pos_st0"), sem("pos_st1")]
        stage_used, ident_done = sem("stage_used"), sem("ident_done")
        ang_ready, sin_ready, ids_ready = sem("ang_ready"), sem("sin_ready"), sem("ids_ready")
        h_full, h_pre, h_exp, h_ready = sem("h_full"), sem("h_pre"), sem("h_exp"), sem("h_ready")
        pos_full, pos_ready = sem("pos_full"), [sem("pos_ready0"), sem("pos_ready1")]
        abs_ready, mean_full = sem("abs_ready"), sem("mean_full")
        vchain = sem("vchain")
        block = ctx.enter_context(nc.Block())

        @block.sync
        def _(sp):
            sp.dma_start(pos_in[:], I["pos_const"]).then_inc(pos_ld, 16)
            sp.dma_start(w1[:], I["W1"].rearrange("e p n -> p e n")).then_inc(w_ld[0], 16)
            sp.dma_start(b12[:], I["b12"]).then_inc(ids_ld, 16)
            sp.dma_start(ids[:], I["ids"]).then_inc(ids_ld, 16)
            sp.dma_start(bqk[:], I["bind_qk"]).then_inc(in_ld, 16)
            sp.dma_start(b3[:], I["b3"]).then_inc(in_ld, 16)
            sp.dma_start(pick[:], I["pick"]).then_inc(in_ld, 16)
            sp.dma_start(w2[:].rearrange("p e c n -> p (e c) n"), I["W2"].rearrange("e (c p) n -> p (e c) n", p=P)).then_inc(w_ld[1], 16)
            sp.dma_start(bv[:].rearrange("p h d -> p (h d)"), I["bv_v"].to_broadcast([P, D])).then_inc(in_ld, 16)
            for e in range(NE):
                sp.dma_start(w3[:, e], I["W3"][e].rearrange("(c p) n -> p c n", p=P)).then_inc(w3_ld[e], 16)
            for e in range(NE):
                sp.wait_ge(pos_ready[e % 2], 2 * (e // 2) + 2)
                sp.dma_start(scratch["pos"][e * CANVAS:(e + 1) * CANVAS, :], posrow[e % 2]).then_inc(pos_st[e % 2], 16)
            for k in range(2):
                sp.wait_ge(pos_st[k], 16 * NE // 2)

        @block.scalar
        def _(act):
            act.dma_start(W["raw_ra"][:], I["ra_w"].rearrange("(c p) n -> p c n", p=P)).then_inc(const_ld, 16)
            act.dma_start(W["lora_b"][:], I["lora_b"]).then_inc(const_ld, 16)
            act.dma_start(W["down"][:], I["w_down"].rearrange("(c p) n -> p c n", p=P)).then_inc(const_ld, 16)
            act.dma_start(W["b_down"][:], I["b_down"]).then_inc(const_ld, 16)
            act.dma_start(W["base_b"][:], I["base_b"].to_broadcast([P, D])).then_inc(const_ld, 16)
            act.dma_start(W["router_b"][:], I["router_b"].to_broadcast([P, NR])).then_inc(const_ld, 16)
            act.dma_start(W["emap_i"][:], I["expert_map"].to_broadcast([P, NR])).then_inc(const_ld, 16)
            for c in range(2):
                act.dma_start(stage[:, c, :], I["base_w"][c * P:(c + 1) * P, :]).then_inc(stage_ld[c % 2], 16)
            act.wait_ge(ang_ready, 1)
            act.activation(ang[:], ang[:], ACT.Sin).then_inc(sin_ready, 1)
            def fetch_base(c):
                act.wait_ge(stage_used, c - 1)
                act.dma_start(stage[:, c % 2, :], I["base_w"][c * P:(c + 1) * P, :]).then_inc(stage_ld[c % 2], 16)

            for s in range(2):
                act.wait_ge(h_pre, s + 1)
                act.activation(lnx, absx, ACT.Exp).then_inc(h_exp, 1)
                act.wait_ge(h_exp, 2 * s + 1)
                act.activation(lnx, lnx, ACT.Ln, bias=1.0).then_inc(h_exp, 1)
            for e in range(NE):
                fetch_base(2 + e)
                act.wait_ge(pos_full, 2 * e + 1)
                if e >= 2:
                    act.wait_ge(pos_st[e % 2], 16 * (e // 2))
                elif e == 0:
                    act.wait_ge(h_ready, 2)
                act.activation(posrow[e % 2][:, 0:512], pp[e % 2][0:CANVAS, 0, :], ACT.Copy).then_inc(pos_ready[e % 2], 1)
            for c in range(2 + NE, DC):
                fetch_base(c)
            act.wait_ge(const_ld, 16 * 7)

        @block.gpsimd
        def _(pool):
            pool.memset(persist["neg_half"][:], -0.5)
            pool.memset(mean_w[:], 1.0 / HD)
            pool.memset(ident[:], 0.0).then_inc(ident_done, 1)
            pool.memset(persist["causal"][:], 1.0).then_inc(ident_done, 1)
            pool.wait_ge(ident_done, 2)
            pool.affine_select(out=ident[:], in_=ident[:], compare_op=ALU.not_equal, fill=1.0, base=0,
                               pattern=[[-1, P]], channel_multiplier=1).then_inc(ident_done, 1)
            pool.affine_select(out=persist["causal"][:], in_=persist["causal"][:], compare_op=ALU.is_ge, fill=0.0,
                               base=0, pattern=[[1, P]], channel_multiplier=-1).then_inc(ident_done, 1)
            pool.wait_ge(ids_ready, 1)
            for t in range(TT):
                pool.indirect_dma_start(W["emb"][:, t, :], None, I["embed"],
                                        bass.IndirectOffsetOnAxis(ap=ids_emb[:, t:t + 1], axis=0),
                                        bounds_check=N_TOK - 1, oob_is_err=False).then_inc(W["emb_part"], 16)

        @block.vector
        def _(dve):
            chain = Chain(dve, vchain)
            dve.wait_ge(pos_ld, 16)
            chain(dve.tensor_scalar(turns[:], pos_in[:, 2:], 1.0 / CANVAS, float(CANVAS), ALU.mult, ALU.mult))
            chain(dve.tensor_scalar(ang[:], turns[:], pos_in[:, 0:1], None, ALU.mult))
            chain(dve.tensor_scalar(turns[:], ang[:], INV2PI, None, ALU.mult))
            chain(dve.tensor_scalar(turns[:], turns[:], pos_in[:, 1:2], ROUND, ALU.add, ALU.add))
            chain(dve.tensor_scalar(turns[:], turns[:], -ROUND, None, ALU.add))
            chain(dve.scalar_tensor_tensor(ang[:], turns[:], -PI_A, ang[:], ALU.mult, ALU.add))
            chain(dve.scalar_tensor_tensor(ang[:], turns[:], -PI_B, ang[:], ALU.mult, ALU.add))
            chain(dve.tensor_scalar(turns[:, 0:1], pos_in[:, 1:2], float(2 * np.pi), None, ALU.mult))
            chain(dve.tensor_scalar(ang[:], ang[:], turns[:, 0:1], None, ALU.add))
            dve.tensor_scalar(ang[:], ang[:], 3.1415925, -3.1415925, ALU.min, ALU.max).then_inc(ang_ready, 1)

            dve.wait_ge(ids_ld, 16 * 2)
            chain(dve.tensor_copy(idf[:], ids[:]))
            chain(dve.tensor_scalar(t0[:], idf[:], 0.0, float(N_TOK), ALU.is_lt, ALU.mult))
            chain(dve.tensor_scalar(t1[:], idf[:], float(N_TOK), None, ALU.is_ge))
            chain(dve.tensor_scalar(t2[:], idf[:], float(N_TOK + N_POS), None, ALU.is_ge))
            chain(dve.tensor_tensor(idf[:], idf[:], t0[:], ALU.add))
            chain(dve.tensor_scalar(t0[:], t1[:], -1.0, 1.0, ALU.mult, ALU.add))
            chain(dve.tensor_tensor(t0[:], t0[:], idf[:], ALU.mult))
            chain(dve.tensor_tensor(t1[:], t1[:], t2[:], ALU.subtract))
            chain(dve.scalar_tensor_tensor(t0[:], t1[:], float(SKIP), t0[:], ALU.mult, ALU.add))
            chain(dve.tensor_copy(ids_emb[:], t0[:]))
            dve.engine_nop().then_inc(ids_ready, 1)
            chain(dve.tensor_scalar(t0[:], idf[:], -float(N_TOK), None, ALU.add))
            chain(dve.tensor_tensor(t0[:], t0[:], t1[:], ALU.mult))
            chain(dve.tensor_scalar(t1[:], t1[:], -float(SKIP), float(SKIP), ALU.mult, ALU.add))
            chain(dve.tensor_tensor(t0[:], t0[:], t1[:], ALU.add))
            chain(dve.tensor_copy(ids_pos[:], t0[:]))

            def softplus(s, h):
                dve.wait_ge(h_full, s + 1)
                for e in range(NE):
                    own = slice(e * CANVAS, (e + 1) * CANVAS)
                    for c in range(2):
                        last = dve.tensor_scalar(h[:, c, own], ph[:, c, own], b12[:, 2 * e + s, c:c + 1], None, ALU.add)
                chain(last)
                dve.scalar_tensor_tensor(absx, h[:], -1.0, h[:], ALU.mult, ALU.min).then_inc(h_pre, 1)
                chain(dve.tensor_scalar(h[:], h[:], 0.0, None, ALU.max))
                dve.wait_ge(h_exp, 2 * s + 2)
                dve.tensor_tensor(h[:], h[:], lnx, ALU.add).then_inc(h_ready, 1)

            softplus(0, h1)

            dve.wait_ge(in_ld, 16 * 4)
            chain(dve.scalar_tensor_tensor(sqk[:], bqk[:], -1.0, bqk[:], ALU.mult, ALU.max))
            dve.engine_nop().then_inc(abs_ready, 1)
            chain(dve.tensor_reduce(alpha[:], bv[:], AX, ALU.add, apply_absolute_value=True))
            chain(dve.tensor_scalar(alpha[:], alpha[:], 1.0 / HD, None, ALU.mult))
            chain(dve.tensor_scalar(sgn[:], bv[:], 0.0, 2.0, ALU.is_ge, ALU.mult))
            for h in range(H):
                last = dve.tensor_scalar(sgn[:, h, :], sgn[:, h, :], -1.0, alpha[:, h:h + 1], ALU.add, ALU.mult)
            chain(last)
            chain(dve.tensor_tensor(sgn[:], sgn[:], bv[:], ALU.subtract))
            chain(dve.tensor_tensor(vb[:], sgn[:], bv[:], ALU.add))
            dve.wait_ge(mean_full, 1)
            chain(dve.tensor_copy(aqk[:], pq[:, 0:2 * DC:HC]))
            chain(dve.tensor_tensor(aqk[:], aqk[:], pq[:, 1:2 * DC:HC], ALU.add))
            chain(dve.tensor_scalar(sqk[:], bqk[:], 0.0, 2.0, ALU.is_ge, ALU.mult))
            by_head = lambda t: t[:].rearrange("p (h c) -> p h c", c=HC)
            both = aqk[:].rearrange("p (h a) -> p h a", a=1).broadcast_to([P, 2 * H, HC])
            chain(dve.scalar_tensor_tensor(by_head(sqk), by_head(sqk), -1.0, both, ALU.add, ALU.mult))
            chain(dve.tensor_tensor(sqk[:], sqk[:], bqk[:], ALU.subtract))
            chain(dve.tensor_tensor(sqk[:], sqk[:], bqk[:], ALU.add))
            chain(dve.tensor_tensor(qk[:], sqk[:, 0:DC], sqk[:, DC:2 * DC], ALU.mult))

            def split_base(c):
                dve.wait_ge(stage_ld[c % 2], 16 * (c // 2 + 1))
                chain(dve.tensor_copy(baseH[:, c, :], stage[:, c % 2, :]))
                dve.tensor_tensor(baseL[:, c, :], stage[:, c % 2, :], baseH[:, c, :].bitcast(F32),
                                  ALU.subtract).then_inc(stage_used, 1)

            split_base(0)
            split_base(1)
            softplus(1, h2)
            for e in range(NE):
                split_base(2 + e)
                dve.wait_ge(pos_full, 2 * e + 2)
                if e >= 2:
                    dve.wait_ge(pos_st[e % 2], 16 * (e // 2))
                dve.tensor_copy(posrow[e % 2][:, 512:D], pp[e % 2][0:CANVAS, 1, :]).then_inc(pos_ready[e % 2], 1)
            for c in range(2 + NE, DC):
                split_base(c)
            dve.wait_ge(const_ld, 16 * 7)
            chain(dve.tensor_copy(W["emap"][:], W["emap_i"][:]))
            for e in range(E0):
                last = dve.tensor_scalar(W["onehot"][:, e, :], W["emap"][:], float(e), None, ALU.is_equal)
            chain(last)
            dve.wait_ge(stage_used, DC)

        @block.tensor
        def _(pe):
            own = lambda e: slice(e * CANVAS, (e + 1) * CANVAS)
            pe.wait_ge(sin_ready, 1)
            pe.wait_ge(w_ld[0], 16)
            for e in range(NE):
                for c in range(2):
                    last = pe.matmul(ph[:, c, own(e)], w1[:, e, c * P:(c + 1) * P], ang[:, own(e)], start=True, stop=True)
            last.then_inc(h_full, 1)
            pe.wait_ge(abs_ready, 1)
            pe.wait_ge(ident_done, 4)
            pe.matmul(pq[:, 0:2 * DC], mean_w[:], sqk[:], start=True, stop=True).then_inc(mean_full, 1)
            pe.wait_ge(h_ready, 1)
            pe.wait_ge(w_ld[1], 16)
            for e in range(NE):
                for c in range(2):
                    for k in range(2):
                        last = pe.matmul(ph[:, c, own(e)], w2[:, e, k, c * P:(c + 1) * P], h1[:, k, own(e)],
                                         start=k == 0, stop=k == 1)
            last.then_inc(h_full, 1)
            pe.wait_ge(h_ready, 2)
            pe.wait_ge(in_ld, 16 * 4)
            for e in range(NE):
                pe.wait_ge(w3_ld[e], 16)
                if e >= 2:
                    pe.wait_ge(pos_ready[e % 2], 2 * (e // 2))
                for n in range(2):
                    cols = slice(n * 512, (n + 1) * 512)
                    for k in range(2):
                        pe.matmul(pp[e % 2][0:CANVAS, n, :], h2[:, k, own(e)], w3[:, e, k, cols], start=k == 0, stop=False)
                    pe.matmul(pp[e % 2][0:CANVAS, n, :], pick[:, own(e)], b3[:, cols], start=False, stop=True).then_inc(pos_full, 1)


def attend(nc, I, persist, W, scratch):
    ident, causal = persist["ident"], persist["causal"]
    with ExitStack() as ctx:
        sb = lambda n, s, d=F32: ctx.enter_context(nc.sbuf_tensor(n, s, d))
        sem = lambda n: ctx.enter_context(nc.semaphore(n))
        norm = Norm(nc, ctx, "a_")
        NORMS = 3 * TT
        emb, emb_part = W["emb"], W["emb_part"]
        x1 = sb("x1", [P, TT, D])
        xT = sb("xT", [P, DC, T])
        kT = sb("kT", [P, DC, T])
        room = nc.lookup_mloc(kT).addr
        x2HL = [nc.alloc_sbuf_tensor_at(f"x2_{k}", [P, DC, P], F32R, offset=room + k * D * 4) for k in range(4)]
        att = sb("att", [P, 2, TT, T])
        att_flat = att[:].rearrange("p a s t -> p (a s t)")
        x3 = [att_flat[:, k * D:(k + 1) * D] for k in range(2)]
        x3T = [att_flat[:, (2 + k) * D:(3 + k) * D].rearrange("p (c t) -> p c t", c=DC) for k in range(2)]
        xT_flat = xT[:].rearrange("p c t -> p (c t)")
        x2 = [xT_flat[:, k * D:(k + 1) * D] for k in range(2)]
        x2F = [xT_flat[:, (2 + k) * D:(3 + k) * D].rearrange("p (c t) -> p c t", c=DC) for k in range(2)]
        x2H, x2L = [x2HL[0][:], x2HL[2][:]], [x2HL[1][:], x2HL[3][:]]
        hres = sb("hres", [P, TT, D])
        hw, hwT = sb("hw", [P, E0 * R0]), sb("hwT", [P, P])
        lg, rep, ex, top = sb("lg", [P, NR]), sb("rep", [P, NR]), sb("ex", [P, NR]), sb("top", [P, 8])
        pr, w8 = sb("pr", [P, E0, NR]), sb("w8", [P, E0])
        nmax, esum, rinv = sb("nmax", [P, 1]), sb("esum", [P, 1]), sb("rinv", [P, 1])
        cur_emb, cur_pos = sb("cur_emb", [P, TT], I32), sb("cur_pos", [P, TT], I32)
        ps = lambda n, s: ctx.enter_context(nc.psum_tensor(n, s, F32))
        ptr = ps("ptr", [P, 2, 512])
        psc = ps("psc", [P, 2, 512])
        pout = ps("pout", [P, 2, D])
        gather_go = sem("gather_go")
        idx_ready, emb_ready, emb_used = sem("idx_ready"), sem("emb_ready"), sem("emb_used")
        x1_ready, tr_full, tr_out = sem("x1_ready"), sem("tr_full"), sem("tr_out")
        k_ready, sc_full, sc_sig, att_ready = sem("k_ready"), sem("sc_full"), sem("sc_sig"), sem("att_ready")
        out_full, out_free, x2_ready, x2L_ready = sem("out_full"), sem("out_free"), sem("x2_ready"), sem("x2L_ready")
        ra_full, ra_free, nmax_ready, ex_ready = sem("ra_full"), sem("ra_free"), sem("nmax_ready"), sem("ex_ready")
        hw_ready, x3_ready, down_full, down_out = sem("hw_ready"), sem("x3_ready"), sem("down_full"), sem("down_out")
        res_ready, res_stored, vchain, h2_done = sem("res_ready"), sem("res_stored"), sem("vchain2"), sem("h2_done")
        out_half, x2F_ready = sem("out_half"), sem("x2F_ready")
        TRN = DC + 5 * TT
        block = ctx.enter_context(nc.Block())
        raw_ra, baseH, baseL, lora_b, down = W["raw_ra"], W["baseH"], W["baseL"], W["lora_b"], W["down"]

        @block.gpsimd
        def _(pool):
            neg_half = persist["neg_half"]

            def gather_tokens():
                for t in range(TT):
                    pool.indirect_dma_start(emb[:, t, :], None, I["embed"],
                                            bass.IndirectOffsetOnAxis(ap=cur_emb[:, t:t + 1], axis=0),
                                            bounds_check=N_TOK - 1, oob_is_err=False).then_inc(emb_part, 16)

            def gather_positions(i):
                pool.wait_ge(emb_part, i * 64 + 64)
                pool.sem_inc(gather_go, 1)
                for t in range(TT):
                    pool.indirect_dma_start(emb[:, t, :], None, scratch["pos"],
                                            bass.IndirectOffsetOnAxis(ap=cur_pos[:, t:t + 1], axis=0),
                                            bounds_check=N_POS - 1, oob_is_err=False).then_inc(emb_ready, 16)

            pool.wait_ge(idx_ready, 1)
            gather_positions(0)
            for t in range(TT):
                norm.serve(pool, neg_half, t)
            with pool.Fori(0, B) as b:
                for n in range(TT, TT + 2):
                    norm.serve(pool, neg_half, b * NORMS + n)
                pool.wait_ge(emb_used, b + 1)
                pool.sem_inc(gather_go, 1)
                pool.wait_ge(idx_ready, b + 2)
                pool.sem_inc(gather_go, 1)
                gather_tokens()
                norm.serve(pool, neg_half, b * NORMS + TT + 2)
                gather_positions(b + 1)
                for n in range(TT + 3, NORMS + TT):
                    norm.serve(pool, neg_half, b * NORMS + n)

        @block.sync
        def _(sp):
            with sp.Fori(0, B) as b:
                for t in range(TT):
                    sp.wait_ge(res_ready, b * TT + t + 1)
                    sp.dma_start(scratch["res"][ds(b, 1), t, :, :].rearrange("a p d -> (a p) d"),
                                 hres[:, t, :]).then_inc(res_stored, 16)
            sp.wait_ge(res_stored, 16 * TT * B + 16)

        @block.vector
        def _(dve):
            chain = Chain(dve, vchain)

            def next_lists(i):
                dve.tensor_copy(cur_emb[:], persist["ids_emb"][:, ds(i * TT, TT)])
                dve.tensor_copy(cur_pos[:], persist["ids_pos"][:, ds(i * TT, TT)]).then_inc(idx_ready, 1)

            def norm1(i, t):
                if t == 0:
                    dve.wait_ge(emb_ready, i * 64 + 64)
                norm.rows(dve, chain, x1[:, t, :], emb[:, t, :], count()).then_inc(x1_ready, 1)

            done = [0, 0]

            def count():
                done[1] += 1
                return done[0] + done[1] - 1

            def scale_k(n0):
                for c in range(DC):
                    dve.wait_ge(tr_out, n0 + c + 3)
                    dve.tensor_scalar(kT[:, c, :], xT[:, c, :], W["qk"][:, c:c + 1], None, ALU.mult).then_inc(k_ready, 1)

            next_lists(0)
            for t in range(TT):
                norm1(0, t)
            scale_k(0)
            chain.restart()
            with dve.Fori(0, B) as b:
                done[:] = [b * NORMS + TT, 0]
                next_lists(b + 1)
                def mask(h):
                    for s in range(TT):
                        dve.wait_ge(sc_sig, b * H * TT + h * TT + s + 3)
                        diag = att[:, h % 2, s, s * P:(s + 1) * P]
                        dve.tensor_tensor(diag, diag, causal[:], ALU.mult).then_inc(att_ready, 1)

                def add_head(h):
                    cols = slice(h * HD, (h + 1) * HD)
                    dve.wait_ge(out_full, b * (H + TT) + h + 1)
                    if h == 0:
                        dve.wait_ge(res_stored, b * 64 + 16)
                    v = W["vb"][:, h:h + 1, :].broadcast_to([P, TT, HD])
                    acc = hres[:, :, cols]
                    dve.tensor_tensor(acc, pout[:, h % 2, :].rearrange("p (t d) -> p t d", t=TT), v,
                                      ALU.mult).then_inc(out_free, 1)
                    dve.wait_ge(out_free, b * (H + TT) + h + 3)
                    chain(dve.tensor_tensor(acc, acc, emb[:, :, cols], ALU.add))

                def add_half(h, half):
                    if half == 0:
                        dve.wait_ge(out_half, b * 2 + h - 1)
                    else:
                        dve.wait_ge(out_full, b * (H + TT) + h + 1)
                    ts, cols = slice(2 * half, 2 * half + 2), slice(h * HD, (h + 1) * HD)
                    acc = hres[:, ts, cols]
                    chain(dve.tensor_tensor(acc, pout[:, h % 2, half * 512:(half + 1) * 512].rearrange("p (t d) -> p t d", t=2),
                                            W["vb"][:, h:h + 1, :].broadcast_to([P, 2, HD]), ALU.mult))
                    if half == 1:
                        dve.engine_nop().then_inc(out_free, 1)
                    chain(dve.tensor_tensor(acc, acc, emb[:, ts, cols], ALU.add))
                    if half == 1 and h == H - 1:
                        dve.engine_nop().then_inc(emb_used, 1)

                mask(0)
                mask(1)
                add_head(0)
                mask(2)
                add_head(1)
                mask(3)
                add_half(2, 0)
                add_half(3, 0)

                def norm2(t):
                    norm.rows(dve, chain, x2[t % 2], hres[:, t, :], count()).then_inc(x2_ready, 1)
                    dve.tensor_tensor(hres[:, t, :], hres[:, t, :], W["base_b"][:], ALU.add).then_inc(h2_done, 1)

                def low_part(t):
                    dve.wait_ge(tr_out, b * TRN + DC + TR2[t] + 4)
                    dve.tensor_tensor(x2L[t % 2], x2F[t % 2], x2H[t % 2].bitcast(F32), ALU.subtract).then_inc(x2L_ready, 1)

                def route(t):
                    dve.wait_ge(ra_full, b * TT + t + 1)
                    chain(dve.tensor_tensor(lg[:], psc[:, 0, 0:NR], W["router_b"][:], ALU.add))
                    chain(dve.max(top[:], lg[:]))
                    dve.tensor_scalar(nmax[:], top[:, 0:1], -1.0, None, ALU.mult).then_inc(nmax_ready, 1)
                    chain(dve.match_replace(rep[:], top[:], lg[:], NEG))
                    dve.wait_ge(ex_ready, b * TT + t + 1)
                    chain(dve.scalar_tensor_tensor(rep[:], rep[:], -1e38, ex[:], ALU.is_lt, ALU.mult))
                    chain(dve.reciprocal(rinv[:], esum[:]))
                    chain(dve.tensor_tensor(pr[:], W["onehot"][:],
                                            rep[:].rearrange("p (a n) -> p a n", a=1).broadcast_to([P, E0, NR]), ALU.mult))
                    chain(dve.tensor_reduce(w8[:], pr[:], AX, ALU.add))
                    chain(dve.tensor_scalar(w8[:], w8[:], rinv[:, 0:1], 2.0, ALU.mult, ALU.mult))
                    chain(dve.tensor_tensor(hw[:].rearrange("p (e r) -> p e r", e=E0),
                                            psc[:, 0, NR + 1:RA].rearrange("p (e r) -> p e r", e=E0),
                                            w8[:].rearrange("p (e a) -> p e a", a=1).broadcast_to([P, E0, R0]), ALU.mult))
                    dve.engine_nop().then_inc(hw_ready, 1)
                    dve.engine_nop().then_inc(ra_free, 1)

                def add_ffn(t):
                    dve.wait_ge(out_full, b * (H + TT) + H + t + 1)
                    dve.wait_ge(h2_done, b * TT + t + 1)
                    dve.tensor_tensor(hres[:, t, :], hres[:, t, :], pout[:, t % 2, :], ALU.add).then_inc(out_free, 1)
                    dve.wait_ge(out_free, b * (H + TT) + H + t + 3)
                    norm.rows(dve, chain, x3[t % 2], hres[:, t, :], count()).then_inc(x3_ready, 1)
                    add_norm = norm.with_residual(dve, chain, hres[:, t, :])
                    return lambda: add_norm().then_inc(res_ready, 1)

                norm2(0)
                add_half(2, 1)
                add_norm = None
                for t in range(TT):
                    low_part(t)
                    route(t)
                    if t > 0:
                        add_norm()
                    if t < TT - 1:
                        norm2(t + 1)
                    if t == 0:
                        add_half(3, 1)
                    if t >= 2:
                        norm1(b + 1, 2 * t - 4)
                        norm1(b + 1, 2 * t - 3)
                    add_norm = add_ffn(t)
                add_norm()
                scale_k(b * TRN + DC + TR1)
                chain.restart()

        @block.scalar
        def _(act):
            act.sem_inc(tr_out, 2)
            act.sem_inc(sc_sig, 2)
            act.sem_inc(down_out, 1)
            act.sem_inc(out_free, 2)
            act.sem_inc(ra_free, 1)
            act.sem_inc(res_stored, 16)

            def take_x1(n0):
                for c in range(DC):
                    act.wait_ge(tr_full, n0 + c + 1)
                    act.activation(xT[:, c, :], ptr[:, (TR1 + c) % 2, :], ACT.Copy).then_inc(tr_out, 1)

            take_x1(0)
            with act.Fori(0, B) as b:
                for h in range(H):
                    if h >= 2:
                        act.wait_ge(out_full, b * (H + TT) + h - 1)
                    for s in range(TT):
                        k = h * TT + s
                        act.wait_ge(sc_full, b * H * TT + k + 1)
                        act.activation(att[:, h % 2, s, s * P:T], psc[:, k % 2, 0:T - s * P], ACT.Sigmoid,
                                       scale=4.0 * HD ** -0.5).then_inc(sc_sig, 1)

                def take2(t):
                    n0 = DC + TR2[t]
                    src = [ptr[:, (n0 + g) % 2, :].rearrange("p (c t) -> p c t", c=DC // 2) for g in range(2)]
                    half = [slice(g * DC // 2, (g + 1) * DC // 2) for g in range(2)]
                    for g in range(2):
                        act.wait_ge(tr_full, b * TRN + n0 + g + 1)
                        act.activation(x2F[t % 2][:, half[g], :], src[g], ACT.Copy).then_inc(x2F_ready, 1)
                    for g in range(2):
                        act.activation(x2H[t % 2][:, half[g], :], src[g], ACT.Copy).then_inc(tr_out, 1)

                def take3(t):
                    for g in range(2):
                        n = DC + TR3[t] + g
                        act.wait_ge(tr_full, b * TRN + n + 1)
                        src = ptr[:, n % 2, :].rearrange("p (c t) -> p c t", c=DC // 2)
                        act.activation(x3T[t % 2][:, g * DC // 2:(g + 1) * DC // 2, :], src, ACT.Copy).then_inc(tr_out, 1)

                take2(0)
                for t in range(TT):
                    act.wait_ge(nmax_ready, b * TT + t + 1)
                    act.activation(ex[:], lg[:], ACT.Exp, bias=nmax[:, 0:1], accum_out=esum[:, 0:1]).then_inc(ex_ready, 1)
                    if t < TT - 1:
                        take2(t + 1)
                    n = DC + TRW[t]
                    act.wait_ge(tr_full, b * TRN + n + 1)
                    act.activation(hwT[:], ptr[:, n % 2, 0:P], ACT.Copy).then_inc(tr_out, 1)
                    if t > 0:
                        take3(t - 1)
                take_x1(b * TRN + DC + TR1)
                take3(TT - 1)
                act.wait_ge(down_full, b + 1)
                act.activation(persist["xm"][:, ds(b, T, B)], psc[:, 1, :], ACT.Gelu,
                               bias=W["b_down"][:, 0:1]).then_inc(down_out, 1)

        @block.tensor
        def _(pe):
            def turn1(i, n0):
                pe.wait_ge(x1_ready, i * TT + TT)
                for c in range(DC):
                    pe.wait_ge(tr_out, n0 + c + 1)
                    for t in range(TT):
                        last = pe.transpose(ptr[:, (TR1 + c) % 2, t * P:(t + 1) * P], x1[:, t, c * P:(c + 1) * P], ident[:])
                    last.then_inc(tr_full, 1)

            turn1(0, 0)
            with pe.Fori(0, B) as b:
                def bank(n):
                    pe.wait_ge(tr_out, b * TRN + n + 1)
                    return ptr[:, n % 2, :]

                def scores(h):
                    pe.wait_ge(k_ready, b * DC + HC * (h + 1))
                    for s in range(TT):
                        k = h * TT + s
                        pe.wait_ge(sc_sig, b * H * TT + k + 1)
                        if k == 1:
                            pe.wait_ge(down_out, b + 1)
                        for c in range(HC):
                            last = pe.matmul(psc[:, k % 2, 0:T - s * P], kT[:, HC * h + c, s * P:(s + 1) * P],
                                             xT[:, HC * h + c, s * P:T], start=c == 0, stop=c == HC - 1)
                        last.then_inc(sc_full, 1)

                def attn_out(h, tiles):
                    pe.wait_ge(att_ready, b * H * TT + h * TT + tiles[-1] + 1)
                    if tiles[0] == 0:
                        pe.wait_ge(out_free, b * (H + TT) + h + 1)
                    for t in tiles:
                        for s in range(t + 1):
                            last = pe.matmul(pout[:, h % 2, t * HD:(t + 1) * HD], att[:, h % 2, s, t * P:(t + 1) * P],
                                             x1[:, s, h * HD:(h + 1) * HD], start=s == 0, stop=s == t)
                    last.then_inc(out_full if tiles[-1] == TT - 1 else out_half, 1)

                whole, first, second = range(TT), range(TT // 2), range(TT // 2, TT)
                scores(0)
                scores(1)
                attn_out(0, whole)
                scores(2)
                attn_out(1, whole)
                scores(3)
                attn_out(2, first)
                attn_out(3, first)
                attn_out(2, second)
                attn_out(3, second)

                def turn(src, n0):
                    for g in range(2):
                        dst = bank(n0 + g)
                        for k in range(DC // 2):
                            c = g * DC // 2 + k
                            last = pe.transpose(dst[:, k * P:(k + 1) * P], src[:, c * P:(c + 1) * P], ident[:])
                        last.then_inc(tr_full, 1)

                def turn2(t):
                    pe.wait_ge(x2_ready, b * TT + t + 1)
                    turn(x2[t % 2], DC + TR2[t])

                def ra(t):
                    pe.wait_ge(x2F_ready, b * 2 * TT + 2 * t + 2)
                    pe.wait_ge(ra_free, b * TT + t + 1)
                    for c in range(DC):
                        last = pe.matmul(psc[:, 0, 0:RA], x2F[t % 2][:, c, :], raw_ra[:, c, :], start=c == 0, stop=c == DC - 1)
                    last.then_inc(ra_full, 1)

                def base(t):
                    pe.wait_ge(out_free, b * (H + TT) + H + t + 1)
                    pe.wait_ge(tr_out, b * TRN + DC + TR2[t] + 4)
                    for k, (lhs, rhs) in enumerate(((x2H, baseH), (x2H, baseL), (x2L, baseH))):
                        if k == 2:
                            pe.wait_ge(x2L_ready, b * TT + t + 1)
                        for c in range(DC):
                            if k == 2 and c == DC // 2 and t < TT - 1:
                                turn2(t + 1)
                            for n in range(2):
                                pe.matmul(pout[:, t % 2, n * 512:(n + 1) * 512], lhs[t % 2][:, c, :],
                                          rhs[:, c, n * 512:(n + 1) * 512], start=k == 0 and c == 0, stop=False)

                def turn_hw(t):
                    pe.wait_ge(hw_ready, b * TT + t + 1)
                    dst = bank(DC + TRW[t])
                    pe.transpose(dst[:, 0:P], hw[:], ident[:]).then_inc(tr_full, 1)

                def lora(t):
                    pe.wait_ge(tr_out, b * TRN + DC + TRW[t] + 3)
                    for n in range(2):
                        last = pe.matmul(pout[:, t % 2, n * 512:(n + 1) * 512], hwT[:], lora_b[:, n * 512:(n + 1) * 512],
                                         start=False, stop=True)
                    last.then_inc(out_full, 1)

                def turn3(t):
                    pe.wait_ge(x3_ready, b * TT + t + 1)
                    turn(x3[t % 2], DC + TR3[t])

                def project_down(t):
                    pe.wait_ge(tr_out, b * TRN + DC + TR3[t] + 4)
                    for c in range(DC):
                        last = pe.matmul(psc[:, 1, t * P:(t + 1) * P], down[:, c, :], x3T[t % 2][:, c, :],
                                         start=c == 0, stop=c == DC - 1)
                    if t == TT - 1:
                        last.then_inc(down_full, 1)

                turn2(0)
                for t in range(TT):
                    ra(t)
                    base(t)
                    turn_hw(t)
                    if t > 0:
                        turn3(t - 1)
                    lora(t)
                    if t > 0:
                        project_down(t - 1)
                turn1(b + 1, b * TRN + DC + TR1)
                turn3(TT - 1)
                project_down(TT - 1)


def awaited(eng, sem, value):
    if not isinstance(value, int) or value > 0:
        eng.wait_ge(sem, value)


def hydra(nc, I, persist, scratch):
    ident = persist["ident"]
    with ExitStack() as ctx:
        sb = lambda n, s, d=F32: ctx.enter_context(nc.sbuf_tensor(n, s, d))
        sem = lambda n: ctx.enter_context(nc.semaphore(n))
        flow = sb("flow", [P, 3 * B * T])
        cur = [sb(f"cur{k}", [P, IC]) for k in range(2)]
        in_w = sb("in_w", [P, DIN])
        conv_in = sb("conv_in", [P, DIN])
        conv_bc = sb("conv_bc", [P, DTB, DCONV])
        conv_x, conv_bx = sb("conv_x", [P, 2, DCONV]), sb("conv_bx", [P, 2])
        bcdt_w, fcd = sb("bcdt_w", [P, BF]), sb("fcd", [P, 2, NH])
        bias = sb("bias", [P, NB])
        a_half = sb("a_half", [P, 2 * NH])
        out_w, norm_w = sb("out_w", [P, 2, DM]), sb("norm_w", [P, 2])
        ones, block_mask = sb("ones", [P, P]), sb("block_mask", [P, P])
        gate = sb("gate", [P, 3])
        zs = [sb(f"zs{k}", [P, 2, IC]) for k in range(2)]
        xs = [sb(f"xs{k}", [P, 2, IC]) for k in range(2)]
        xraw = sb("xraw", [P, 2, IC])
        before = sb("before", [P, DCONV - 1 + B, BF])
        taps = sb("taps", [P, B, DTB, DCONV])
        rows = [sb(f"rows{k}", [P, B, NB]) for k in range(2)]
        xrow = [sb(f"xrow{k}", [P, B, DIN]) for k in range(2)]
        mix = [sb(f"mix{k}", [P, B, B * NH]) for k in range(2)]
        mixT = [sb(f"mixT{k}", [P, B, B * NH]) for k in range(2)]
        diag = [sb(f"diag{k}", [P, B, NH, P]) for k in range(2)]
        fwd, bwd = sb("fwd", [P, B, B, NH]), sb("bwd", [P, B, B, NH])
        cb, cbn = sb("cb", [P, B, B]), sb("cbn", [P, B, B, DST])
        dt, u, ln1, pol, dec = (sb(n, [P, B, 2 * NH]) for n in ("dt", "u", "ln1", "pol", "dec"))
        yz, sq, sqs, rs = sb("yz", [P, 2, 512]), sb("sq", [P, 2, 512]), sb("sqs", [P, 512]), sb("rs", [P, 512])
        eps_col = sb("eps_col", [P, 1])
        ps = lambda n, s: ctx.enter_context(nc.psum_tensor(n, s, F32))
        pcv, pst = ps("pcv", [P, 2, 512]), ps("pst", [P, 2, 512])
        py, po = ps("py", [P, 2, 512]), ps("po", [P, 2, 512])
        cur_ready = sem("cur_ready")
        x_ld, out_w_ready = sem("hx_ld"), sem("out_w_ready")
        w_ld, w_ready, w_half = sem("hw_ld"), sem("hw_ready2"), sem("w_half")
        cv_full, cv_out, g_full, g_out = (sem(n) for n in ("cv_full", "cv_out", "g_full", "g_out"))
        xraw_ready, xc_ready, xs_ready = sem("xraw_ready"), sem("xc_ready"), sem("xs_ready")
        bc_conv, bc_ready = sem("bc_conv"), sem("bc_ready")
        t_full, t_out, xr_full, xr_out = sem("t_full"), sem("t_out"), sem("xr_full"), sem("xr_out")
        u_ready, ln_ready, dec_in, dec_ready = sem("u_ready"), sem("ln_ready"), sem("dec_in"), sem("dec_ready")
        mix_ready, mix_st, mix_ld = sem("mix_ready"), [sem("mix_st0"), sem("mix_st1")], [sem("mix_ld0"), sem("mix_ld1")]
        diag_ready, y_full, yz_ready, sq_ready = sem("diag_ready"), sem("y_full"), sem("yz_ready"), sem("sq_ready")
        sqs_ready, log_ready = sem("sqs_ready"), sem("log_ready")
        o_full, rs_ready, flow_ready, vchain = sem("o_full"), sem("rs_ready"), sem("flow_ready"), sem("vchain3")
        block = ctx.enter_context(nc.Block())
        NW = 11
        LAST = 2 * NITEM - 1
        SPREAD = 5

        def spread_tiles(eng, k, tiles):
            mask = block_mask[:].rearrange("p (a n) -> p a n", a=1).broadcast_to([P, NH, P])
            for n in tiles:
                src = mixT[k][:, n, :].rearrange("p (a t h) -> p h a t", a=1, h=NH).broadcast_to([P, NH, 16, B])
                last = eng.tensor_tensor(diag[k][:, n].rearrange("p h (q t) -> p h q t", t=B), src,
                                         mask.rearrange("p h (q t) -> p h q t", t=B), ALU.mult)
            return last

        def run(eng, step, restart=lambda: None):
            with eng.Fori(0, NITEM - 1) as j:
                for k in range(2):
                    step(Item(j * 2 + k, k), 2)
                restart()
            for k in range(2):
                step(Item(LAST - 1 + k, k), 1 - k)
            restart()

        @block.sync
        def _(sp):
            sp.dma_start(conv_in[:], I["in_x"]).then_inc(x_ld, 16)
            for dst, name in ((in_w[:], "in_z"), (bcdt_w[:], "in_bcdt"), (conv_bx[:], "conv_bx"),
                              (conv_x[:], "conv_x"), (norm_w[:], "hy_norm")):
                sp.dma_start(dst, I[name]).then_inc(w_ld, 16)
            sp.dma_start(bias[:], I["hy_bias"].to_broadcast([P, NB])).then_inc(w_ld, 16)
            sp.dma_start(conv_bc[:].rearrange("p c k -> p (c k)"), I["conv_bc"].to_broadcast([P, DCONV * DTB])).then_inc(w_ld, 16)
            sp.dma_start(fcd[:], I["fcd"].rearrange("(c p) n -> p c n", p=P)).then_inc(w_ld, 16)
            sp.dma_start(out_w[:], I["hy_out"].rearrange("(c p) n -> p c n", p=P)).then_inc(w_ld, 16)
            sp.dma_start(a_half[:], I["a_log"].to_broadcast([P, 2 * NH])).then_inc(w_ld, 16)
            sp.dma_start(gate[:, 0:1], I["gate1"].to_broadcast([P, 1])).then_inc(w_ld, 16)
            def bounce(i, k):
                sp.wait_ge(mix_ready, i + 1)
                sp.dma_start(scratch["mix"][ds(i * P, P), :], mix[k][:].rearrange("p s c -> p (s c)")).then_inc(mix_st[k], 16)
                sp.wait_ge(mix_st[k], (i - k) * 8 + 32)
                sp.dma_start(mixT[k][:], scratch["mix"][ds(i * P, P), :].rearrange("m (s c) -> (m s) c", s=B)
                             .rearrange("(n p) c -> p n c", p=P)).then_inc(mix_ld[k], 16)

            with sp.Fori(0, NITEM) as j:
                for k in range(2):
                    bounce(j * 2 + k, k)

        @block.gpsimd
        def _(pool):
            for k in range(2):
                pool.tensor_copy(cur[k][:], persist["xm"][:, k * IC:(k + 1) * IC]).then_inc(cur_ready, 1)
            pool.memset(ones[:], 1.0)
            pool.memset(eps_col[:], EPS)
            for m in (fwd, bwd):
                pool.memset(m[:], 0.0)
            pool.memset(block_mask[:], 1.0).then_inc(w_half, 1)
            pool.wait_ge(w_half, 1)
            m = block_mask[:].rearrange("p (r t) -> p r t", t=B)
            pool.affine_select(out=m, in_=m, compare_op=ALU.is_ge, fill=0.0, base=0,
                               pattern=[[-B, 16], [0, B]], channel_multiplier=1).then_inc(w_half, 1)
            pool.wait_ge(w_half, 2)
            pool.affine_select(out=m, in_=m, compare_op=ALU.is_ge, fill=0.0, base=B - 1,
                               pattern=[[B, 16], [0, B]], channel_multiplier=-1).then_inc(w_half, 1)
            pool.wait_ge(w_half, 3)
            for m in (fwd, bwd):
                flat = m[:].rearrange("p c s h -> p (c s) h")
                pool.memset(flat[:, 0:B * B:B + 1, :], 1.0).then_inc(w_half, 1)

            def take_item(i, k):
                pool.tensor_copy(cur[k][:], flow[:, ds(i * IC, IC)]).then_inc(cur_ready, 1)

            def spread(i, k):
                pool.wait_ge(mix_ld[k], (i - k) * 8 + 16)
                spread_tiles(pool, k, range(SPREAD)).then_inc(diag_ready, 1)

            def step(it, more):
                i, k, n = it.n, it.k, it.n + 1
                if more > 1:
                    pool.wait_ge(flow_ready, i * 2 + 1)
                    pool.wait_ge(cv_full, i * 8 + 8)
                    pool.wait_ge(t_full, i + 1)
                    take_item(i + 2, k)
                for blk in range(2):
                    pool.wait_ge(sq_ready, i * 2 + blk + 1)
                    pool.tensor_tensor(sqs[:], sq[:, 0, :], sq[:, 1, :], ALU.add).then_inc(sqs_ready, 1)
                if more:
                    spread(n, 1 - k)

            spread(0, 0)
            run(pool, step)

        @block.scalar
        def _(act):
            act.activation(flow[:, 0:B * T], persist["xm"][:], ACT.Copy).then_inc(flow_ready, 1)
            act.wait_ge(w_ld, 16 * NW)
            act.sem_inc(cv_out, 2)
            act.sem_inc(xr_out, 1)
            for k in range(2):
                act.sem_inc(mix_st[k], 16)

            def take_x(i, k, blk):
                if blk == 0:
                    awaited(act, xc_ready, i)
                for c in range(2):
                    act.wait_ge(cv_full, i * 8 + 2 * blk + c + 1)
                    cols = slice(blk * 512, (blk + 1) * 512)
                    act.activation(xraw[:, c, cols], pcv[:, c, :], ACT.Copy)
                    act.activation(xs[k][:, c, cols], pcv[:, c, :], ACT.Copy, scale=conv_x[:, c, DCONV - 1:DCONV]).then_inc(cv_out, 1)
                if blk == 1:
                    act.wait_ge(cv_out, i * 8 + 4 + 2)
                    act.sem_inc(xraw_ready, 1)

            def silu_x(i, k):
                act.wait_ge(xc_ready, i + 1)
                for c in range(2):
                    act.activation(xs[k][:, c, :], xs[k][:, c, :], ACT.Silu, bias=conv_bx[:, c:c + 1]).then_inc(xs_ready, 1)

            def take_z(i, k, blk):
                for c in range(2):
                    act.wait_ge(cv_full, i * 8 + 4 + 2 * blk + c + 1)
                    act.activation(zs[k][:, c, blk * 512:(blk + 1) * 512], pcv[:, c, :], ACT.Silu).then_inc(cv_out, 1)

            def take_rows(i):
                act.wait_ge(t_full, i + 1)
                act.activation(before[:, DCONV - 1:, :], pst[:, 0, 0:B * BF].rearrange("p (s n) -> p s n", s=B), ACT.Copy).then_inc(t_out, 1)

            def silu_rows(i, k):
                act.wait_ge(bc_conv, i + 1)
                act.activation(rows[k][:, :, 0:DTB], rows[k][:, :, 0:DTB], ACT.Silu).then_inc(bc_ready, 1)

            def take_gates(i, k):
                act.wait_ge(g_full, i + 1)
                act.activation(rows[k][:, :, BF:NB], pst[:, 1, 0:B * NH].rearrange("p (s n) -> p s n", s=B), ACT.Copy).then_inc(g_out, 1)

            def take_xrows(i, k, half):
                for n in (2 * half, 2 * half + 1):
                    act.wait_ge(xr_full, i * 4 + n + 1)
                    act.activation(xrow[k][:, 2 * n:2 * n + 2, :],
                                   pst[:, n % 2, :].rearrange("p (a c) -> p a c", a=2), ACT.Copy).then_inc(xr_out, 1)

            def square(i, blk):
                act.wait_ge(yz_ready, i * 2 + blk + 1)
                act.activation(sq[:], yz[:], ACT.Square).then_inc(sq_ready, 1)

            def root(i, blk):
                act.wait_ge(o_full, i * 2 + blk + 1)
                act.activation(rs[:], po[:, 1, :], ACT.Ln, bias=eps_col[:, 0:1], scale=1.0 / DIN).then_inc(log_ready, 1)
                act.wait_ge(log_ready, i * 2 + blk + 1)
                act.activation(rs[:], rs[:], ACT.Exp, scale=-0.5).then_inc(rs_ready, 1)

            def soft(i):
                act.wait_ge(u_ready, i + 1)
                act.activation(u[:], u[:], ACT.Exp).then_inc(ln_ready, 1)
                act.wait_ge(ln_ready, i * 2 + 1)
                act.activation(ln1[:], u[:], ACT.Ln, bias=1.0).then_inc(ln_ready, 1)

            def decays(i):
                act.wait_ge(dec_in, i + 1)
                act.activation(dec[:], dec[:], ACT.Exp, scale=-1.0).then_inc(dec_ready, 1)

            def step(it, more):
                i, k, n = it.n, it.k, it.n + 1
                if more:
                    for blk in range(2):
                        take_z(n, 1 - k, blk)
                    silu_x(n, 1 - k)
                    silu_rows(n, 1 - k)
                    soft(n)
                for blk in range(2):
                    square(i, blk)
                    if more > 1:
                        take_x(i + 2, k, blk)
                    if more and blk == 1:
                        take_gates(n, 1 - k)
                        take_xrows(n, 1 - k, 0)
                    root(i, blk)
                    if more:
                        if blk == 0:
                            decays(n)
                        else:
                            take_xrows(n, 1 - k, 1)
                if more > 1:
                    take_rows(i + 2)

            for blk in range(2):
                take_x(0, 0, blk)
            take_rows(0)
            for blk in range(2):
                take_z(0, 0, blk)
            silu_x(0, 0)
            for blk in range(2):
                take_x(1, 1, blk)
            silu_rows(0, 0)
            take_gates(0, 0)
            act.wait_ge(w_ready, 1)
            act.activation(a_half[:], a_half[:], ACT.Exp, scale=0.5).then_inc(w_ready, 1)
            soft(0)
            decays(0)
            for half in range(2):
                take_xrows(0, 0, half)
            take_rows(1)
            act.activation(gate[:, 1:2], gate[:, 0:1], ACT.Sigmoid).then_inc(w_ready, 1)
            act.wait_ge(w_ready, 3)
            act.activation(gate[:, 0:1], gate[:, 1:2], ACT.Copy, bias=1.0).then_inc(w_ready, 1)
            act.activation(gate[:, 2:3], gate[:, 1:2], ACT.Copy, bias=1.0, scale=-1.0).then_inc(w_ready, 1)
            act.wait_ge(w_ready, 5)
            act.wait_ge(cur_ready, 2)
            act.activation(persist["xm"][:], persist["xm"][:], ACT.Copy, scale=gate[:, 0:1]).then_inc(w_ready, 1)
            run(act, step)

        @block.vector
        def _(dve):
            chain = Chain(dve, vchain)
            dve.wait_ge(w_ld, 16 * NW)
            dve.tensor_scalar(a_half[:], a_half[:], 88.0, None, ALU.min).then_inc(w_ready, 1)
            dve.memset(before[:, 0:DCONV - 1, :], 0.0)
            for c in range(2):
                last = dve.tensor_scalar(out_w[:, c, :], out_w[:, c, :], norm_w[:, c:c + 1], None, ALU.mult)
            last.then_inc(out_w_ready, 1)
            dve.wait_ge(w_half, 5)
            chain.restart()
            def raw_dt(k):
                return rows[k][:, :, DTB:DTB + 2 * NH]

            def convolve_rows(i, k):
                dve.wait_ge(t_out, i + 1)
                windows = bass.AP(before, 0, [list(before[:].ap[0]), [BF, B], [1, DTB], [BF, DCONV]])
                w = conv_bc[:].rearrange("p (a c) k -> p a c k", a=1).broadcast_to([P, B, DTB, DCONV])
                chain(dve.tensor_tensor(taps[:], windows, w, ALU.mult))
                bc = rows[k][:, :, 0:DTB]
                chain(dve.tensor_reduce(bc, taps[:], AX, ALU.add))
                over = lambda a, b: bias[:, a:b].rearrange("p (a c) -> p a c", a=1).broadcast_to([P, B, b - a])
                dve.tensor_tensor(bc, bc, over(0, DTB), ALU.add).then_inc(bc_conv, 1)
                chain(dve.tensor_tensor(raw_dt(k), before[:, DCONV - 1:, DTB:BF], over(DTB, BF), ALU.add))
                raw = raw_dt(k)
                dve.scalar_tensor_tensor(u[:], raw, -1.0, raw, ALU.mult, ALU.min).then_inc(u_ready, 1)

            def pairs(i, k):
                r = rows[k]
                dve.wait_ge(bc_ready, i + 1)
                cc = r[:, :, DST:2 * DST].rearrange("p c (a n) -> p c a n", a=1).broadcast_to([P, B, B, DST])
                bb = r[:, :, 0:DST].rearrange("p (a s) n -> p a s n", a=1).broadcast_to([P, B, B, DST])
                chain(dve.tensor_tensor(cbn[:], cc, bb, ALU.mult))
                chain(dve.tensor_reduce(cb[:], cbn[:], AX, ALU.add))

            def softplus(i, k):
                raw = raw_dt(k)
                dve.wait_ge(ln_ready, i * 2 + 2)
                chain(dve.tensor_scalar(pol[:], u[:], -1.0 / 6, None, ALU.mult))
                for coef in (1.0 / 5, -1.0 / 4, 1.0 / 3, -1.0 / 2, 1.0):
                    chain(dve.scalar_tensor_tensor(pol[:], pol[:], coef, u[:], ALU.add, ALU.mult))
                chain(dve.tensor_tensor(pol[:], pol[:], ln1[:], ALU.subtract))
                chain(dve.scalar_tensor_tensor(pol[:], u[:], 0.0625, pol[:], ALU.is_lt, ALU.mult))
                chain(dve.tensor_tensor(pol[:], pol[:], ln1[:], ALU.add))
                chain(dve.scalar_tensor_tensor(dt[:], raw, 0.0, pol[:], ALU.max, ALU.add))

                ah = a_half[:].rearrange("p (a h) -> p a h", a=1).broadcast_to([P, B, 2 * NH])
                chain(dve.tensor_tensor(dec[:], dt[:], ah, ALU.mult))
                chain(dve.scalar_tensor_tensor(dec[:], dec[:], 1e18, ah, ALU.min, ALU.mult))
                dve.tensor_scalar(dec[:], dec[:], 200.0, None, ALU.min).then_inc(dec_in, 1)

            def decay_products(i):
                dve.wait_ge(dec_ready, i + 1)
                for c in range(1, B - 1):
                    a = dec[:, c:c + 1, 0:NH].broadcast_to([P, c, NH])
                    dve.tensor_tensor(fwd[:, c, 0:c, :], fwd[:, c - 1, 0:c, :], a, ALU.mult)
                    d = B - 1 - c
                    a = dec[:, d:d + 1, NH:2 * NH].broadcast_to([P, c, NH])
                    chain(dve.tensor_tensor(bwd[:, d, d + 1:B, :], bwd[:, d + 1, d + 1:B, :], a, ALU.mult))

            def mixing(i, k):
                r = rows[k]
                w = mix[k][:].rearrange("p s (t h) -> p t s h", h=NH)
                flat = mix[k][:].rearrange("p s (t h) -> p (s t) h", h=NH)
                scale = cbn[:].rearrange("p c s (a h) -> p c s a h", h=NH)[:, :, :, 0, :]
                scale2 = cbn[:].rearrange("p c s (a h) -> p c s a h", h=NH)[:, :, :, 1, :]
                cb4 = cb[:].rearrange("p c (s a) -> p c s a", a=1).broadcast_to([P, B, B, NH])
                for dst, src, off in ((scale, fwd, 0), (scale2, bwd, NH)):
                    d4 = dt[:, :, off:off + NH].rearrange("p (a s) h -> p a s h", a=1).broadcast_to([P, B, B, NH])
                    chain(dve.tensor_tensor(dst, src[:], d4, ALU.mult))
                    chain(dve.tensor_tensor(dst, dst, cb4, ALU.mult))
                dve.wait_ge(mix_st[k], (i - k) * 8 + 16)
                chain(dve.tensor_copy(w[:, 1:B], scale[:, 0:B - 1]))
                chain(dve.memset(w[:, 0:1], 0.0))
                chain(dve.tensor_tensor(w[:, 0:B - 1], w[:, 0:B - 1], scale2[:, 1:B], ALU.add))
                dve.wait_ge(g_out, i + 1)
                dve.tensor_tensor(flat[:, 0:B * B:B + 1, :], r[:, :, BF:NB], bias[:, BF:NB].rearrange("p (a h) -> p a h", a=1)
                                  .broadcast_to([P, B, NH]), ALU.add).then_inc(mix_ready, 1)

            def spread(i, k):
                dve.wait_ge(mix_ld[k], (i - k) * 8 + 16)
                spread_tiles(dve, k, range(SPREAD, B)).then_inc(diag_ready, 1)

            def convolve(i, k):
                dve.wait_ge(xraw_ready, i + 1)
                for d in range(1, DCONV):
                    for c in range(2):
                        acc = xs[k][:, c, :].rearrange("p (q s) -> p q s", s=B)[:, :, d:B]
                        src = xraw[:, c, :].rearrange("p (q s) -> p q s", s=B)[:, :, 0:B - d]
                        tap = conv_x[:, c, DCONV - 1 - d:DCONV - d]
                        last = dve.scalar_tensor_tensor(acc, src, tap, acc, ALU.mult, ALU.add)
                    chain(last)
                dve.engine_nop().then_inc(xc_ready, 1)

            def gated(i, k, blk):
                dve.wait_ge(y_full, i * 2 + blk + 1)
                cols = slice(blk * 512, (blk + 1) * 512)
                dve.tensor_tensor(yz[:], py[:], zs[k][:, :, cols], ALU.mult).then_inc(yz_ready, 1)

            def finish(i, blk):
                dve.wait_ge(rs_ready, i * 2 + blk + 1)
                at = (i + NITEM) * IC + blk * 512
                dve.tensor_tensor(flow[:, ds(at, 512)], po[:, 0, :], rs[:], ALU.mult).then_inc(flow_ready, 1)

            def combine(first, end=NITEM):
                dve.wait_ge(w_ready, 6)
                dve.wait_ge(flow_ready, 1 + 2 * (NITEM + end))
                cols = slice(first * IC, end * IC)
                xm = persist["xm"][:, cols]
                chain(dve.scalar_tensor_tensor(xm, flow[:, 2 * B * T:][:, cols], gate[:, 2:3], xm, ALU.mult, ALU.add))

            def step(it, more):
                i, k, n = it.n, it.k, it.n + 1
                if more:
                    pairs(n, 1 - k)
                else:
                    combine(0, NITEM - 1)
                gated(i, k, 0)
                if more:
                    softplus(n, 1 - k)
                finish(i, 0)
                gated(i, k, 1)
                if more:
                    decay_products(n)
                    mixing(n, 1 - k)
                if more > 1:
                    convolve(i + 2, k)
                finish(i, 1)
                if more > 1:
                    convolve_rows(i + 2, k)
                if more:
                    spread(n, 1 - k)

            convolve(0, 0)
            convolve_rows(0, 0)
            pairs(0, 0)
            dve.wait_ge(w_ready, 2)
            softplus(0, 0)
            decay_products(0)
            mixing(0, 0)
            convolve(1, 1)
            convolve_rows(1, 1)
            spread(0, 0)
            chain.restart()
            run(dve, step, chain.restart)
            combine(NITEM - 1)

        @block.tensor
        def _(pe):

            def block_of(k, blk):
                return cur[k][:, blk * 512:(blk + 1) * 512]

            def project_x(i, k, blk):
                pe.wait_ge(cur_ready, i + 1)
                for c in range(2):
                    pe.wait_ge(cv_out, i * 8 + 2 * blk + c + 1)
                    pe.matmul(pcv[:, c, :], conv_in[:, c * P:(c + 1) * P], block_of(k, blk), start=True, stop=True).then_inc(cv_full, 1)

            def project_z(i, k, blk):
                for c in range(2):
                    pe.wait_ge(cv_out, i * 8 + 4 + 2 * blk + c + 1)
                    pe.matmul(pcv[:, c, :], in_w[:, c * P:(c + 1) * P], block_of(k, blk), start=True, stop=True).then_inc(cv_full, 1)

            def project_rows(i, k):
                pe.wait_ge(xr_out, i * 4 + 1)
                at_step = cur[k][:].rearrange("p (q s) -> p s q", s=B)
                for s in range(B):
                    last = pe.matmul(pst[:, 0, s * BF:(s + 1) * BF], at_step[:, s, :], bcdt_w[:], start=True, stop=True)
                last.then_inc(t_full, 1)

            def project_gates(i, k):
                pe.wait_ge(xs_ready, i * 2 + 2)
                for s in range(B):
                    dst = pst[:, 1, s * NH:(s + 1) * NH]
                    for c in range(2):
                        last = pe.matmul(dst, xs[k][:, c, :].rearrange("p (q s) -> p s q", s=B)[:, s, :], fcd[:, c, :],
                                         start=c == 0, stop=c == 1)
                last.then_inc(g_full, 1)

            def turn_x(i, k, half):
                for n in (2 * half, 2 * half + 1):
                    if n == 0:
                        pe.wait_ge(t_out, i + 1)
                    elif n == 1:
                        pe.wait_ge(g_out, i + 1)
                    else:
                        pe.wait_ge(xr_out, i * 4 + n)
                    for a in range(2):
                        for c in range(2):
                            t = 2 * n + a
                            last = pe.transpose(pst[:, n % 2, (2 * a + c) * P:(2 * a + c + 1) * P],
                                                xs[k][:, c, t * P:(t + 1) * P], ident[:])
                    last.then_inc(xr_full, 1)

            def apply(i, k, blk):
                for n in range(4):
                    t = 4 * blk + n
                    for h in range(NH):
                        q = HDIM * (h % 2)
                        last = pe.matmul(py[q:q + HDIM, h // 2, n * P:(n + 1) * P],
                                         xrow[k][:, t, h * HDIM:(h + 1) * HDIM], diag[k][:, t, h, :],
                                         start=True, stop=True)
                last.then_inc(y_full, 1)

            def project_out(i, blk):
                pe.wait_ge(yz_ready, i * 2 + blk + 1)
                for c in range(2):
                    pe.matmul(po[:, 0, :], out_w[:, c, :], yz[:, c, :], start=c == 0, stop=c == 1)
                pe.wait_ge(sqs_ready, i * 2 + blk + 1)
                pe.matmul(po[:, 1, :], ones[:], sqs[:], start=True, stop=True).then_inc(o_full, 1)

            def step(it, more):
                i, k, n = it.n, it.k, it.n + 1
                if more:
                    for blk in range(2):
                        project_z(n, 1 - k, blk)
                pe.wait_ge(diag_ready, i * 2 + 2)
                pe.wait_ge(xr_out, i * 4 + 5)
                for blk in range(2):
                    apply(i, k, blk)
                    if more > 1:
                        project_x(i + 2, k, blk)
                    if more and blk == 1:
                        project_gates(n, 1 - k)
                        turn_x(n, 1 - k, 0)
                    pe.wait_ge(flow_ready, i * 2 + blk + 1)
                    project_out(i, blk)
                if more:
                    turn_x(n, 1 - k, 1)
                if more > 1:
                    project_rows(i + 2, k)

            pe.wait_ge(x_ld, 16)
            for blk in range(2):
                project_x(0, 0, blk)
            pe.wait_ge(w_ld, 16 * NW)
            project_rows(0, 0)
            for blk in range(2):
                project_z(0, 0, blk)
            for blk in range(2):
                project_x(1, 1, blk)
            project_gates(0, 0)
            for half in range(2):
                turn_x(0, 0, half)
            project_rows(1, 1)
            pe.wait_ge(w_half, 5)
            pe.wait_ge(out_w_ready, 1)
            run(pe, step)


class Item:

    def __init__(self, n, k):
        self.n, self.k = n, k


class Tile:

    def __init__(self, i, k):
        self.i, self.k = (i + k // TT, k % TT) if k // TT else (i, k)
        self.n = self.i * TT + self.k
        self.exists = not isinstance(self.n, int) or 0 <= self.n < B * TT

    def after(self, d):
        return Tile(self.i, self.k + d)


def experts(nc, I, persist, scratch, out):
    ident, neg_half, xm = persist["ident"], persist["neg_half"], persist["xm"]
    KR = KE * RANK
    with ExitStack() as ctx:
        sb = lambda n, s, d=F32: ctx.enter_context(nc.sbuf_tensor(n, s, d))
        sem = lambda n: ctx.enter_context(nc.semaphore(n))
        norm = Norm(nc, ctx, "e_")
        aH, aL = sb("aH", [P, DC, KR], F32R), sb("aL", [P, DC, KR], F32R)
        bH, bL = sb("bH", [P, DC, D], F32R), sb("bL", [P, DC, D], F32R)
        wr, up, b_up = sb("wr", [P, DC, KE]), sb("up", [P, D]), sb("b_up", [P, D])
        h = sb("h", [P, TT, D])
        x5, hg = sb("x5", [P, D]), sb("hg", [P, KR])
        xF, xH, xL = sb("xF", [P, DC, P]), sb("xH", [P, DC, P], F32R), sb("xL", [P, DC, P], F32R)
        gH, gL = sb("gH", [P, DC, P], F32R), sb("gL", [P, DC, P], F32R)
        mid = sb("mid", [P, 2, P])
        sc = sb("sc5", [P, KE])
        top, rep, rep2, ex, gt = sb("top5", [P, 16]), sb("rep5", [P, KE]), sb("rep6", [P, KE]), sb("ex5", [P, KE]), sb("gt", [P, KE])
        nmax, gsum, ginv = sb("nmax5", [P, 1]), sb("gsum", [P, 1]), sb("ginv", [P, 1])
        ps = lambda n, s: ctx.enter_context(nc.psum_tensor(n, s, F32))
        ptr, pup, psc, pa, po = ps("ptr5", [P, 2, 512]), ps("pup", [P, 512]), ps("psc5", [P, 512]), ps("pa", [P, 2, 512]), ps("po5", [P, 2, 512])
        up_ld, b_up_ld, wr_ld = sem("up_ld"), sem("b_up_ld"), sem("wr_ld")
        raw_ld, split_done, high_done = [sem(f"raw_ld{k}") for k in range(DC)], sem("split_done"), sem("high_done")
        res_ld, out_st = [sem(f"res_ld{k}") for k in range(TT)], [sem(f"out_st{k}") for k in range(TT)]
        bias_ready, mid_ready, up_full, up_added = sem("bias_ready"), sem("mid_ready"), sem("up_full"), sem("up_added")
        x5_ready, t5_full, t5_out, xL_ready = sem("x5_ready"), sem("t5_full"), sem("t5_out"), sem("xL_ready")
        xF_ready = sem("xF_ready")
        sc_full, sc_used, nmax_ready, ex_ready = sem("sc_full5"), sem("sc_used"), sem("nmax5_ready"), sem("ex5_ready")
        a_full, hg_ready, t6_full, t6_high, t6_low = (sem(n) for n in ("a_full", "hg_ready", "t6_full", "t6_high", "t6_low"))
        store_go = sem("store_go")
        b_full, out_ready, vchain = sem("b_full"), sem("out_ready"), sem("vchain4")
        block = ctx.enter_context(nc.Block())
        GROUPS = B

        def run(eng, step, weights, restart=lambda: None):
            weights(0)
            step(Tile(0, -1))
            weights(1)
            step(Tile(0, 0))
            weights(2)
            for k in range(1, TT):
                step(Tile(0, k))
            restart()
            with eng.Fori(1, GROUPS - 1) as i:
                for k in range(TT):
                    step(Tile(i, k))
                restart()
            for k in range(TT + 1):
                step(Tile(GROUPS - 1, k))
            restart()

        raw_at = lambda n, t: nc.alloc_sbuf_tensor_at(n, [P, DC, D], F32, offset=nc.lookup_mloc(t).addr)
        a_raw, b_raw = raw_at("a_raw", aL), raw_at("b_raw", bL)
        chunks = [(a_raw, aH, aL, c) for c in range(DC)] + [(b_raw, bH, bL, c) for c in range(DC)]
        part = lambda n: ((0, 2), (2, 2 * DC), (0, 0))[n]

        @block.sync
        def _(sp):
            def load(t):
                if t.exists:
                    awaited(sp, out_st[t.k], 16 * t.i)
                    sp.dma_start(h[:, t.k, :], scratch["res"][at(t.i), t.k, :, :].rearrange("a p d -> (a p) d")).then_inc(res_ld[t.k], 16)

            def step(t):
                if t.after(-1).exists:
                    last = t.after(-1)
                    sp.wait_ge(out_ready, last.n + 1)
                    sp.sem_inc(store_go, 1)
                    sp.dma_start(out[at(last.i), last.k * P:(last.k + 1) * P, :].rearrange("a p d -> (a p) d"),
                                 h[:, last.k, :]).then_inc(out_st[last.k], 16)
                load(t.after(3))

            load(Tile(0, 0))
            for n in range(0, 2 * DC, 2):
                if n == 2:
                    load(Tile(0, 1))
                raw, _, _, c = chunks[n]
                src = I["ea_w" if n < DC else "eb_w"][c * P:(c + 2) * P, :]
                sp.dma_start(raw[:, c:c + 2, :], src.rearrange("(c p) n -> p c n", p=P)).then_inc(raw_ld[n // 2], 16)
            run(sp, step, lambda n: None)
            for k in range(TT):
                sp.wait_ge(out_st[k], 16 * B)

        @block.gpsimd
        def _(pool):
            def bias(t):
                if t.exists:
                    pool.wait_ge(res_ld[t.k], 16 * t.i + 16)
                    pool.tensor_tensor(h[:, t.k, :], h[:, t.k, :], b_up[:], ALU.add).then_inc(bias_ready, 1)

            def step(t):
                if t.after(1).exists:
                    norm.serve(pool, neg_half, t.after(1).n)
                bias(t.after(2))

            pool.wait_ge(b_up_ld, 16)
            bias(Tile(0, 0))
            run(pool, step, lambda n: None)

        @block.scalar
        def _(act):
            act.dma_start(up[:], I["w_up"]).then_inc(up_ld, 16)
            act.dma_start(b_up[:], I["b_up"].to_broadcast([P, D])).then_inc(b_up_ld, 16)
            act.dma_start(wr[:], I["wr"].rearrange("(c p) n -> p c n", p=P)).then_inc(wr_ld, 16)

            def weights(part_n):
                for n in range(*part(part_n)):
                    raw, high, _, c = chunks[n]
                    act.wait_ge(raw_ld[n // 2], 16)
                    act.activation(high[:, c, :], raw[:, c, :], ACT.Copy).then_inc(high_done, 1)

            def take_mid(t):
                if t.exists:
                    awaited(act, up_full, 2 * t.n - 2)
                    act.activation(mid[:, t.k % 2, :], xm[:, ds(t.i + t.k * P * B, P, B)], ACT.Copy).then_inc(mid_ready, 1)

            def step(t):
                if t.after(-1).exists:
                    last = t.after(-1)
                    for g in range(2):
                        act.wait_ge(t6_full, 2 * last.n + g + 1)
                        act.activation(gH[:, 4 * g:4 * g + 4, :], ptr[:, g, :].rearrange("p (c t) -> p c t", c=4), ACT.Copy).then_inc(t6_high, 1)
                if t.exists:
                    act.wait_ge(nmax_ready, t.n + 1)
                    act.activation(ex[:], sc[:], ACT.Exp, bias=nmax[:, 0:1]).then_inc(ex_ready, 1)
                take_mid(t.after(2))
                if t.after(1).exists:
                    nxt = t.after(1)
                    src = [ptr[:, g, :].rearrange("p (c t) -> p c t", c=4) for g in range(2)]
                    for g in range(2):
                        act.wait_ge(t5_full, 2 * nxt.n + g + 1)
                        act.activation(xF[:, 4 * g:4 * g + 4, :], src[g], ACT.Copy).then_inc(xF_ready, 1)
                    for g in range(2):
                        act.activation(xH[:, 4 * g:4 * g + 4, :], src[g], ACT.Copy).then_inc(t5_out, 1)

            take_mid(Tile(0, 0))
            run(act, step, weights)

        @block.vector
        def _(dve):
            chain = Chain(dve, vchain)

            def weights(part_n):
                for n in range(*part(part_n)):
                    raw, high, low, c = chunks[n]
                    dve.wait_ge(high_done, n + 1)
                    dve.tensor_tensor(low[:, c, :], raw[:, c, :], high[:, c, :].bitcast(F32), ALU.subtract).then_inc(split_done, 1)

            def add_up(t, n):
                if t.exists:
                    if n == 0:
                        dve.wait_ge(bias_ready, t.n + 1)
                    dve.wait_ge(up_full, 2 * t.n + n + 1)
                    half = h[:, t.k, n * 512:(n + 1) * 512]
                    dve.tensor_tensor(half, half, pup[:], ALU.add).then_inc(up_added, 1)

            def gates(t):
                dve.wait_ge(sc_full, t.n + 1)
                chain(dve.tensor_copy(sc[:], psc[:, 0:KE]))
                dve.engine_nop().then_inc(sc_used, 1)
                chain(dve.max(top[:, 0:8], sc[:]))
                dve.tensor_scalar(nmax[:], top[:, 0:1], -1.0, None, ALU.mult).then_inc(nmax_ready, 1)
                chain(dve.match_replace(rep[:], top[:, 0:8], sc[:], NEG))
                chain(dve.max(top[:, 8:16], rep[:]))
                chain(dve.match_replace(rep2[:], top[:, 8:16], rep[:], NEG))
                dve.wait_ge(ex_ready, t.n + 1)
                chain(dve.scalar_tensor_tensor(gt[:], rep2[:], -1e38, ex[:], ALU.is_lt, ALU.mult))
                chain(dve.tensor_reduce(gsum[:], gt[:], AX, ALU.add))
                chain(dve.reciprocal(ginv[:], gsum[:]))
                chain(dve.tensor_scalar(gt[:], gt[:], ginv[:, 0:1], 2.0, ALU.mult, ALU.mult))

            def weigh(t):
                dve.wait_ge(a_full, t.n + 1)
                awaited(dve, t6_full, 2 * t.n)
                g4 = gt[:].rearrange("p (a k) -> p a k", a=1).broadcast_to([P, RANK // 2, KE])
                for n in range(2):
                    last = dve.tensor_tensor(hg[:, n * 512:(n + 1) * 512].rearrange("p (r k) -> p r k", k=KE),
                                             pa[:, n, :].rearrange("p (r k) -> p r k", k=KE), g4, ALU.mult)
                last.then_inc(hg_ready, 1)

            def step(t):
                nxt, last = t.after(1), t.after(-1)
                if nxt.exists:
                    dve.wait_ge(up_added, 2 * nxt.n + 2)
                    awaited(dve, t5_full, 2 * nxt.n)
                    norm.rows(dve, chain, x5[:], h[:, nxt.k, :], nxt.n).then_inc(x5_ready, 1)
                if last.exists:
                    for g in range(2):
                        dve.wait_ge(t6_high, 2 * last.n + g + 1)
                        dve.tensor_tensor(gL[:, 4 * g:4 * g + 4, :], ptr[:, g, :].rearrange("p (c t) -> p c t", c=4),
                                          gH[:, 4 * g:4 * g + 4, :].bitcast(F32), ALU.subtract).then_inc(t6_low, 1)
                if t.exists:
                    gates(t)
                    weigh(t)
                add_up(t.after(2), 0)
                if nxt.exists:
                    dve.wait_ge(t5_out, 2 * nxt.n + 2)
                    dve.tensor_tensor(xL[:], xF[:], xH[:].bitcast(F32), ALU.subtract).then_inc(xL_ready, 1)
                add_up(t.after(2), 1)
                if last.exists:
                    dve.wait_ge(b_full, last.n + 1)
                    dve.tensor_tensor(h[:, last.k, :], h[:, last.k, :], po[:].rearrange("p a n -> p (a n)"), ALU.add).then_inc(out_ready, 1)

            for n in range(2):
                add_up(Tile(0, 0), n)
            run(dve, step, weights, chain.restart)

        @block.tensor
        def _(pe):
            def weights(part_n):
                if part_n == 0:
                    pe.wait_ge(wr_ld, 16)
                else:
                    pe.wait_ge(split_done, DC * part_n)

            def project_up(t, n):
                if t.exists:
                    pe.wait_ge(mid_ready, t.n + 1)
                    awaited(pe, up_added, 2 * t.n + n)
                    pe.matmul(pup[:], mid[:, t.k % 2, :], up[:, n * 512:(n + 1) * 512], start=True, stop=True).then_inc(up_full, 1)

            def products(dst, high, low, wH, wL, low_ready):
                for k, (lhs, rhs) in enumerate(((high, wH), (high, wL), (low, wH))):
                    if k == 2:
                        low_ready()
                    for c in range(DC):
                        for n in range(2):
                            last = pe.matmul(dst[:, n, :], lhs[:, c, :], rhs[:, c, n * 512:(n + 1) * 512],
                                             start=k == 0 and c == 0, stop=k == 2 and c == DC - 1)
                return last

            def turn(src, g):
                for c in range(4):
                    k = 4 * g + c
                    last = pe.transpose(ptr[:, g, c * P:(c + 1) * P], src[:, k * P:(k + 1) * P], ident[:])
                return last

            def step(t):
                nxt, last = t.after(1), t.after(-1)
                if t.exists:
                    pe.wait_ge(t5_out, 2 * t.n + 2)
                    awaited(pe, hg_ready, t.n)
                    products(pa, xH, xL, aH, aL, lambda: pe.wait_ge(xL_ready, t.n + 1)).then_inc(a_full, 1)
                if nxt.exists:
                    pe.wait_ge(x5_ready, nxt.n + 1)
                    for g in range(2):
                        awaited(pe, t6_low, 2 * nxt.n - 3 + g)
                        turn(x5, g).then_inc(t5_full, 1)
                project_up(t.after(2), 0)
                if nxt.exists:
                    pe.wait_ge(xF_ready, 2 * nxt.n + 2)
                    awaited(pe, sc_used, nxt.n)
                    for c in range(DC):
                        s = pe.matmul(psc[:, 0:KE], xF[:, c, :], wr[:, c, :], start=c == 0, stop=c == DC - 1)
                    s.then_inc(sc_full, 1)
                project_up(t.after(2), 1)
                if last.exists:
                    pe.wait_ge(t6_high, 2 * last.n + 2)
                    awaited(pe, out_ready, last.n)
                    products(po, gH, gL, bH, bL, lambda: pe.wait_ge(t6_low, 2 * last.n + 2)).then_inc(b_full, 1)
                if t.exists:
                    pe.wait_ge(hg_ready, t.n + 1)
                    for g in range(2):
                        pe.wait_ge(t5_out, 2 * nxt.n + g + 1) if nxt.exists else None
                        turn(hg, g).then_inc(t6_full, 1)

            pe.wait_ge(up_ld, 16)
            for n in range(2):
                project_up(Tile(0, 0), n)
            run(pe, step, weights)


def at(i):
    return slice(i, i + 1) if isinstance(i, int) else ds(i, 1)


def program(nc, I, out):
    with ExitStack() as ctx:
        sb = lambda n, s, d=F32: ctx.enter_context(nc.sbuf_tensor(n, s, d))
        persist = {"ident": sb("ident", [P, P]), "causal": sb("causal", [P, P]), "xm": sb("xm", [P, T * B]), "neg_half": sb("neg_half", [P, 1]),
                   "ids_emb": sb("ids_emb", [P, (B + 1) * TT], I32), "ids_pos": sb("ids_pos", [P, (B + 1) * TT], I32)}
        scratch = {"pos": nc.dram_tensor("pos_rows", [N_POS, D], F32).ap(),
                   "res": nc.dram_tensor("residual", [B, TT, P, D], F32).ap(),
                   "mix": nc.dram_tensor("mixing", [2 * T, B * B * NH], F32).ap()}
        with ExitStack() as wctx:
            wb = lambda n, s, d=F32: wctx.enter_context(nc.sbuf_tensor(n, s, d))
            W = {"baseH": wb("baseH", [P, DC, D], F32R), "baseL": wb("baseL", [P, DC, D], F32R),
                 "raw_ra": wb("raw_ra", [P, DC, RA]), "lora_b": wb("lora_b", [P, D]), "down": wb("down", [P, DC, DM]),
                 "b_down": wb("b_down", [P, 1]), "base_b": wb("base_b", [P, D]), "router_b": wb("router_b", [P, NR]),
                 "emap_i": wb("emap_i", [P, NR], I32), "emap": wb("emap", [P, NR]), "onehot": wb("onehot", [P, E0, NR]),
                 "qk": wb("qk", [P, DC]), "vb": wb("vb", [P, H, HD]),
                 "emb": wb("emb", [P, TT, D]), "emb_part": wctx.enter_context(nc.semaphore("emb_part"))}
            tables(nc, I, persist, W, scratch)
            attend(nc, I, persist, W, scratch)
        hydra(nc, I, persist, scratch)
        experts(nc, I, persist, scratch, out)


def layout(inputs):
    a = {k: np.asarray(v) for k, v in inputs.items()}
    f = np.float32
    half = P // 2
    freq = np.exp(np.arange(half, dtype=f) * f(-np.log(100.0) / (half - 1))).astype(f)
    pos_const = np.zeros((P, 2 + N_POS), f)
    pos_const[:, 0] = np.concatenate([freq, freq])
    pos_const[half:, 1] = 0.25
    pos_const[:, 2:] = np.arange(N_POS, dtype=f)
    ids = np.zeros((P, (B + 1) * TT), np.int32)
    ids[:, :B * TT] = a["x"].reshape(B * TT, P).T
    row = lambda v: np.ascontiguousarray(v.reshape(1, -1))
    con = np.ascontiguousarray
    ra_w = np.zeros((D, RA), f)
    ra_w[:, :NR] = a["L0_ffn_router_W"].T
    ra_w[:, NR + 1:] = a["L0_ffn_A"].reshape(E0 * R0, D).T
    b12 = np.stack([a["L0_tok_b1"], a["L0_tok_b2"]], 1).reshape(E_POS * 2, 2, P)
    return {
        "pos_const": pos_const, "ids": ids, "embed": a["L0_tok_embed_table"],
        "W1": a["L0_tok_W1"], "W2": a["L0_tok_W2"], "W3": a["L0_tok_W3"], "b3": a["L0_tok_b3"],
        "b12": con(b12.transpose(2, 0, 1)),
        "bind_qk": con(np.concatenate([a["L0_attn_bv_q"].reshape(DC, P).T, a["L0_attn_bv_k"].reshape(DC, P).T], 1)),
        "bv_v": row(a["L0_attn_bv_v"]), "pick": np.repeat(np.eye(E_POS, dtype=f), CANVAS, 1),
        "base_w": con(a["L0_ffn_base_W"].T), "base_b": row(a["L0_ffn_base_b"]), "ra_w": ra_w,
        "router_b": row(a["L0_ffn_router_b"]), "expert_map": row(a["L0_ffn_expert_map"]),
        "lora_b": con(a["L0_ffn_B"].transpose(0, 2, 1).reshape(E0 * R0, D)),
        "in_z": con(a["L1_attn_hy_in_w"][:DIN].T), "in_x": con(a["L1_attn_hy_in_w"][DIN:2 * DIN].T),
        "in_bcdt": con(a["L1_attn_hy_in_w"][2 * DIN:].T),
        "conv_bx": con(a["L1_attn_hy_conv_b"][:DIN].reshape(2, P).T),
        "hy_bias": con(np.concatenate([a["L1_attn_hy_conv_b"][DIN:]] + [a["L1_attn_hy_dt_bias"]] * 2 + [a["L1_attn_hy_D"]]).reshape(1, NB)),
        "hy_norm": con(a["L1_attn_hy_norm_w"].reshape(2, P).T),
        "conv_x": con(a["L1_attn_hy_conv_w"][:DIN, 0, :].reshape(2, P, DCONV).transpose(1, 0, 2)),
        "conv_bc": con(a["L1_attn_hy_conv_w"][DIN:, 0, :].reshape(1, -1)), "fcd": con(a["L1_attn_hy_fcD_w"].T),
        "hy_out": con(a["L1_attn_hy_out_w"].T), "a_log": con(np.concatenate([a["L1_attn_hy_A_log"]] * 2).reshape(1, -1)),
        "gate1": con(a["L1_attn_gate1"].reshape(1, 1)),
        "ea_w": con(a["L1_ffn_A"].transpose(2, 1, 0).reshape(D, RANK * KE)),
        "eb_w": con(a["L1_ffn_B"].transpose(2, 0, 1).reshape(RANK * KE, D)),
        "wr": con(a["L1_ffn_Wr"].T), "w_up": con(a["L1_attn_w_up"].T), "b_up": row(a["L1_attn_b_up"]),
        "w_down": con(a["L1_attn_w_down"].T), "b_down": a["L1_attn_b_down"].reshape(P, 1),
    }


def kernel(**inputs):
    from concourse import bacc
    from concourse.bass_utils import run_bass_kernel_spmd

    nc = bacc.Bacc("TRN2", target_bir_lowering=False, num_devices=1)
    arrays = {"in_" + k: v for k, v in layout(inputs).items()}
    I = {k[3:]: nc.dram_tensor(k, v.shape, mybir.dt.from_np(v.dtype), kind="ExternalInput").ap() for k, v in arrays.items()}
    out = nc.dram_tensor("out", (B, T, D), F32, kind="ExternalOutput").ap()
    program(nc, I, out)
    return run_bass_kernel_spmd(nc, [arrays], core_ids=[0]).results[0]["out"]
```
